# Optimizing a Trainium2 kernel written in Bass

```python
import numpy as np
import jax
import jax.numpy as jnp

def _softmax(x, axis=-1):
    return jax.nn.softmax(x, axis=axis)

def _gelu(x):
    return jax.nn.gelu(x, approximate=True)

def _silu(x):
    return jax.nn.silu(x)

def _sigmoid(x):
    return jax.nn.sigmoid(x)

def _layernorm(x, axis=-1, eps=1e-05):
    m = jnp.mean(x, axis=axis, keepdims=True)
    v = jnp.var(x, axis=axis, keepdims=True)
    return (x - m) / jnp.sqrt(v + eps)

def _scatter_add(tgt, idx, src, axis=0):
    return tgt.at[idx].add(src)

def _segment_sum(src, seg, n):
    return jax.ops.segment_sum(src, seg, n)
kernel_name = 'mk_sandwich_d2_jaxref_r8_af835d'

def setup_inputs(seed: int=0):
    np.random.seed(seed)
    _w = jnp.asarray

    def _L0_attn_setup():
        import jax, jax.numpy as jnp
        import numpy as np
        B, L, H = (2, 512, 128)
        NH, DK, DV = (4, 32, 32)
        CHUNK = 32
        CONV_K, FIR_S, FIR_L = (4, 3, 63)
        GATE_HID = 128
        FLOOR_NOW = 0.05

        def _l2norm(x, eps=1e-06):
            return x * jax.lax.rsqrt(jnp.sum(x * x, -1, keepdims=True) + eps)

        def _depthwise_causal(x_bcl, w_c1k):
            K = w_c1k.shape[-1]
            return jax.lax.conv_general_dilated(x_bcl, w_c1k, (1,), [(K - 1, 0)], dimension_numbers=('NCH', 'OIH', 'NCH'), feature_group_count=x_bcl.shape[1])

        def _short_conv_silu(x, w):
            y = _depthwise_causal(jnp.swapaxes(x, 1, 2), w[:, None, :])
            return jax.nn.silu(jnp.swapaxes(y, 1, 2))

        def _fir(x, filt):
            b, l, h, d = x.shape
            xf = jnp.swapaxes(x.reshape(b, l, h * d), 1, 2)
            y = _depthwise_causal(xf, filt.reshape(h * d, 1, -1))
            return jnp.swapaxes(y, 1, 2).reshape(b, l, h, d)

        def _delta_rule_chunkwise(q, k, v, beta, chunk=CHUNK):
            b, h, Lq, dk = q.shape
            dv = v.shape[-1]
            q = _l2norm(q)
            k = _l2norm(k)
            v = v * beta[..., None]
            k_beta = k * beta[..., None]
            n = Lq // chunk
            rs = lambda t: t.reshape(b, h, n, chunk, -1)
            q, k, v, k_beta = map(rs, (q, k, v, k_beta))
            idx = jnp.arange(chunk)
            strict_lower = idx[:, None] > idx[None, :]
            incl_lower = idx[:, None] >= idx[None, :]
            A = jnp.where(strict_lower, -jnp.einsum('bhnck,bhnjk->bhncj', k_beta, k), 0.0)
            for i in range(1, chunk):
                row = A[..., i, :]
                A = A.at[..., i, :].set(row + jnp.einsum('bhnj,bhnjc->bhnc', row, A))
            T = A + jnp.eye(chunk, dtype=A.dtype)
            u = jnp.einsum('bhncj,bhnjd->bhncd', T, v)
            w = jnp.einsum('bhncj,bhnjd->bhncd', T, k_beta)

            def step(S, inp):
                q_i, k_i, u_i, w_i = inp
                attn = jnp.where(incl_lower, jnp.einsum('bhck,bhjk->bhcj', q_i, k_i), 0.0)
                u_adj = u_i - jnp.einsum('bhck,bhkd->bhcd', w_i, S)
                o_i = jnp.einsum('bhck,bhkd->bhcd', q_i, S) + jnp.einsum('bhcj,bhjd->bhcd', attn, u_adj)
                S = S + jnp.einsum('bhck,bhcd->bhkd', k_i, u_adj)
                return (S, o_i)
            mv = lambda t: jnp.moveaxis(t, 2, 0)
            S0 = jnp.zeros((b, h, dk, dv), q.dtype)
            S, out = jax.lax.scan(step, S0, (mv(q), mv(k), mv(u), mv(w)))
            out = jnp.moveaxis(out, 0, 2).reshape(b, h, Lq, dv)
            return (out, S)

        def _stats(x):
            mean = jnp.mean(x, -1, keepdims=True)
            var = jnp.var(x, -1, keepdims=True)
            am = jnp.mean(jnp.abs(x), -1, keepdims=True)
            l2 = jnp.linalg.norm(x, axis=-1, keepdims=True)
            return jnp.concatenate([mean, var, am, l2], -1)

        def _forward(hs, Wq, Wk, Wv, cwq, cwk, cwv, Wb, Wid, alpha_id, firs, firl, gW1, gb1, gW2, gb2, log_temp, floor_param, conv_res_logit, o_norm_w, Wo):
            b, l, _ = hs.shape
            q = _short_conv_silu(hs @ Wq, cwq)
            k = _short_conv_silu(hs @ Wk, cwk)
            v = _short_conv_silu(hs @ Wv, cwv)
            q = q.reshape(b, l, NH, DK)
            k = k.reshape(b, l, NH, DK)
            v_direct = v.reshape(b, l, NH, DV)
            beta = jax.nn.sigmoid(hs @ Wb)
            tp = lambda t: jnp.transpose(t, (0, 2, 1, 3))
            delta_out, _S = _delta_rule_chunkwise(tp(q), tp(k), tp(v_direct), jnp.transpose(beta, (0, 2, 1)))
            delta_out = tp(delta_out)
            local_short = _fir(v_direct, firs)
            local_long = _fir(v_direct, firl)
            stats = jnp.concatenate([_stats(t) for t in (local_short, local_long, delta_out, v_direct)], -1)
            hs_exp = jnp.broadcast_to(hs[:, :, None, :], (b, l, NH, hs.shape[-1]))
            gin = jnp.concatenate([hs_exp, stats], -1)
            logits = jax.nn.gelu(gin @ gW1 + gb1, approximate=False) @ gW2 + gb2
            logits = logits / jnp.exp(log_temp)[None, None]
            probs = jax.nn.softmax(logits, -1)
            floor = FLOOR_NOW * jax.nn.sigmoid(floor_param)
            probs = probs * (1.0 - jnp.sum(floor, -1, keepdims=True)) + floor
            o = probs[..., 0:1] * local_short + probs[..., 1:2] * local_long + probs[..., 2:3] * delta_out + probs[..., 3:4] * v_direct
            o = o + jax.nn.sigmoid(conv_res_logit)[None, None, :, None] * local_short
            id_val = (hs @ Wid).reshape(b, l, NH, DV)
            o = o + alpha_id[None, None, :, None] * id_val
            o = o * jax.lax.rsqrt(jnp.mean(o * o, -1, keepdims=True) + 1e-05) * o_norm_w
            return o.reshape(b, l, NH * DV) @ Wo
        key = jax.random.key(seed)
        ks = jax.random.split(key, 16)
        nrm = lambda i, shape, sc=0.02: jax.random.normal(ks[i], shape, jnp.float32) * sc

        def dirac_fir(i, K):
            f = jnp.zeros((NH, DV, K), jnp.float32).at[..., -1].set(1.0)
            return f + 0.01 * jax.random.normal(ks[i], (NH, DV, K), jnp.float32)
        return {'hs': jax.random.normal(ks[0], (B, L, H), jnp.float32), 'Wq': nrm(1, (H, NH * DK)), 'Wk': nrm(2, (H, NH * DK)), 'Wv': nrm(3, (H, NH * DV)), 'cwq': nrm(4, (NH * DK, CONV_K), 0.2), 'cwk': nrm(5, (NH * DK, CONV_K), 0.2), 'cwv': nrm(6, (NH * DV, CONV_K), 0.2), 'Wb': nrm(7, (H, NH)), 'Wid': nrm(8, (H, NH * DV)), 'alpha_id': 0.5 * jnp.ones((NH,), jnp.float32), 'firs': dirac_fir(9, FIR_S), 'firl': dirac_fir(10, FIR_L), 'gW1': nrm(11, (H + 16, GATE_HID)), 'gb1': jnp.zeros((GATE_HID,), jnp.float32), 'gW2': nrm(12, (GATE_HID, 4)), 'gb2': jnp.zeros((4,), jnp.float32).at[3].set(1.5), 'log_temp': jnp.zeros((NH, 4), jnp.float32), 'floor_param': jnp.zeros((NH, 4), jnp.float32), 'conv_res_logit': jnp.full((NH,), float(np.log(0.05 / 0.95)), jnp.float32), 'o_norm_w': jnp.ones((DV,), jnp.float32), 'Wo': nrm(13, (NH * DV, H))}
    _L0_attn_in = _L0_attn_setup()

    def _L0_ffn_setup():
        import jax, jax.numpy as jnp
        import numpy as np
        D = 128
        H = 4
        DF = 512
        E = 8
        EPS = 1e-05

        def _layer_norm(x, g, b):
            mu = jnp.mean(x, axis=-1, keepdims=True)
            var = jnp.mean(jnp.square(x - mu), axis=-1, keepdims=True)
            return (x - mu) * jax.lax.rsqrt(var + EPS) * g + b

        def _mha(x, Wqkv, bqkv, Wo, bo):
            S, B, _ = x.shape
            hd = D // H
            qkv = x @ Wqkv.T + bqkv
            q, k, v = jnp.split(qkv, 3, axis=-1)
            to_heads = lambda t: t.reshape(S, B, H, hd).transpose(1, 2, 0, 3)
            q, k, v = (to_heads(q), to_heads(k), to_heads(v))
            scores = jnp.einsum('bhqd,bhkd->bhqk', q, k) * (1.0 / np.sqrt(hd))
            att = jax.nn.softmax(scores, axis=-1)
            o = jnp.einsum('bhqk,bhkd->bhqd', att, v)
            o = o.transpose(2, 0, 1, 3).reshape(S, B, D)
            return o @ Wo.T + bo

        def _moe(x, Wg, W1, b1, W2, b2):
            S, B, _ = x.shape
            xf = x.reshape(S * B, D)
            logits = xf @ Wg.T
            idx = jnp.argmax(logits, axis=-1)
            out = jnp.zeros_like(xf)
            for e in range(E):
                m = (idx == e)[:, None].astype(xf.dtype)
                h = jax.nn.relu(xf @ W1[e] + b1[e])
                out = out + m * (h @ W2[e] + b2[e])
            return out.reshape(S, B, D)
        key = jax.random.key(seed)
        ks = jax.random.split(key, 16)
        S, B = (64, 8)
        s = lambda k, shape, fan: jax.random.normal(k, shape, jnp.float32) * (1.0 / np.sqrt(fan))
        return {'x': jax.random.normal(ks[0], (S, B, D), jnp.float32), 'Wqkv': s(ks[1], (3 * D, D), D), 'bqkv': jnp.zeros((3 * D,), jnp.float32), 'Wo': s(ks[2], (D, D), D), 'bo': jnp.zeros((D,), jnp.float32), 'g1': jnp.ones((D,), jnp.float32), 'be1': jnp.zeros((D,), jnp.float32), 'g2': jnp.ones((D,), jnp.float32), 'be2': jnp.zeros((D,), jnp.float32), 'Wg': s(ks[3], (E, D), D), 'W1': s(ks[4], (E, D, DF), D), 'b1': jnp.zeros((E, DF), jnp.float32), 'W2': s(ks[5], (E, DF, D), DF), 'b2': jnp.zeros((E, D), jnp.float32)}
    _L0_ffn_in = _L0_ffn_setup()

    def _L1_attn_setup():
        import jax, jax.numpy as jnp
        import numpy as np
        DIM = 128
        H = 16
        HD = DIM // H
        R = 8
        QK = 32
        B = 4
        S = 128
        EPS = 1e-05

        def _lin(x, W, b):
            return x @ W.T + b

        def _ln(x, g, b):
            m = x.mean(-1, keepdims=True)
            v = ((x - m) ** 2).mean(-1, keepdims=True)
            return (x - m) / jnp.sqrt(v + EPS) * g + b
        key = jax.random.key(seed)
        ks = iter(jax.random.split(key, 32))

        def w(shape, fan):
            s = 1.0 / np.sqrt(fan)
            return jax.random.uniform(next(ks), shape, jnp.float32, -s, s)
        d = {}
        d['x'] = jax.random.normal(next(ks), (B, S, DIM), jnp.float32)
        d['Wq'] = w((DIM, DIM), DIM)
        d['bq'] = w((DIM,), DIM)
        d['Wk'] = w((DIM, DIM), DIM)
        d['bk'] = w((DIM,), DIM)
        d['Wv'] = w((HD * R, DIM), DIM)
        d['bv'] = w((HD * R,), DIM)
        d['Wqv'] = w((QK * H, DIM), DIM)
        d['bqv'] = w((QK * H,), DIM)
        d['Ws'] = w((1, HD + QK), HD + QK)
        d['bs'] = w((1,), HD + QK)
        d['Wf'] = w((DIM, DIM), DIM)
        d['bf'] = w((DIM,), DIM)
        d['Wr1'] = w((2 * DIM, DIM), DIM)
        d['br1'] = w((2 * DIM,), DIM)
        d['Wr2'] = w((DIM, 2 * DIM), 2 * DIM)
        d['br2'] = w((DIM,), 2 * DIM)
        d['g1'] = jnp.ones((DIM,), jnp.float32)
        d['b1'] = jnp.zeros((DIM,), jnp.float32)
        d['g2'] = jnp.ones((DIM,), jnp.float32)
        d['b2'] = jnp.zeros((DIM,), jnp.float32)
        return d
    _L1_attn_in = _L1_attn_setup()

    def _L1_ffn_setup():
        import jax, jax.numpy as jnp
        import numpy as np
        D_IN, D_HID = (128, 512)

        def _ternary(key, shape):
            return jax.random.randint(key, shape, -1, 2).astype(jnp.float32)

        def _tlin(x, w, s):
            return jnp.einsum('bsi,oi->bso', x, w) * s
        key = jax.random.key(seed)
        ks = jax.random.split(key, 12)
        inv = lambda fan: 1.0 / np.sqrt(fan).astype(np.float32)
        return {'x': jax.random.normal(ks[0], (4, 256, D_IN), dtype=jnp.float32), 'w1_w': _ternary(ks[1], (D_HID, D_IN)), 'w1_s': jax.random.uniform(ks[2], (D_HID,), dtype=jnp.float32) * inv(D_IN), 'w2_w': _ternary(ks[3], (D_HID, D_IN)), 'w2_s': jax.random.uniform(ks[4], (D_HID,), dtype=jnp.float32) * inv(D_IN), 'h1_w': _ternary(ks[5], (D_HID, D_HID)), 'h1_s': jax.random.uniform(ks[6], (D_HID,), dtype=jnp.float32) * inv(D_HID), 'h2_w': _ternary(ks[7], (D_HID, D_HID)), 'h2_s': jax.random.uniform(ks[8], (D_HID,), dtype=jnp.float32) * inv(D_HID), 'w3_w': _ternary(ks[9], (D_IN, D_HID)), 'w3_s': jax.random.uniform(ks[10], (D_IN,), dtype=jnp.float32) * inv(D_HID)}
    _L1_ffn_in = _L1_ffn_setup()
    _d = {'L0_attn_hs': _L0_attn_in['hs'], 'L0_attn_Wq': _L0_attn_in['Wq'], 'L0_attn_Wk': _L0_attn_in['Wk'], 'L0_attn_Wv': _L0_attn_in['Wv'], 'L0_attn_cwq': _L0_attn_in['cwq'], 'L0_attn_cwk': _L0_attn_in['cwk'], 'L0_attn_cwv': _L0_attn_in['cwv'], 'L0_attn_Wb': _L0_attn_in['Wb'], 'L0_attn_Wid': _L0_attn_in['Wid'], 'L0_attn_alpha_id': _L0_attn_in['alpha_id'], 'L0_attn_firs': _L0_attn_in['firs'], 'L0_attn_firl': _L0_attn_in['firl'], 'L0_attn_gW1': _L0_attn_in['gW1'], 'L0_attn_gb1': _L0_attn_in['gb1'], 'L0_attn_gW2': _L0_attn_in['gW2'], 'L0_attn_gb2': _L0_attn_in['gb2'], 'L0_attn_log_temp': _L0_attn_in['log_temp'], 'L0_attn_floor_param': _L0_attn_in['floor_param'], 'L0_attn_conv_res_logit': _L0_attn_in['conv_res_logit'], 'L0_attn_o_norm_w': _L0_attn_in['o_norm_w'], 'L0_attn_Wo': _L0_attn_in['Wo'], 'L0_ffn_Wqkv': _L0_ffn_in['Wqkv'], 'L0_ffn_bqkv': _L0_ffn_in['bqkv'], 'L0_ffn_Wo': _L0_ffn_in['Wo'], 'L0_ffn_bo': _L0_ffn_in['bo'], 'L0_ffn_g1': _L0_ffn_in['g1'], 'L0_ffn_be1': _L0_ffn_in['be1'], 'L0_ffn_g2': _L0_ffn_in['g2'], 'L0_ffn_be2': _L0_ffn_in['be2'], 'L0_ffn_Wg': _L0_ffn_in['Wg'], 'L0_ffn_W1': _L0_ffn_in['W1'], 'L0_ffn_b1': _L0_ffn_in['b1'], 'L0_ffn_W2': _L0_ffn_in['W2'], 'L0_ffn_b2': _L0_ffn_in['b2'], 'L1_attn_Wq': _L1_attn_in['Wq'], 'L1_attn_bq': _L1_attn_in['bq'], 'L1_attn_Wk': _L1_attn_in['Wk'], 'L1_attn_bk': _L1_attn_in['bk'], 'L1_attn_Wv': _L1_attn_in['Wv'], 'L1_attn_bv': _L1_attn_in['bv'], 'L1_attn_Wqv': _L1_attn_in['Wqv'], 'L1_attn_bqv': _L1_attn_in['bqv'], 'L1_attn_Ws': _L1_attn_in['Ws'], 'L1_attn_bs': _L1_attn_in['bs'], 'L1_attn_Wf': _L1_attn_in['Wf'], 'L1_attn_bf': _L1_attn_in['bf'], 'L1_attn_Wr1': _L1_attn_in['Wr1'], 'L1_attn_br1': _L1_attn_in['br1'], 'L1_attn_Wr2': _L1_attn_in['Wr2'], 'L1_attn_br2': _L1_attn_in['br2'], 'L1_attn_g1': _L1_attn_in['g1'], 'L1_attn_b1': _L1_attn_in['b1'], 'L1_attn_g2': _L1_attn_in['g2'], 'L1_attn_b2': _L1_attn_in['b2'], 'L1_ffn_w1_w': _L1_ffn_in['w1_w'], 'L1_ffn_w1_s': _L1_ffn_in['w1_s'], 'L1_ffn_w2_w': _L1_ffn_in['w2_w'], 'L1_ffn_w2_s': _L1_ffn_in['w2_s'], 'L1_ffn_h1_w': _L1_ffn_in['h1_w'], 'L1_ffn_h1_s': _L1_ffn_in['h1_s'], 'L1_ffn_h2_w': _L1_ffn_in['h2_w'], 'L1_ffn_h2_s': _L1_ffn_in['h2_s'], 'L1_ffn_w3_w': _L1_ffn_in['w3_w'], 'L1_ffn_w3_s': _L1_ffn_in['w3_s']}
    _x0 = _d['L0_attn_hs']
    _d['L0_attn_hs'] = jax.random.normal(jax.random.fold_in(jax.random.key(seed), 1), (8, 256, 128), dtype=_x0.dtype)
    del _x0
    return _d

def reference(L0_attn_hs, L0_attn_Wq, L0_attn_Wk, L0_attn_Wv, L0_attn_cwq, L0_attn_cwk, L0_attn_cwv, L0_attn_Wb, L0_attn_Wid, L0_attn_alpha_id, L0_attn_firs, L0_attn_firl, L0_attn_gW1, L0_attn_gb1, L0_attn_gW2, L0_attn_gb2, L0_attn_log_temp, L0_attn_floor_param, L0_attn_conv_res_logit, L0_attn_o_norm_w, L0_attn_Wo, L0_ffn_Wqkv, L0_ffn_bqkv, L0_ffn_Wo, L0_ffn_bo, L0_ffn_g1, L0_ffn_be1, L0_ffn_g2, L0_ffn_be2, L0_ffn_Wg, L0_ffn_W1, L0_ffn_b1, L0_ffn_W2, L0_ffn_b2, L1_attn_Wq, L1_attn_bq, L1_attn_Wk, L1_attn_bk, L1_attn_Wv, L1_attn_bv, L1_attn_Wqv, L1_attn_bqv, L1_attn_Ws, L1_attn_bs, L1_attn_Wf, L1_attn_bf, L1_attn_Wr1, L1_attn_br1, L1_attn_Wr2, L1_attn_br2, L1_attn_g1, L1_attn_b1, L1_attn_g2, L1_attn_b2, L1_ffn_w1_w, L1_ffn_w1_s, L1_ffn_w2_w, L1_ffn_w2_s, L1_ffn_h1_w, L1_ffn_h1_s, L1_ffn_h2_w, L1_ffn_h2_s, L1_ffn_w3_w, L1_ffn_w3_s):

    def _L0_attn_ref(hs, Wq, Wk, Wv, cwq, cwk, cwv, Wb, Wid, alpha_id, firs, firl, gW1, gb1, gW2, gb2, log_temp, floor_param, conv_res_logit, o_norm_w, Wo):
        import jax, jax.numpy as jnp
        import numpy as np
        B, L, H = (2, 512, 128)
        NH, DK, DV = (4, 32, 32)
        CHUNK = 32
        CONV_K, FIR_S, FIR_L = (4, 3, 63)
        GATE_HID = 128
        FLOOR_NOW = 0.05

        def _l2norm(x, eps=1e-06):
            return x * jax.lax.rsqrt(jnp.sum(x * x, -1, keepdims=True) + eps)

        def _depthwise_causal(x_bcl, w_c1k):
            K = w_c1k.shape[-1]
            return jax.lax.conv_general_dilated(x_bcl, w_c1k, (1,), [(K - 1, 0)], dimension_numbers=('NCH', 'OIH', 'NCH'), feature_group_count=x_bcl.shape[1])

        def _short_conv_silu(x, w):
            y = _depthwise_causal(jnp.swapaxes(x, 1, 2), w[:, None, :])
            return jax.nn.silu(jnp.swapaxes(y, 1, 2))

        def _fir(x, filt):
            b, l, h, d = x.shape
            xf = jnp.swapaxes(x.reshape(b, l, h * d), 1, 2)
            y = _depthwise_causal(xf, filt.reshape(h * d, 1, -1))
            return jnp.swapaxes(y, 1, 2).reshape(b, l, h, d)

        def _delta_rule_chunkwise(q, k, v, beta, chunk=CHUNK):
            b, h, Lq, dk = q.shape
            dv = v.shape[-1]
            q = _l2norm(q)
            k = _l2norm(k)
            v = v * beta[..., None]
            k_beta = k * beta[..., None]
            n = Lq // chunk
            rs = lambda t: t.reshape(b, h, n, chunk, -1)
            q, k, v, k_beta = map(rs, (q, k, v, k_beta))
            idx = jnp.arange(chunk)
            strict_lower = idx[:, None] > idx[None, :]
            incl_lower = idx[:, None] >= idx[None, :]
            A = jnp.where(strict_lower, -jnp.einsum('bhnck,bhnjk->bhncj', k_beta, k), 0.0)
            for i in range(1, chunk):
                row = A[..., i, :]
                A = A.at[..., i, :].set(row + jnp.einsum('bhnj,bhnjc->bhnc', row, A))
            T = A + jnp.eye(chunk, dtype=A.dtype)
            u = jnp.einsum('bhncj,bhnjd->bhncd', T, v)
            w = jnp.einsum('bhncj,bhnjd->bhncd', T, k_beta)

            def step(S, inp):
                q_i, k_i, u_i, w_i = inp
                attn = jnp.where(incl_lower, jnp.einsum('bhck,bhjk->bhcj', q_i, k_i), 0.0)
                u_adj = u_i - jnp.einsum('bhck,bhkd->bhcd', w_i, S)
                o_i = jnp.einsum('bhck,bhkd->bhcd', q_i, S) + jnp.einsum('bhcj,bhjd->bhcd', attn, u_adj)
                S = S + jnp.einsum('bhck,bhcd->bhkd', k_i, u_adj)
                return (S, o_i)
            mv = lambda t: jnp.moveaxis(t, 2, 0)
            S0 = jnp.zeros((b, h, dk, dv), q.dtype)
            S, out = jax.lax.scan(step, S0, (mv(q), mv(k), mv(u), mv(w)))
            out = jnp.moveaxis(out, 0, 2).reshape(b, h, Lq, dv)
            return (out, S)

        def _stats(x):
            mean = jnp.mean(x, -1, keepdims=True)
            var = jnp.var(x, -1, keepdims=True)
            am = jnp.mean(jnp.abs(x), -1, keepdims=True)
            l2 = jnp.linalg.norm(x, axis=-1, keepdims=True)
            return jnp.concatenate([mean, var, am, l2], -1)

        def _forward(hs, Wq, Wk, Wv, cwq, cwk, cwv, Wb, Wid, alpha_id, firs, firl, gW1, gb1, gW2, gb2, log_temp, floor_param, conv_res_logit, o_norm_w, Wo):
            b, l, _ = hs.shape
            q = _short_conv_silu(hs @ Wq, cwq)
            k = _short_conv_silu(hs @ Wk, cwk)
            v = _short_conv_silu(hs @ Wv, cwv)
            q = q.reshape(b, l, NH, DK)
            k = k.reshape(b, l, NH, DK)
            v_direct = v.reshape(b, l, NH, DV)
            beta = jax.nn.sigmoid(hs @ Wb)
            tp = lambda t: jnp.transpose(t, (0, 2, 1, 3))
            delta_out, _S = _delta_rule_chunkwise(tp(q), tp(k), tp(v_direct), jnp.transpose(beta, (0, 2, 1)))
            delta_out = tp(delta_out)
            local_short = _fir(v_direct, firs)
            local_long = _fir(v_direct, firl)
            stats = jnp.concatenate([_stats(t) for t in (local_short, local_long, delta_out, v_direct)], -1)
            hs_exp = jnp.broadcast_to(hs[:, :, None, :], (b, l, NH, hs.shape[-1]))
            gin = jnp.concatenate([hs_exp, stats], -1)
            logits = jax.nn.gelu(gin @ gW1 + gb1, approximate=False) @ gW2 + gb2
            logits = logits / jnp.exp(log_temp)[None, None]
            probs = jax.nn.softmax(logits, -1)
            floor = FLOOR_NOW * jax.nn.sigmoid(floor_param)
            probs = probs * (1.0 - jnp.sum(floor, -1, keepdims=True)) + floor
            o = probs[..., 0:1] * local_short + probs[..., 1:2] * local_long + probs[..., 2:3] * delta_out + probs[..., 3:4] * v_direct
            o = o + jax.nn.sigmoid(conv_res_logit)[None, None, :, None] * local_short
            id_val = (hs @ Wid).reshape(b, l, NH, DV)
            o = o + alpha_id[None, None, :, None] * id_val
            o = o * jax.lax.rsqrt(jnp.mean(o * o, -1, keepdims=True) + 1e-05) * o_norm_w
            return o.reshape(b, l, NH * DV) @ Wo
        return _forward(hs, Wq, Wk, Wv, cwq, cwk, cwv, Wb, Wid, alpha_id, firs, firl, gW1, gb1, gW2, gb2, log_temp, floor_param, conv_res_logit, o_norm_w, Wo)

    def _L0_ffn_ref(x, Wqkv, bqkv, Wo, bo, g1, be1, g2, be2, Wg, W1, b1, W2, b2):
        import jax, jax.numpy as jnp
        import numpy as np
        D = 128
        H = 4
        DF = 512
        E = 8
        EPS = 1e-05

        def _layer_norm(x, g, b):
            mu = jnp.mean(x, axis=-1, keepdims=True)
            var = jnp.mean(jnp.square(x - mu), axis=-1, keepdims=True)
            return (x - mu) * jax.lax.rsqrt(var + EPS) * g + b

        def _mha(x, Wqkv, bqkv, Wo, bo):
            S, B, _ = x.shape
            hd = D // H
            qkv = x @ Wqkv.T + bqkv
            q, k, v = jnp.split(qkv, 3, axis=-1)
            to_heads = lambda t: t.reshape(S, B, H, hd).transpose(1, 2, 0, 3)
            q, k, v = (to_heads(q), to_heads(k), to_heads(v))
            scores = jnp.einsum('bhqd,bhkd->bhqk', q, k) * (1.0 / np.sqrt(hd))
            att = jax.nn.softmax(scores, axis=-1)
            o = jnp.einsum('bhqk,bhkd->bhqd', att, v)
            o = o.transpose(2, 0, 1, 3).reshape(S, B, D)
            return o @ Wo.T + bo

        def _moe(x, Wg, W1, b1, W2, b2):
            S, B, _ = x.shape
            xf = x.reshape(S * B, D)
            logits = xf @ Wg.T
            idx = jnp.argmax(logits, axis=-1)
            out = jnp.zeros_like(xf)
            for e in range(E):
                m = (idx == e)[:, None].astype(xf.dtype)
                h = jax.nn.relu(xf @ W1[e] + b1[e])
                out = out + m * (h @ W2[e] + b2[e])
            return out.reshape(S, B, D)
        y = _layer_norm(x + _mha(x, Wqkv, bqkv, Wo, bo), g1, be1)
        z = _layer_norm(y + _moe(y, Wg, W1, b1, W2, b2), g2, be2)
        return z

    def _L1_attn_ref(x, Wq, bq, Wk, bk, Wv, bv, Wqv, bqv, Ws, bs, Wf, bf, Wr1, br1, Wr2, br2, g1, b1, g2, b2):
        import jax, jax.numpy as jnp
        import numpy as np
        DIM = 128
        H = 16
        HD = DIM // H
        R = 8
        QK = 32
        B = 4
        S = 128
        EPS = 1e-05

        def _lin(x, W, b):
            return x @ W.T + b

        def _ln(x, g, b):
            m = x.mean(-1, keepdims=True)
            v = ((x - m) ** 2).mean(-1, keepdims=True)
            return (x - m) / jnp.sqrt(v + EPS) * g + b
        b, n, _ = x.shape
        res = x
        xn = _ln(x, g1, b1)
        q = _lin(xn, Wq, bq).reshape(b, n, H, HD) / np.sqrt(HD).astype(np.float32)
        k = _lin(xn, Wk, bk).reshape(b, n, H, HD)
        score = jax.nn.softmax(jnp.einsum('bihd,bjhd->bhij', q, k), axis=-1)
        v = _lin(xn, Wv, bv).reshape(b, n, R, HD)
        out = jnp.einsum('bhij,bjrd->bihrd', score, v)
        qv = _lin(xn, Wqv, bqv).reshape(b, n, H, 1, QK) / np.sqrt(QK).astype(np.float32)
        qv = jnp.broadcast_to(qv, (b, n, H, R, QK))
        comp = jnp.concatenate([qv, out], axis=-1) @ Ws.T + bs
        comp = jax.nn.softmax(comp, axis=3)
        out = (comp * out).sum(axis=3).reshape(b, n, DIM)
        out = res + _lin(out, Wf, bf)
        res2 = out
        on = _ln(out, g2, b2)
        ffn = _lin(jax.nn.relu(_lin(on, Wr1, br1)), Wr2, br2)
        return res2 + ffn

    def _L1_ffn_ref(x, w1_w, w1_s, w2_w, w2_s, h1_w, h1_s, h2_w, h2_s, w3_w, w3_s):
        import jax, jax.numpy as jnp
        import numpy as np
        D_IN, D_HID = (128, 512)

        def _ternary(key, shape):
            return jax.random.randint(key, shape, -1, 2).astype(jnp.float32)

        def _tlin(x, w, s):
            return jnp.einsum('bsi,oi->bso', x, w) * s
        h = jax.nn.silu(_tlin(x, w1_w, w1_s)) * _tlin(x, w2_w, w2_s)
        h = jax.nn.gelu(_tlin(h, h1_w, h1_s), approximate=False)
        h = jax.nn.gelu(_tlin(h, h2_w, h2_s), approximate=False)
        return _tlin(h, w3_w, w3_s)
    x = L0_attn_hs
    x = x + _layernorm(_L0_attn_ref(_layernorm(x, axis=-1), L0_attn_Wq, L0_attn_Wk, L0_attn_Wv, L0_attn_cwq, L0_attn_cwk, L0_attn_cwv, L0_attn_Wb, L0_attn_Wid, L0_attn_alpha_id, L0_attn_firs, L0_attn_firl, L0_attn_gW1, L0_attn_gb1, L0_attn_gW2, L0_attn_gb2, L0_attn_log_temp, L0_attn_floor_param, L0_attn_conv_res_logit, L0_attn_o_norm_w, L0_attn_Wo), axis=-1)
    x = x + _layernorm(_L0_ffn_ref(_layernorm(x, axis=-1), L0_ffn_Wqkv, L0_ffn_bqkv, L0_ffn_Wo, L0_ffn_bo, L0_ffn_g1, L0_ffn_be1, L0_ffn_g2, L0_ffn_be2, L0_ffn_Wg, L0_ffn_W1, L0_ffn_b1, L0_ffn_W2, L0_ffn_b2), axis=-1)
    x = x + _layernorm(_L1_attn_ref(_layernorm(x, axis=-1), L1_attn_Wq, L1_attn_bq, L1_attn_Wk, L1_attn_bk, L1_attn_Wv, L1_attn_bv, L1_attn_Wqv, L1_attn_bqv, L1_attn_Ws, L1_attn_bs, L1_attn_Wf, L1_attn_bf, L1_attn_Wr1, L1_attn_br1, L1_attn_Wr2, L1_attn_br2, L1_attn_g1, L1_attn_b1, L1_attn_g2, L1_attn_b2), axis=-1)
    x = x + _layernorm(_L1_ffn_ref(_layernorm(x, axis=-1), L1_ffn_w1_w, L1_ffn_w1_s, L1_ffn_w2_w, L1_ffn_w2_s, L1_ffn_h1_w, L1_ffn_h1_s, L1_ffn_h2_w, L1_ffn_h2_s, L1_ffn_w3_w, L1_ffn_w3_s), axis=-1)
    return x

_drawn_inputs = setup_inputs


def setup_inputs(seed=0):
    import zlib

    import numpy as np

    out = dict(_drawn_inputs(seed))
    spreads = {'L0_attn_alpha_id': (0.5, 0.2),
     'L0_attn_gb1': (0.0, 0.8),
     'L0_attn_log_temp': (0.0, 0.386),
     'L0_attn_floor_param': (0.0, 0.8),
     'L0_attn_conv_res_logit': (-2.944438934326172, 0.2),
     'L0_attn_o_norm_w': (1.0, 0.2),
     'L0_ffn_bqkv': (0.0, 0.1),
     'L0_ffn_bo': (0.0, 0.1),
     'L0_ffn_g1': (1.0, 0.2),
     'L0_ffn_be1': (0.0, 0.1),
     'L0_ffn_g2': (1.0, 0.2),
     'L0_ffn_be2': (0.0, 0.1),
     'L0_ffn_b1': (0.0, 0.322),
     'L0_ffn_b2': (0.0, 0.1),
     'L1_attn_g1': (1.0, 0.6),
     'L1_attn_b1': (0.0, 0.8),
     'L1_attn_g2': (1.0, 0.6),
     'L1_attn_b2': (0.0, 2.0)}
    factors = {'L0_attn_Wb': 3.029,
     'L0_attn_firs': 5.455,
     'L0_attn_gW1': 8.0,
     'L0_attn_gW2': 7.343,
     'L1_attn_Wq': 8.0,
     'L1_attn_bq': 8.0,
     'L1_attn_Wk': 8.0,
     'L1_attn_bk': 200.0,
     'L1_attn_Wv': 7.936,
     'L1_attn_bv': 8.0,
     'L1_attn_Wqv': 200.0,
     'L1_attn_bqv': 200.0,
     'L1_attn_Ws': 8.0,
     'L1_attn_Wf': 8.0,
     'L1_attn_bf': 130.262,
     'L1_attn_br1': 64.0,
     'L1_attn_br2': 192.589,
     'L1_attn_Wr1': 8.0,
     'L1_attn_Wr2': 8.0}
    for name, (base, spread) in spreads.items():
        noise = np.random.default_rng([zlib.crc32(name.encode()), seed]).standard_normal(out[name].shape)
        drawn = base * np.exp(spread * noise) if base else spread * noise
        out[name] = jnp.asarray(drawn.astype(out[name].dtype))
    for name, factor in factors.items():
        out[name] = (out[name] * factor).astype(out[name].dtype)
    return out
```

```python
import math
from contextlib import ExitStack

import numpy as np

import concourse.bass as bass
from concourse import mybir

F32 = mybir.dt.float32
ALU = mybir.AluOpType
ACT = mybir.ActivationFunctionType
AX = mybir.AxisListType

P = 128
B, L, D = 8, 256, 128
NT = B * L // P
NG = NT // 4
NH, DK = 4, 32
TAPS, FIRS, FIRL = 4, 3, 63
PAD = FIRL
E, DF = 8, 512
H2, HD2, R2, QK2 = 16, 8, 8, 32
VX = R2 * HD2 + R2 + 1
DH = 512
FLOOR = 0.05
LEVELS = 7


PACK_A = [("ident", 128), ("low", 128), ("upp", 128), ("incl", 128), ("wqkv", 384), ("cwb", 1536),
          ("wid", 128), ("wb", 4), ("firs", 4), ("firl", 64), ("gw1h", 128), ("gw1s", 512), ("gb1", 1),
          ("gw2", 4), ("gb2", 16), ("ltemp", 16), ("floor", 16), ("crl", 4), ("alpha", 4), ("onw", 1),
          ("wo", 128)]
PACK_B = [("ident", 128), ("wqkv", 384), ("bqkv", 384), ("wo", 128), ("bo", 128), ("g1", 128), ("be1", 128),
          ("g2", 128), ("be2", 128), ("wg", 8), ("w1", E * DF), ("b1", E * 4), ("w2", E * DF), ("b2", 128),
          ("iota", 8)]
PACK_C = [("wq", 512), ("wk", 512), ("bq", 4), ("bk", 4), ("wv", 64), ("bv", 64), ("wqv", 512),
          ("bqv", 4), ("wsq", 1), ("mask4", 4), ("wso", 8), ("bs", 1), ("wf", 128), ("bf", 128), ("wr1", 256),
          ("br1", 2), ("wr2", 256), ("br2", 128), ("g1", 128), ("b1", 128), ("g2", 128), ("b2", 128)]
PACK_D = [("w1", DH), ("w2", DH), ("h1", 4 * DH), ("h2", 4 * DH), ("w3", DH), ("s1", 4), ("s2", 4),
          ("t1", 4), ("t2", 4), ("s3", 128)]


def offsets(pack):
    at, out = 0, {}
    for name, width in pack:
        out[name] = (at, width)
        at += width
    return out, at


class Chain:

    def __init__(self, eng, sem):
        self.eng, self.sem, self.done, self.base, self.inside = eng, sem, 0, None, 0

    def enter(self, turn, per):
        self.base, self.inside, self.per = turn * per, 0, per

    def leave(self, turns):
        assert self.inside == self.per, (self.inside, self.per)
        self.done += turns * self.per
        self.base = None

    def mark(self, ins):
        ins.then_inc(self.sem, 1)
        if self.base is None:
            self.done += 1
            return self.done
        self.inside += 1
        return self.base + (self.done + self.inside)

    def link(self, ins):
        self.eng.wait_ge(self.sem, self.mark(ins))


class Uses:

    def __init__(self, full, sems, engines):
        self.full, self.sems, self.n = full, sems, len(engines)
        self.per = {e: 0 for e in sems}
        self.at = []
        for e in engines:
            self.per[e] += 1
            self.at.append((e, self.per[e]))

    def open(self, eng, e):
        eng.sem_inc(self.sems[e], 1)

    def wait_start(self, pe, g):
        for e, s in self.sems.items():
            pe.wait_ge(s, g * self.per[e] + 1)

    def wait_empty(self, pe, g, n):
        if n >= 8:
            self.wait_taken(pe, g, n - 8)

    def wait_taken(self, pe, g, n):
        e, k = self.at[n]
        pe.wait_ge(self.sems[e], g * self.per[e] + (k + 1))

    def wait_full(self, eng, g, n):
        eng.wait_ge(self.full, g * self.n + (n + 1))


def build(nc, x_in, pa_in, pb_in, pc_in, pd_in, out_dram):
    ctx = ExitStack()
    with ctx:
        names = {}

        def sem(name):
            if name not in names:
                names[name] = ctx.enter_context(nc.semaphore(name))
            return names[name]

        def sbuf(stack, name, shape):
            return stack.enter_context(nc.sbuf_tensor(name, shape, F32))

        X = sbuf(ctx, "X", [P, NT, D])
        NRM = sbuf(ctx, "NRM", [P, NT, D])
        TR = sbuf(ctx, "TR", [P, NT * D])
        STAT = sbuf(ctx, "STAT", [P, NT, 6])
        MV = sbuf(ctx, "MV", [P, NT, 2])
        SQA = sbuf(ctx, "SQA", [P, 256])
        SQR = sbuf(ctx, "SQR", [P, 256])
        RS = sbuf(ctx, "RS", [P, NT])
        oa, na = offsets(PACK_A)
        ob, nb = offsets(PACK_B)
        oc, ncc = offsets(PACK_C)
        od, nd = offsets(PACK_D)
        PB = sbuf(ctx, "PB", [P, nb])
        PS = ctx.enter_context(nc.psum_tensor("PS", [P, 8, 512], F32))

        def pb(name, rows=P):
            at, width = ob[name]
            return PB[0:rows, at:at + width]

        ident = pb("ident")
        loadA, loadB, loadC, loadD = sem("load_a"), sem("load_b"), sem("load_c"), sem("load_d")
        load_x = sem("load_x")
        dve_step, act_step, pool_step = sem("dve_step"), sem("act_step"), sem("pool_step")
        sqrt_asked, sqrt_given = sem("sqrt_asked"), sem("sqrt_given")
        norm_ready = sem("norm_ready")
        tr_bank, tr_copied = sem("tr_bank"), sem("tr_copied")
        V = Chain(nc.vector, dve_step)
        A = Chain(nc.scalar, act_step)
        G = Chain(nc.gpsimd, pool_step)
        count = {"sqrt_v": 0, "sqrt_a": 0, "norm_v": 0, "norm_p": 0, "tr_p": 0, "tr_a": 0, "tr_v": 0}

        def tile4(ap):
            return ap.rearrange("p (t c) -> p t c", t=4)

        def bcast(ap, n):
            return ap.unsqueeze(2).to_broadcast([P, ap.shape[1], n])

        def rows(ap, n):
            return ap.unsqueeze(1).to_broadcast([P, n, ap.shape[1]])

        def v_sqrt(arg_width):
            count["sqrt_v"] += 1
            nc.vector.wait_ge(sqrt_given, count["sqrt_v"])

        def a_sqrt(width):
            count["sqrt_a"] += 1
            nc.scalar.wait_ge(sqrt_asked, count["sqrt_a"])
            nc.scalar.activation(SQR[:, :width], SQA[:, :width], ACT.Sqrt).then_inc(sqrt_given, 1)

        def v_ask(ins):
            ins.then_inc(sqrt_asked, 1)

        def v_norm(src, dst, eps=1e-5, tiles=NT):
            for t in range(tiles):
                last = nc.vector.bn_stats(STAT[:, t, :], src(t))
            V.link(last)
            for t in range(tiles):
                last = nc.vector.bn_aggr(MV[:, t, :], STAT[:, t, :])
            V.link(last)
            v_ask(nc.vector.tensor_scalar(SQA[:, :tiles], MV[:, :tiles, 1], eps, None, ALU.add))
            v_sqrt(tiles)
            V.link(nc.vector.reciprocal(RS[:, :tiles], SQR[:, :tiles]))
            for t in range(tiles):
                last = nc.vector.tensor_scalar(dst(t), src(t), MV[:, t, 0:1], RS[:, t:t + 1],
                                               ALU.subtract, ALU.mult)
            return last

        def v_ready(last):
            last.then_inc(norm_ready, 1)
            count["norm_v"] += 1

        def p_transpose(src, banks=(0, 1, 2, 3), ready=True):
            if ready:
                count["norm_p"] += 1
                nc.tensor.wait_ge(norm_ready, count["norm_p"])
            for j, bank in enumerate(banks):
                for t in range(4):
                    last = nc.tensor.transpose(PS[:, bank, t * P:(t + 1) * P], src(4 * j + t), ident)
                last.then_inc(tr_bank, 1)
            count["tr_p"] += len(banks)

        def a_transposed(dst, banks=(0, 1, 2, 3)):
            for j, bank in enumerate(banks):
                count["tr_a"] += 1
                nc.scalar.wait_ge(tr_bank, count["tr_a"])
                nc.scalar.activation(dst(j), PS[:, bank, :], ACT.Copy).then_inc(tr_copied, 1)

        def p_copied():
            nc.tensor.wait_ge(tr_copied, count["tr_p"])

        sa = ctx.enter_context(ExitStack())
        DEL = sbuf(sa, "DEL", [P, NT, D])
        QTK = sbuf(sa, "QTK", [P, NT, D])
        KTK = sbuf(sa, "KTK", [P, NT, D])
        VTK = sbuf(sa, "VTK", [P, NT, D])
        ITK = sbuf(sa, "ITK", [P, NT, D])
        VPT = sbuf(sa, "VPT", [P, B, PAD + L])
        FS = sbuf(sa, "FS", [P, B, L])
        FL0 = sbuf(sa, "FL0", [P, B, L])
        FL1 = sbuf(sa, "FL1", [P, B, L])
        XT = sbuf(sa, "XT", [P, B, 3 + L])
        PA = sbuf(sa, "PA", [P, na])
        BETA = sbuf(sa, "BETA", [P, NT, NH])

        def pa(name):
            at, width = oa[name]
            return PA[:, at:at + width]

        s1 = ExitStack()
        with s1:
            WT = sbuf(s1, "WT", [P, 3, TAPS, D])
            ST = sbuf(s1, "ST", [P, 4, 512])
            SB = sbuf(s1, "SB", [NH, 512])
            xt_zero, wt_ready, x_turned = sem("xt_zero"), sem("wt_ready"), sem("x_turned")
            a1_proj, a1_staged, a1_turned, a1_out = (sem("a1_proj"), sem("a1_staged"), sem("a1_turned"),
                                                     sem("a1_out"))
            with nc.Block() as block:
                @block.sync
                def _(sp):
                    sp.dma_start(X[:, :, :], x_in).then_inc(load_x, 16)
                    sp.dma_start(PA[:, :], pa_in).then_inc(loadA, 16)
                    sp.dma_start(PB[:, :], pb_in).then_inc(loadB, 16)

                @block.gpsimd
                def _(pool):
                    nc.gpsimd.memset(XT[:, :, 0:3], 0.0).then_inc(xt_zero, 1)
                    nc.gpsimd.memset(VPT[:, :, 0:PAD], 0.0).then_inc(xt_zero, 1)
                    nc.gpsimd.memset(FS[:, :, :], 0.0).then_inc(xt_zero, 1)
                    nc.gpsimd.memset(FL0[:, :, :], 0.0).then_inc(xt_zero, 1)
                    nc.gpsimd.memset(FL1[:, :, :], 0.0).then_inc(xt_zero, 1)

                @block.vector
                def _(dve):
                    dve.wait_ge(load_x, 16)
                    v_ready(v_norm(lambda t: X[:, t, :], lambda t: NRM[:, t, :]))
                    dve.wait_ge(loadA, 16)
                    for p in range(3):
                        last = nc.vector.tensor_tensor(
                            WT[:, p, :, :], rows(pa("wqkv")[:, p * D:(p + 1) * D], TAPS),
                            pa("cwb")[:, p * 512:(p + 1) * 512].rearrange("p (j c) -> p j c", j=TAPS), ALU.mult)
                    last.then_inc(wt_ready, 1)
                    dve.sem_inc(a1_out, 1)
                    with dve.Fori(0, NG) as g:
                        for n, (bank, dst) in enumerate(((5, QTK), (6, KTK), (7, VTK), (5, ITK))):
                            dve.wait_ge(a1_turned, g * 5 + (n + 2))
                            nc.vector.tensor_copy(dst[:, bass.ds(g * 4, 4), :], tile4(PS[:, bank, :]))\
                                .then_inc(a1_out, 1)
                        dve.wait_ge(a1_turned, g * 5 + 6)
                        nc.vector.tensor_copy(BETA[:, bass.ds(g * 4, 4), :],
                                              PS[:, 6, 0:16].rearrange("p (t h) -> p t h", t=4)).then_inc(a1_out, 1)
                        nc.vector.tensor_copy(VPT[:, bass.ds(g * 2, 2), PAD:PAD + L],
                                              ST[:, 2, :].rearrange("p (b l) -> p b l", b=2)).then_inc(a1_out, 1)

                @block.tensor
                def _(pe):
                    pe.wait_ge(loadB, 16)
                    p_transpose(lambda t: NRM[:, t, :])
                    p_copied()
                    pe.wait_ge(wt_ready, 1)
                    pe.wait_ge(xt_zero, 1)
                    pe.sem_inc(a1_turned, 1)
                    with pe.Fori(0, NG) as g:
                        for p in range(3):
                            for j in range(TAPS):
                                last = nc.tensor.matmul(PS[:, p, :].rearrange("p (b l) -> p b l", b=2),
                                                        WT[:, p, j, :], XT[:, bass.ds(g * 2, 2), j:j + L],
                                                        start=(j == 0), stop=(j == TAPS - 1))
                            last.then_inc(a1_proj, 1)
                        now = XT[:, bass.ds(g * 2, 2), 3:3 + L]
                        nc.tensor.matmul(PS[:, 3, :].rearrange("p (b l) -> p b l", b=2), pa("wid"), now,
                                         start=True, stop=True).then_inc(a1_proj, 1)
                        nc.tensor.matmul(PS[0:NH, 4, :].rearrange("p (b l) -> p b l", b=2), pa("wb"), now,
                                         start=True, stop=True).then_inc(a1_proj, 1)
                        pe.wait_ge(a1_out, g * 6 + 1)
                        for n, bank in enumerate((5, 6, 7, 5)):
                            pe.wait_ge(a1_staged, g * 5 + (n + 1))
                            if n == 3:
                                pe.wait_ge(a1_staged, g * 5 + 5)
                                pe.wait_ge(a1_out, g * 6 + 3)
                            for t in range(4):
                                last = nc.tensor.transpose(PS[:, bank, t * P:(t + 1) * P],
                                                           ST[:, n, t * P:(t + 1) * P], ident)
                            last.then_inc(a1_turned, 1)
                        for t in range(4):
                            last = nc.tensor.transpose(PS[:, 6, t * NH:(t + 1) * NH],
                                                       SB[:, t * P:(t + 1) * P], ident[0:NH, 0:NH])
                        last.then_inc(a1_turned, 1)

                @block.scalar
                def _(act):
                    a_sqrt(NT)
                    a_transposed(lambda j: XT[:, 2 * j:2 * j + 2, 3:3 + L])
                    with act.Fori(0, NG) as g:
                        act.wait_ge(a1_turned, g * 5 + 1)
                        act.wait_ge(a1_out, g * 6 + 1)
                        for n in range(5):
                            act.wait_ge(a1_proj, g * 5 + (n + 1))
                            dst, src, func = ((ST[:, n, :], PS[:, n, :], ACT.Silu if n < 3 else ACT.Copy) if n < 4
                                              else (SB[:, :], PS[0:NH, 4, :], ACT.Sigmoid))
                            nc.scalar.activation(dst, src, func).then_inc(a1_staged, 1)

        s2 = ExitStack()
        with s2:
            RQ = sbuf(s2, "RQ", [P, NT * NH])
            RK = sbuf(s2, "RK", [P, NT * NH])
            RKB = sbuf(s2, "RKB", [P, NT * NH])
            QH = NRM[:, 0:4, :]
            KH = NRM[:, 4:8, :]
            Y = sbuf(s2, "Y", [P, 4, 2, D])
            TQ = sbuf(s2, "TQ", [P, 3, 4, P])
            PW = [sbuf(s2, f"PW{n}", [P, 16, 2, P]) for n in range(2)]
            AT = TR[:, :].rearrange("p (u c) -> p u c", u=16)
            SS = sbuf(s2, "SS", [P, 2, D])
            W1T = sbuf(s2, "W1T", [P, 2, P])
            a2_prep, a2_bank, a2_act, a2_dve = sem("a2_prep"), sem("a2_bank"), sem("a2_act"), sem("a2_dve")

            uses = [("turn", "A")] * 3 + [("mask", "V")] * 12
            for lv in range(LEVELS):
                uses += [("apply", "V")] * 2
                uses += [("square", "A")] * (8 if lv < LEVELS - 2 else 4 if lv == LEVELS - 2 else 0)
            uses += [("state", "V"), ("w1", "A"), ("ws", "V"), ("o", "V")]
            NU = len(uses)
            U = Uses(a2_bank, {"A": a2_act, "V": a2_dve}, [e for _, e in uses])

            pairs = [2 * h + b for b in range(2) for h in range(NH)]

            def bank_of(n):
                return n % 8

            ss_zero = sem("ss_zero")
            with nc.Block() as block:
                @block.gpsimd
                def _(pool):
                    nc.gpsimd.memset(SS[:, :, :], 0.0).then_inc(ss_zero, 1)

                @block.tensor
                def _(pe):
                    with pe.Fori(0, NG) as g:
                        n = 0
                        U.wait_start(pe, g)
                        for k, src in enumerate((QH, KH, None)):
                            pe.wait_ge(a2_prep, g * 4 + (k + 1))
                            for t in range(4):
                                last = nc.tensor.transpose(PS[:, bank_of(n), t * P:(t + 1) * P],
                                                           Y[:, t, 1, :] if src is None else src[:, t, :], ident)
                            last.then_inc(a2_bank, 1)
                            n += 1
                        for l, r in ((2, 1), (1, 2), (1, 0)):
                            U.wait_taken(pe, g, max(l, r))
                            for h in range(NH):
                                U.wait_empty(pe, g, n + h)
                            for t in range(4):
                                for h in range(NH):
                                    hs = slice(DK * h, DK * h + DK)
                                    last = nc.tensor.matmul(PS[:, bank_of(n + h), t * P:(t + 1) * P],
                                                            TQ[hs, l, t, :], TQ[hs, r, t, :], start=True, stop=True)
                                    if t == 3:
                                        last.then_inc(a2_bank, 1)
                            n += NH
                        ready = [10] * 16
                        y_use = None
                        pe.wait_ge(a2_prep, g * 4 + 4)
                        for lv in range(LEVELS):
                            old = PW[lv % 2]
                            new_y = []
                            for half in range(2):
                                U.wait_empty(pe, g, n)
                                U.wait_taken(pe, g, ready[4 * (NH - 1) + 2 * half])
                                if y_use is not None:
                                    U.wait_taken(pe, g, y_use[half])
                                for t in (2 * half, 2 * half + 1):
                                    for h in range(NH):
                                        o = PS[:, bank_of(n), :].rearrange("p (t k c) -> p t k c", t=2, k=2)
                                        last = nc.tensor.matmul(o[:, t % 2, :, h * DK:(h + 1) * DK],
                                                                old[:, 4 * h + t, 1, :],
                                                                Y[:, t, :, h * DK:(h + 1) * DK],
                                                                start=True, stop=True)
                                last.then_inc(a2_bank, 1)
                                new_y.append(n)
                                n += 1
                            y_use = new_y
                            if lv < LEVELS - 2:
                                for pair in pairs:
                                    U.wait_empty(pe, g, n)
                                    U.wait_taken(pe, g, ready[2 * pair + 1])
                                    for u in (2 * pair, 2 * pair + 1):
                                        at = (u % 2) * 256
                                        nc.tensor.matmul(PS[:, bank_of(n), at:at + P], old[:, u, 1, :],
                                                         old[:, u, 0, :], start=True, stop=True)
                                        last = nc.tensor.matmul(PS[:, bank_of(n), at + P:at + 2 * P],
                                                                old[:, u, 0, :], old[:, u, 1, :],
                                                                start=True, stop=True)
                                    last.then_inc(a2_bank, 1)
                                    ready[2 * pair] = ready[2 * pair + 1] = n
                                    n += 1
                            elif lv == LEVELS - 2:
                                for quad in range(4):
                                    U.wait_empty(pe, g, n)
                                    U.wait_taken(pe, g, ready[4 * quad + 3])
                                    for u in range(4 * quad, 4 * quad + 4):
                                        last = nc.tensor.matmul(PS[:, bank_of(n), (u % 4) * P:(u % 4 + 1) * P],
                                                                old[:, u, 0, :], old[:, u, 1, :],
                                                                start=True, stop=True)
                                    last.then_inc(a2_bank, 1)
                                    for u in range(4 * quad, 4 * quad + 4):
                                        ready[u] = n
                                    n += 1
                        U.wait_empty(pe, g, n)
                        U.wait_taken(pe, g, y_use[0])
                        U.wait_taken(pe, g, y_use[1])
                        n_state = n
                        for b in range(2):
                            for h in range(NH):
                                hs = slice(DK * h, DK * h + DK)
                                last = nc.tensor.matmul(PS[hs, bank_of(n), b * DK:(b + 1) * DK], KH[:, 2 * b, hs],
                                                        Y[:, 2 * b, 0, hs], start=True, stop=True)
                        last.then_inc(a2_bank, 1)
                        n += 1
                        U.wait_empty(pe, g, n)
                        n_w1 = n
                        for b in range(2):
                            last = nc.tensor.transpose(PS[:, bank_of(n), b * P:(b + 1) * P], Y[:, 2 * b + 1, 1, :],
                                                       ident)
                        last.then_inc(a2_bank, 1)
                        n += 1
                        U.wait_empty(pe, g, n)
                        U.wait_taken(pe, g, n_state)
                        U.wait_taken(pe, g, n_w1)
                        for b in range(2):
                            last = nc.tensor.matmul(PS[:, bank_of(n), b * P:(b + 1) * P], W1T[:, b, :], SS[:, b, :],
                                                    start=True, stop=True)
                        last.then_inc(a2_bank, 1)
                        n_ws = n
                        n += 1
                        U.wait_empty(pe, g, n)
                        U.wait_taken(pe, g, 14)
                        for t in (0, 2, 1, 3):
                            if t == 1:
                                U.wait_taken(pe, g, n_ws)
                            if t % 2:
                                nc.tensor.matmul(PS[:, bank_of(n), t * P:(t + 1) * P], TQ[:, 0, t, :],
                                                 SS[:, t // 2, :], start=True, stop=False)
                            for h in range(NH):
                                hs = slice(DK * h, DK * h + DK)
                                o = PS[:, bank_of(n), t * P + h * DK:t * P + (h + 1) * DK]
                                last = nc.tensor.matmul(o, AT[:, 4 * h + t, :], Y[:, t, 0, hs],
                                                        start=(t % 2 == 0), stop=(t % 2 == 0 or h == NH - 1))
                        last.then_inc(a2_bank, 1)
                        n += 1
                        assert n == NU

                @block.scalar
                def _(act):
                    a_sqrt(NT * NH)
                    a_sqrt(NT * NH)
                    U.open(act, "A")
                    with act.Fori(0, NG) as g:
                        pair = quad = 0
                        turned = 0
                        lv = -1
                        for n, (what, e) in enumerate(uses):
                            if what == "apply" and uses[n - 1][0] != "apply":
                                lv += 1
                                pair = quad = 0
                            if e != "A":
                                continue
                            U.wait_full(act, g, n)
                            src = PS[:, bank_of(n), :]
                            if what == "turn":
                                dst = TQ[:, turned, :, :]
                                src = tile4(src)
                                turned += 1
                            elif what == "square" and lv < LEVELS - 2:
                                dst = PW[(lv + 1) % 2][:, 2 * pairs[pair]:2 * pairs[pair] + 2, :, :]
                                src = src.rearrange("p (u k c) -> p u k c", u=2, k=2)
                                pair += 1
                            elif what == "square":
                                dst = PW[(lv + 1) % 2][:, 4 * quad:4 * quad + 4, 1, :]
                                src = tile4(src)
                                quad += 1
                            else:
                                dst = W1T[:, :, :]
                                src = PS[:, bank_of(n), 0:256].rearrange("p (b c) -> p b c", b=2)
                            nc.scalar.activation(dst, src, ACT.Copy).then_inc(a2_act, 1)

                @block.vector
                def _(dve):
                    heads = lambda ap: ap.rearrange("p t (h d) -> p (t h) d", h=NH)
                    for src, dst in ((QTK, RQ), (KTK, RK)):
                        V.link(nc.vector.tensor_tensor(NRM[:, :, :], src[:, :, :], src[:, :, :], ALU.mult))
                        V.link(nc.vector.tensor_reduce(RKB[:, :], heads(NRM[:, :, :]), AX.X, ALU.add))
                        v_ask(nc.vector.tensor_scalar(SQA[:, :NT * NH], RKB[:, :], 1e-6, None, ALU.add))
                        v_sqrt(NT * NH)
                        V.link(nc.vector.reciprocal(dst[:, :], SQR[:, :NT * NH]))
                    V.link(nc.vector.tensor_tensor(RKB[:, :], RK[:, :], BETA[:, :, :].rearrange("p t h -> p (t h)"),
                                                   ALU.mult))
                    dve.wait_ge(ss_zero, 1)
                    per_chain = 17
                    U.open(dve, "V")
                    with dve.Fori(0, NG) as g:
                        V.enter(g, per_chain)
                        tiles = bass.ds(g * 4, 4)
                        gh = bass.ds(g * 16, 16)
                        four = lambda ap: ap.rearrange("p (t h) d -> p t h d", t=4)
                        sc = lambda r: r[:, gh].unsqueeze(2).to_broadcast([P, 16, DK])
                        h4 = lambda ap: ap.rearrange("p t (h d) -> p (t h) d", h=NH)
                        hy = lambda k: Y[:, :, k, :].rearrange("p t (h d) -> p t h d", h=NH)
                        sc4 = lambda r: r.rearrange("p (t h) -> p t h", t=4).unsqueeze(3).to_broadcast([P, 4, NH, DK])
                        nc.vector.tensor_tensor(h4(QH[:, :, :]), h4(QTK[:, tiles, :]), sc(RQ), ALU.mult)\
                            .then_inc(a2_prep, 1)
                        nc.vector.tensor_tensor(h4(KH[:, :, :]), h4(KTK[:, tiles, :]), sc(RK), ALU.mult)\
                            .then_inc(a2_prep, 1)
                        nc.vector.tensor_tensor(hy(1), KTK[:, tiles, :].rearrange("p t (h d) -> p t h d", h=NH),
                                                sc4(RKB[:, gh]), ALU.mult).then_inc(a2_prep, 1)
                        nc.vector.tensor_tensor(hy(0), VTK[:, tiles, :].rearrange("p t (h d) -> p t h d", h=NH),
                                                BETA[:, tiles, :].unsqueeze(3).to_broadcast([P, 4, NH, DK]),
                                                ALU.mult).then_inc(a2_prep, 1)
                        taps_done = []

                        def tap(acc, filt, base, k):
                            ins = nc.vector.scalar_tensor_tensor(
                                out=acc[:, :, :], in0=VPT[:, :, bass.ds(k + base, L)],
                                scalar=pa(filt)[:, bass.ds(k, 1)], in1=acc[:, :, :], op0=ALU.mult, op1=ALU.add)
                            taps_done.append(V.mark(ins))

                        def long_tap():
                            k = len(taps_done) - 1
                            if k >= 2:
                                dve.wait_ge(dve_step, taps_done[-2])
                            tap((FL0, FL1)[k % 2], "firl", 0, g * 16 + k)

                        dve.wait_ge(dve_step, g * per_chain + V.done)
                        tap(FS, "firs", PAD - FIRS, g)
                        long_tap()
                        long_tap()
                        masks, lv = 0, 0
                        for n, (what, e) in enumerate(uses):
                            if e != "V":
                                continue
                            U.wait_full(dve, g, n)
                            src = PS[:, bank_of(n), :]
                            if what == "mask":
                                kind, h = divmod(masks, NH)
                                dst = (PW[0][:, 4 * h:4 * h + 4, 0, :], PW[0][:, 4 * h:4 * h + 4, 1, :],
                                       AT[:, 4 * h:4 * h + 4, :])[kind]
                                nc.vector.tensor_tensor(dst, tile4(src), rows(pa(("low", "upp", "incl")[kind]), 4),
                                                        ALU.mult).then_inc(a2_dve, 1)
                                masks += 1
                            elif what == "apply":
                                half = lv % 2
                                yy = Y[:, 2 * half:2 * half + 2, :, :].rearrange("p t k c -> p (t k c)")
                                nc.vector.tensor_tensor(yy, yy, src, ALU.add).then_inc(a2_dve, 1)
                                lv += 1
                                if half:
                                    long_tap()
                                    long_tap()
                            elif what == "state":
                                for h in range(NH):
                                    hs = slice(DK * h, DK * h + DK)
                                    last = nc.vector.tensor_copy(SS[hs, :, hs], PS[hs, bank_of(n), 0:2 * DK].rearrange(
                                        "p (b c) -> p b c", b=2))
                                last.then_inc(a2_dve, 1)
                            elif what == "ws":
                                yy = Y[:, 1:4:2, 0, :]
                                nc.vector.tensor_tensor(yy, yy, PS[:, bank_of(n), 0:256].rearrange(
                                    "p (b c) -> p b c", b=2), ALU.subtract).then_inc(a2_dve, 1)
                            else:
                                nc.vector.tensor_copy(DEL[:, tiles, :], tile4(src)).then_inc(a2_dve, 1)
                        assert len(taps_done) == 17
                        V.leave(NG)

        s3 = ExitStack()
        with s3:
            STK = QTK
            LTK = KTK
            SF = sbuf(s3, "SF", [P, NT, NH, DK])
            GH = sbuf(s3, "GH", [P, NH, 512])
            LG = sbuf(s3, "LG", [P, NT, 16])
            TMP = sbuf(s3, "TMP", [P, NT, D])
            SM = sbuf(s3, "SM", [P, 6, 64])
            GC = sbuf(s3, "GC", [P, 4, 16])
            WO = sbuf(s3, "WO", [P, D])
            long_ready, sf_zero, gate_const = sem("long_ready"), sem("sf_zero"), sem("gate_const")
            a3_hid, a3_gelu, a3_log, a3_lg = sem("a3_hid"), sem("a3_gelu"), sem("a3_log"), sem("a3_lg")
            a3_need, a3_exp, wo_ready, a3_out, src_ready = (sem("a3_need"), sem("a3_exp"), sem("wo_ready"),
                                                            sem("a3_out"), sem("src_ready"))
            with nc.Block() as block:
                @block.gpsimd
                def _(pool):
                    nc.gpsimd.memset(SF[:, :, :, 16:32], 0.0).then_inc(sf_zero, 1)

                @block.tensor
                def _(pe):
                    p_transpose(lambda t: FS[:, t // 2, (t % 2) * P:(t % 2 + 1) * P], ready=False)
                    pe.wait_ge(long_ready, 1)
                    p_transpose(lambda t: FL0[:, t // 2, (t % 2) * P:(t % 2 + 1) * P], (4, 5, 6, 7), ready=False)
                    p_copied()
                    pe.wait_ge(sf_zero, 1)
                    p_transpose(lambda t: SF[:, t, :, :].rearrange("p h s -> p (h s)"))
                    p_copied()
                    pe.sem_inc(a3_log, 1)
                    with pe.Fori(0, NG) as g:
                        for h in range(NH):
                            nc.tensor.matmul(PS[:, h, :].rearrange("p (b l) -> p b l", b=2), pa("gw1h"),
                                             XT[:, bass.ds(g * 2, 2), 3:3 + L], start=True, stop=False)
                            nc.tensor.matmul(PS[:, h, :], pa("gw1s")[:, h * P:(h + 1) * P],
                                             TR[:, bass.ds(g * 512, 512)], start=False, stop=True)\
                                .then_inc(a3_hid, 1)
                        pe.wait_ge(a3_lg, g + 1)
                        for h in range(NH):
                            pe.wait_ge(a3_gelu, g * NH + (h + 1))
                            for t in range(4):
                                at = t * 16 + h * 4
                                last = nc.tensor.matmul(PS[:, 4, at:at + 4], GH[:, h, t * P:(t + 1) * P],
                                                        pa("gw2"), start=True, stop=True)
                        last.then_inc(a3_log, 1)
                    p_transpose(lambda t: TMP[:, t, :])
                    p_copied()
                    pe.wait_ge(wo_ready, 1)
                    for t in range(NT):
                        last = nc.tensor.matmul(PS[:, 4 + t // 4, (t % 4) * P:(t % 4 + 1) * P],
                                                TR[:, t * P:(t + 1) * P], WO[:, :], start=True, stop=True)
                        if t % 4 == 3:
                            last.then_inc(a3_out, 1)

                @block.scalar
                def _(act):
                    a_transposed(lambda j: STK[:, 4 * j:4 * j + 4, :].rearrange("p t c -> p (t c)"))
                    a_transposed(lambda j: LTK[:, 4 * j:4 * j + 4, :].rearrange("p t c -> p (t c)"), (4, 5, 6, 7))
                    a_sqrt(256)
                    a_transposed(lambda j: TR[:, j * 512:(j + 1) * 512])
                    with act.Fori(0, NG) as g:
                        act.wait_ge(a3_log, g + 1)
                        for h in range(NH):
                            act.wait_ge(a3_hid, g * NH + (h + 1))
                            nc.scalar.activation(GH[:, h, :], PS[:, h, :], ACT.Gelu, bias=pa("gb1"))\
                                .then_inc(a3_gelu, 1)
                    nc.scalar.activation(GC[:, 3, 0:4], pa("crl"), ACT.Sigmoid).then_inc(gate_const, 1)
                    nc.scalar.activation(GC[:, 1, :], pa("floor"), ACT.Sigmoid).then_inc(gate_const, 1)
                    nc.scalar.activation(GC[:, 0, :], pa("ltemp"), ACT.Exp, scale=-1.0).then_inc(gate_const, 1)
                    act.wait_ge(a3_need, 1)
                    nc.scalar.activation(LG[:, :, :], LG[:, :, :], ACT.Exp).then_inc(a3_exp, 1)
                    a_sqrt(NT * NH)
                    a_transposed(lambda j: TR[:, j * 512:(j + 1) * 512])
                    a_sqrt(NT)

                @block.vector
                def _(dve):
                    flat = lambda ap: ap.rearrange("p t c -> p (t c)")
                    per_head = lambda ap: ap.rearrange("p t (h d) -> p (t h) d", h=NH)
                    nc.vector.tensor_tensor(FL0[:, :, :], FL0[:, :, :], FL1[:, :, :], ALU.add).then_inc(long_ready, 1)
                    nc.vector.tensor_scalar(WO[:, :], pa("wo"), pa("onw"), None, ALU.mult).then_inc(wo_ready, 1)
                    for s, src in ((3, VTK), (2, DEL), (0, STK), (1, LTK)):
                        if s == 0:
                            dve.wait_ge(tr_copied, 8)
                        if s == 1:
                            dve.wait_ge(tr_copied, 12)
                        stat = lambda k: SF[:, :, :, 4 * s + k].rearrange("p t h -> p (t h)")
                        nc.vector.tensor_reduce(SM[:, 0, :], per_head(src[:, :, :]), AX.X, ALU.add)
                        nc.vector.tensor_reduce(SM[:, 1, :], per_head(src[:, :, :]), AX.X, ALU.add,
                                                apply_absolute_value=True)
                        V.link(nc.vector.tensor_tensor(flat(TMP[:, :, :]), flat(src[:, :, :]), flat(src[:, :, :]),
                                                       ALU.mult))
                        V.link(nc.vector.tensor_reduce(SQA[:, s * 64:(s + 1) * 64], per_head(TMP[:, :, :]), AX.X,
                                                       ALU.add))
                        V.link(nc.vector.tensor_scalar(stat(0), SM[:, 0, :], 1.0 / DK, None, ALU.mult))
                        nc.vector.tensor_scalar(stat(2), SM[:, 1, :], 1.0 / DK, None, ALU.mult)
                        V.link(nc.vector.tensor_tensor(SM[:, 2, :], stat(0), stat(0), ALU.mult))
                        V.link(nc.vector.scalar_tensor_tensor(out=stat(1), in0=SQA[:, s * 64:(s + 1) * 64],
                                                              scalar=1.0 / DK, in1=SM[:, 2, :], op0=ALU.mult,
                                                              op1=ALU.subtract))
                    v_ask(nc.vector.tensor_scalar(SM[:, 3, 0:1], SM[:, 2, 0:1], 0.0, None, ALU.mult))
                    v_sqrt(256)
                    last = None
                    for s in range(4):
                        last = nc.vector.tensor_copy(SF[:, :, :, 4 * s + 3].rearrange("p t h -> p (t h)"),
                                                     SQR[:, s * 64:(s + 1) * 64])
                    v_ready(last)
                    dve.sem_inc(a3_lg, 1)
                    with dve.Fori(0, NG) as g:
                        dve.wait_ge(a3_log, g + 2)
                        nc.vector.tensor_copy(LG[:, bass.ds(g * 4, 4), :],
                                              PS[:, 4, 0:64].rearrange("p (t c) -> p t c", t=4)).then_inc(a3_lg, 1)
                    dve.wait_ge(a3_lg, NG + 1)
                    dve.wait_ge(gate_const, 3)
                    quad = lambda ap: ap.rearrange("p t (h s) -> p (t h) s", h=NH)
                    V.link(nc.vector.tensor_tensor(LG[:, :, :], LG[:, :, :], rows(pa("gb2"), NT), ALU.add))
                    V.link(nc.vector.tensor_tensor(LG[:, :, :], LG[:, :, :], rows(GC[:, 0, :], NT), ALU.mult))
                    V.link(nc.vector.tensor_reduce(SM[:, 0, :], quad(LG[:, :, :]), AX.X, ALU.max))
                    nc.vector.tensor_tensor(quad(LG[:, :, :]), quad(LG[:, :, :]), bcast(SM[:, 0, :], 4),
                                            ALU.subtract).then_inc(a3_need, 1)
                    V.link(nc.vector.tensor_scalar(GC[:, 1, :], GC[:, 1, :], FLOOR, None, ALU.mult))
                    V.link(nc.vector.tensor_reduce(GC[:, 2, 0:4], GC[:, 1, :].rearrange("p (h s) -> p h s", h=NH), AX.X,
                                                   ALU.add))
                    V.link(nc.vector.tensor_scalar(GC[:, 2, 0:4], GC[:, 2, 0:4], -1.0, 1.0, ALU.mult, ALU.add))
                    dve.wait_ge(a3_exp, 1)
                    V.link(nc.vector.tensor_reduce(SM[:, 0, :], quad(LG[:, :, :]), AX.X, ALU.add))
                    V.link(nc.vector.reciprocal(SM[:, 1, :], SM[:, 0, :]))
                    by_head = lambda k: SM[:, k, :].rearrange("p (t h) -> p t h", t=NT)
                    V.link(nc.vector.tensor_tensor(by_head(1), by_head(1), rows(GC[:, 2, 0:4], NT), ALU.mult))
                    V.link(nc.vector.tensor_tensor(quad(LG[:, :, :]), quad(LG[:, :, :]), bcast(SM[:, 1, :], 4),
                                                   ALU.mult))
                    V.link(nc.vector.tensor_tensor(LG[:, :, :], LG[:, :, :], rows(GC[:, 1, :], NT), ALU.add))
                    weight = lambda s: LG[:, :, :].rearrange("p t (h s) -> p (t h) s", h=NH)[:, :, s]
                    V.link(nc.vector.tensor_tensor(LG[:, :, 0:16:4], LG[:, :, 0:16:4], rows(GC[:, 3, 0:4], NT),
                                                   ALU.add))
                    for s, src in enumerate((STK, LTK, DEL, VTK)):
                        nc_last = nc.vector.tensor_tensor(per_head(src[:, :, :]), per_head(src[:, :, :]),
                                                          weight(s).unsqueeze(2).to_broadcast([P, NT * NH, DK]),
                                                          ALU.mult)
                    V.link(nc_last)
                    alpha_rows = pa("alpha").unsqueeze(1).unsqueeze(3).to_broadcast([P, NT, NH, DK])
                    V.link(nc.vector.tensor_tensor(ITK[:, :, :].rearrange("p t (h d) -> p t h d", h=NH),
                                                   ITK[:, :, :].rearrange("p t (h d) -> p t h d", h=NH), alpha_rows,
                                                   ALU.mult))
                    nc.vector.tensor_tensor(flat(STK[:, :, :]), flat(STK[:, :, :]), flat(LTK[:, :, :]), ALU.add)
                    V.link(nc.vector.tensor_tensor(flat(DEL[:, :, :]), flat(DEL[:, :, :]), flat(VTK[:, :, :]), ALU.add))
                    V.link(nc.vector.tensor_tensor(flat(STK[:, :, :]), flat(STK[:, :, :]), flat(DEL[:, :, :]), ALU.add))
                    V.link(nc.vector.tensor_tensor(flat(STK[:, :, :]), flat(STK[:, :, :]), flat(ITK[:, :, :]), ALU.add))
                    V.link(nc.vector.tensor_tensor(flat(TMP[:, :, :]), flat(STK[:, :, :]), flat(STK[:, :, :]), ALU.mult))
                    V.link(nc.vector.tensor_reduce(SM[:, 0, :], per_head(TMP[:, :, :]), AX.X, ALU.add))
                    v_ask(nc.vector.tensor_scalar(SQA[:, :64], SM[:, 0, :], 1.0 / DK, 1e-5, ALU.mult, ALU.add))
                    v_sqrt(64)
                    V.link(nc.vector.reciprocal(SM[:, 1, :], SQR[:, :64]))
                    v_ready(nc.vector.tensor_tensor(per_head(TMP[:, :, :]), per_head(STK[:, :, :]),
                                                    bcast(SM[:, 1, :], DK), ALU.mult))
                    dve.wait_ge(a3_out, 4)
                    V.link(v_norm(lambda t: PS[:, 4 + t // 4, (t % 4) * P:(t % 4 + 1) * P], lambda t: NRM[:, t, :]))
                    V.link(nc.vector.tensor_tensor(flat(X[:, :, :]), flat(X[:, :, :]), flat(NRM[:, :, :]), ALU.add))
        sa.close()

        PC = sbuf(ctx, "PC", [P, ncc])
        PD = sbuf(ctx, "PD", [P, nd])
        flat = lambda ap: ap.rearrange("p t c -> p (t c)")

        def pc(name, rows_=P):
            at, width = oc[name]
            return PC[0:rows_, at:at + width]

        def pd(name):
            at, width = od[name]
            return PD[:, at:at + width]

        def v_affine(dst, gain, shift):
            V.link(nc.vector.tensor_tensor(dst[:, :, :], dst[:, :, :], rows(gain, NT), ALU.mult))
            return nc.vector.tensor_tensor(dst[:, :, :], dst[:, :, :], rows(shift, NT), ALU.add)

        sb = ExitStack()
        with sb:
            QKV = sbuf(sb, "QKV", [P, NT, 384])
            PR = sbuf(sb, "PR", [P, 64, DK])
            OB = sbuf(sb, "OB", [P, NT, D])
            SC = sbuf(sb, "SC", [P, 2, NH, B, B])
            SR = sbuf(sb, "SR", [P, 64])
            MS = sbuf(sb, "MS", [P, NT, E])
            LE = sbuf(sb, "LE", [P, NT, E])
            MT = sbuf(sb, "MT", [E, NT * P])
            HID = sbuf(sb, "HID", [P, 2, 4, 512])
            b_qkv, b_qkv_out, b_exp_need, b_exp, b_wo, b_logit, b_bias = (
                sem("b_qkv"), sem("b_qkv_out"), sem("b_exp_need"), sem("b_exp"), sem("b_wo"), sem("b_logit"),
                sem("b_bias"))
            moe_full, moe_act, moe_dve = sem("moe_full"), sem("moe_act"), sem("moe_dve")
            copied0 = count["tr_p"]
            with nc.Block() as block:
                @block.sync
                def _(sp):
                    sp.dma_start(PC[:, :], pc_in).then_inc(loadC, 16)
                    sp.dma_start(PD[:, :], pd_in).then_inc(loadD, 16)

                @block.tensor
                def _(pe):
                    p_transpose(lambda t: NRM[:, t, :])
                    p_copied()
                    for t in range(NT):
                        if t >= 8:
                            pe.wait_ge(b_qkv_out, t - 7)
                        nc.tensor.matmul(PS[:, t % 8, 0:384], TR[:, t * P:(t + 1) * P], pb("wqkv"), start=True,
                                         stop=True).then_inc(b_qkv, 1)
                    pe.wait_ge(b_qkv_out, NT)
                    p_transpose(lambda t: OB[:, t, :])
                    p_copied()
                    for t in range(NT):
                        last = nc.tensor.matmul(PS[:, 4 + t // 4, (t % 4) * P:(t % 4 + 1) * P],
                                                TR[:, t * P:(t + 1) * P], pb("wo"), start=True, stop=True)
                    last.then_inc(b_wo, 1)
                    p_transpose(lambda t: NRM[:, t, :])
                    p_copied()
                    for t in range(NT):
                        last = nc.tensor.matmul(PS[:, 4, t * E:(t + 1) * E], TR[:, t * P:(t + 1) * P], pb("wg"),
                                                start=True, stop=True)
                    last.then_inc(b_logit, 1)
                    count["norm_p"] += 1
                    pe.wait_ge(norm_ready, count["norm_p"])
                    for j in range(4):
                        for t in range(4):
                            last = nc.tensor.transpose(PS[0:E, j, t * P:(t + 1) * P], MS[:, 4 * j + t, :], ident)
                        last.then_inc(tr_bank, 1)
                    count["tr_p"] += 4
                    p_copied()
                    for t in range(NT):
                        last = nc.tensor.matmul(PS[:, 4 + t // 4, (t % 4) * P:(t % 4 + 1) * P],
                                                MT[:, t * P:(t + 1) * P], pb("b2", E), start=True, stop=True)
                    last.then_inc(b_bias, 1)

                @block.scalar
                def _(act):
                    a_sqrt(NT)
                    a_transposed(lambda j: TR[:, j * 512:(j + 1) * 512])
                    act.wait_ge(b_exp_need, 1)
                    nc.scalar.activation(SC[:, :, :, :, :].rearrange("p f h q k -> p (f h q k)"),
                                         SC[:, :, :, :, :].rearrange("p f h q k -> p (f h q k)"), ACT.Exp)\
                        .then_inc(b_exp, 1)
                    a_transposed(lambda j: TR[:, j * 512:(j + 1) * 512])
                    a_sqrt(NT)
                    a_transposed(lambda j: TR[:, j * 512:(j + 1) * 512])
                    for j in range(4):
                        count["tr_a"] += 1
                        act.wait_ge(tr_bank, count["tr_a"])
                        nc.scalar.activation(MT[:, j * 512:(j + 1) * 512], PS[0:E, j, :], ACT.Copy)\
                            .then_inc(tr_copied, 1)

                @block.vector
                def _(dve):
                    v_ready(v_norm(lambda t: X[:, t, :], lambda t: NRM[:, t, :]))
                    for t in range(NT):
                        dve.wait_ge(b_qkv, t + 1)
                        nc.vector.tensor_tensor(QKV[:, t, :], PS[:, t % 8, 0:384], pb("bqkv"), ALU.add)\
                            .then_inc(b_qkv_out, 1)
                    dve.wait_ge(b_qkv_out, NT)
                    part = lambda f, h, k: QKV[:, f:NT:2, k * D + h * DK:k * D + (h + 1) * DK]
                    for f in range(2):
                        for h in range(NH):
                            q = part(f, h, 0).unsqueeze(2).to_broadcast([P, B, B, DK])
                            k = part(f, h, 1).unsqueeze(1).to_broadcast([P, B, B, DK])
                            V.link(nc.vector.tensor_tensor(PR[:, :, :].rearrange("p (a b) d -> p a b d", a=B), q, k,
                                                           ALU.mult))
                            V.link(nc.vector.tensor_reduce(SC[:, f, h, :, :].rearrange("p q k -> p (q k)"),
                                                           PR[:, :, :], AX.X, ALU.add))
                    scores = SC[:, :, :, :, :].rearrange("p f h q k -> p (f h q) k")
                    V.link(nc.vector.tensor_scalar(scores, scores, 1.0 / math.sqrt(DK), None, ALU.mult))
                    V.link(nc.vector.tensor_reduce(SR[:, :], scores, AX.X, ALU.max))
                    nc.vector.tensor_tensor(scores, scores, bcast(SR[:, :], B), ALU.subtract).then_inc(b_exp_need, 1)
                    dve.wait_ge(b_exp, 1)
                    V.link(nc.vector.tensor_reduce(SR[:, :], scores, AX.X, ALU.add))
                    V.link(nc.vector.reciprocal(SR[:, :], SR[:, :]))
                    V.link(nc.vector.tensor_tensor(scores, scores, bcast(SR[:, :], B), ALU.mult))
                    for f in range(2):
                        for h in range(NH):
                            a = SC[:, f, h, :, :].unsqueeze(2).to_broadcast([P, B, DK, B])
                            v = part(f, h, 2).rearrange("p b d -> p d b").unsqueeze(1).to_broadcast([P, B, DK, B])
                            pr = PR[:, :, :].rearrange("p (a x) (y b) -> p a (x y) b", a=B, b=B)
                            V.link(nc.vector.tensor_tensor(pr, a, v, ALU.mult))
                            last = nc.vector.tensor_reduce(OB[:, f:NT:2, h * DK:(h + 1) * DK], pr, AX.X, ALU.add)
                            if f < 1 or h < NH - 1:
                                V.link(last)
                    v_ready(last)
                    dve.wait_ge(b_wo, 1)
                    V.link(nc.vector.tensor_tensor(NRM[:, :, :], NRM[:, :, :], rows(pb("bo"), NT), ALU.add))
                    for j in range(4):
                        last = nc.vector.tensor_tensor(NRM[:, 4 * j:4 * j + 4, :], NRM[:, 4 * j:4 * j + 4, :],
                                                       tile4(PS[:, 4 + j, :]), ALU.add)
                    V.link(last)
                    V.link(v_norm(lambda t: NRM[:, t, :], lambda t: NRM[:, t, :]))
                    v_ready(v_affine(NRM, pb("g1"), pb("be1")))
                    dve.wait_ge(b_logit, 1)
                    V.link(nc.vector.tensor_copy(LE[:, :, :], PS[:, 4, 0:NT * E].rearrange("p (t e) -> p t e", t=NT)))
                    V.link(nc.vector.tensor_reduce(SR[:, 0:NT], LE[:, :, :], AX.X, ALU.max))
                    V.link(nc.vector.tensor_tensor(LE[:, :, :], LE[:, :, :], bcast(SR[:, 0:NT], E), ALU.is_equal))
                    V.link(nc.vector.tensor_tensor(LE[:, :, :], LE[:, :, :], rows(pb("iota"), NT), ALU.mult))
                    V.link(nc.vector.tensor_reduce(SR[:, 0:NT], LE[:, :, :], AX.X, ALU.min))
                    v_ready(nc.vector.tensor_tensor(MS[:, :, :], rows(pb("iota"), NT), bcast(SR[:, 0:NT], E),
                                                    ALU.is_equal))
                    dve.wait_ge(b_bias, 1)
                    for j in range(4):
                        nc.vector.tensor_tensor(OB[:, 4 * j:4 * j + 4, :], NRM[:, 4 * j:4 * j + 4, :],
                                                tile4(PS[:, 4 + j, :]), ALU.add)

            engines, order = [], []
            for e in range(E + 1):
                if e < E:
                    order += [("up", e, c) for c in range(4)]
                if e >= 1:
                    order.append(("down", e - 1, 0))
            engines = ["A" if k == "up" else "V" for k, _, _ in order]
            U = Uses(moe_full, {"A": moe_act, "V": moe_dve}, engines)
            where = {k: n for n, k in enumerate(order)}
            with nc.Block() as block:
                @block.tensor
                def _(pe):
                    with pe.Fori(0, NG) as g:
                        U.wait_start(pe, g)
                        for n, (kind, e, c) in enumerate(order):
                            U.wait_empty(pe, g, n)
                            if kind == "up":
                                at = e * DF + c * P
                                last = nc.tensor.matmul(PS[:, n % 8, :], pb("w1")[:, at:at + P],
                                                        TR[:, bass.ds(g * 512, 512)], start=True, stop=True)
                            else:
                                U.wait_taken(pe, g, where[("up", e, 3)])
                                for t in range(4):
                                    for k in range(4):
                                        last = nc.tensor.matmul(PS[:, n % 8, t * P:(t + 1) * P],
                                                                HID[:, e % 2, k, t * P:(t + 1) * P],
                                                                pb("w2")[:, (4 * e + k) * P:(4 * e + k + 1) * P],
                                                                start=(k == 0), stop=(k == 3))
                            last.then_inc(moe_full, 1)

                @block.scalar
                def _(act):
                    U.open(act, "A")
                    with act.Fori(0, NG) as g:
                        for n, (kind, e, c) in enumerate(order):
                            if kind == "up":
                                if e >= 2:
                                    U.wait_full(act, g, where[("down", e - 2, 0)])
                                U.wait_full(act, g, n)
                                at = 4 * e + c
                                nc.scalar.activation(HID[:, e % 2, c, :], PS[:, n % 8, :], ACT.Relu,
                                                     bias=pb("b1")[:, at:at + 1]).then_inc(moe_act, 1)

                @block.vector
                def _(dve):
                    U.open(dve, "V")
                    with dve.Fori(0, NG) as g:
                        for n, (kind, e, c) in enumerate(order):
                            if kind == "down":
                                U.wait_full(dve, g, n)
                                if e:
                                    U.wait_taken(dve, g, where[("down", e - 1, 0)])
                                for t in range(4):
                                    acc = OB[:, bass.ds(g * 4 + t, 1), :].rearrange("p t c -> p (t c)")
                                    last = nc.vector.scalar_tensor_tensor(
                                        out=acc, in0=PS[:, n % 8, t * P:(t + 1) * P],
                                        scalar=MS[:, bass.ds(g * 4 + t, 1), e], in1=acc, op0=ALU.mult, op1=ALU.add)
                                last.then_inc(moe_dve, 1)

            with nc.Block() as block:
                @block.scalar
                def _(act):
                    a_sqrt(NT)
                    a_sqrt(NT)

                @block.vector
                def _(dve):
                    V.link(v_norm(lambda t: OB[:, t, :], lambda t: NRM[:, t, :]))
                    V.link(v_affine(NRM, pb("g2"), pb("be2")))
                    V.link(v_norm(lambda t: NRM[:, t, :], lambda t: NRM[:, t, :]))
                    V.link(nc.vector.tensor_tensor(flat(X[:, :, :]), flat(X[:, :, :]), flat(NRM[:, :, :]), ALU.add))

        sc_ = ExitStack()
        with sc_:
            XL = sbuf(sc_, "XL", [P, NT, D])
            VXT = sbuf(sc_, "VXT", [P, NT, VX])
            CT = sbuf(sc_, "CT", [P, NT, H2])
            BD = sbuf(sc_, "BD", [P, 4, H2])
            WEF = sbuf(sc_, "WEF", [P, H2])
            CRW = sbuf(sc_, "CRW", [P, H2])
            BQS = sbuf(sc_, "BQS", [P, 4])
            QF = sbuf(sc_, "QF", [P, 4, L])
            KF = sbuf(sc_, "KF", [P, 4, L])
            MX = sbuf(sc_, "MX", [P, 2, 4, P])
            PT = sbuf(sc_, "PT", [P, 4, 2, L])
            UB = sbuf(sc_, "UB", [P, H2, 2, VX])
            CM = sbuf(sc_, "CM", [P, 2 * H2, R2])
            RI = sbuf(sc_, "RI", [P, 3, 2 * H2])
            UP = sbuf(sc_, "UP", [P, 2 * H2, HD2, R2])
            OC = sbuf(sc_, "OC", [P, NT, D])
            HR = sbuf(sc_, "HR", [P, 2, NT * P])
            c_zero, c_bd, c_w, c_wef, c_v, c_vout, c_ct = (sem("c_zero"), sem("c_bd"), sem("c_w"), sem("c_wef"),
                                                           sem("c_v"), sem("c_vout"), sem("c_ct"))
            with nc.Block() as block:
                @block.gpsimd
                def _(pool):
                    nc.gpsimd.memset(BD[:, :, :], 0.0).then_inc(c_zero, 1)
                    nc.gpsimd.memset(MX[:, :, :, :], 0.0).then_inc(c_zero, 1)
                    nc.gpsimd.memset(VXT[:, :, VX - 1:VX], 1.0).then_inc(c_zero, 1)

                @block.tensor
                def _(pe):
                    pe.wait_ge(c_bd, 1)
                    for c in range(4):
                        nc.tensor.matmul(PS[:, 6, 0:H2], pc("wqv")[:, c * P:(c + 1) * P], BD[:, c, :],
                                         start=(c == 0), stop=(c == 3))
                    for c in range(4):
                        last = nc.tensor.matmul(PS[:, 7, 0:H2], pc("bqv")[:, c:c + 1].to_broadcast([P, P]),
                                                BD[:, c, :], start=(c == 0), stop=(c == 3))
                    last.then_inc(c_w, 1)
                    p_transpose(lambda t: NRM[:, t, :])
                    p_copied()
                    for t in range(NT):
                        last = nc.tensor.matmul(PS[:, 4 + t // 8, (t % 8) * 64:(t % 8 + 1) * 64],
                                                TR[:, t * P:(t + 1) * P], pc("wv"), start=True, stop=True)
                    last.then_inc(c_v, 1)
                    pe.wait_ge(c_wef, 1)
                    for t in range(NT):
                        last = nc.tensor.matmul(PS[:, 6, t * H2:(t + 1) * H2], TR[:, t * P:(t + 1) * P], WEF[:, :],
                                                start=True, stop=True)
                    last.then_inc(c_ct, 1)

                @block.scalar
                def _(act):
                    a_sqrt(NT)
                    a_sqrt(NT)
                    a_transposed(lambda j: TR[:, j * 512:(j + 1) * 512])

                @block.vector
                def _(dve):
                    dve.wait_ge(loadC, 16)
                    dve.wait_ge(c_zero, 1)
                    for c in range(4):
                        last = nc.vector.tensor_scalar(BD[:, c, 4 * c:4 * c + 4], pc("mask4"), pc("wsq"), None,
                                                       ALU.mult)
                    last.then_inc(c_bd, 1)
                    nc.vector.tensor_scalar(BQS[:, :], pc("bq"), 1.0 / math.sqrt(HD2), None, ALU.mult)
                    V.link(v_norm(lambda t: X[:, t, :], lambda t: XL[:, t, :]))
                    V.link(v_norm(lambda t: XL[:, t, :], lambda t: NRM[:, t, :]))
                    v_ready(v_affine(NRM, pc("g1"), pc("b1")))
                    dve.wait_ge(c_w, 1)
                    nc.vector.tensor_scalar(CRW[:, :], PS[:, 7, 0:H2], 1.0 / math.sqrt(QK2), pc("bs"), ALU.mult,
                                            ALU.add)
                    nc.vector.tensor_scalar(WEF[:, :], PS[:, 6, 0:H2], 1.0 / math.sqrt(QK2), None, ALU.mult)\
                        .then_inc(c_wef, 1)
                    dve.wait_ge(c_v, 1)
                    for j in range(2):
                        last = nc.vector.tensor_tensor(VXT[:, 8 * j:8 * j + 8, 0:64],
                                                       PS[:, 4 + j, :].rearrange("p (t c) -> p t c", t=8),
                                                       rows(pc("bv"), 8), ALU.add)
                    V.link(last)
                    prod = UP[:, :, :, :].rearrange("p a b c -> p (a b c)")[:, 0:NT * 64]
                    V.link(nc.vector.tensor_tensor(prod.rearrange("p (t r d) -> p t r d", t=NT, r=R2),
                                                   VXT[:, :, 0:64].rearrange("p t (r d) -> p t r d", r=R2),
                                                   pc("wso").unsqueeze(1).unsqueeze(1).to_broadcast([P, NT, R2, HD2]),
                                                   ALU.mult))
                    nc.vector.tensor_reduce(VXT[:, :, 64:72], prod.rearrange("p (t r d) -> p t r d", t=NT, r=R2), AX.X,
                                            ALU.add)
                    dve.wait_ge(c_ct, 1)
                    V.link(nc.vector.tensor_tensor(CT[:, :, :], PS[:, 6, 0:NT * H2].rearrange("p (t h) -> p t h", t=NT),
                                                   rows(CRW[:, :], NT), ALU.add))

            LAG = 2
            order = [("q", 0), ("q", 1), ("k", 0), ("k", 1)] + [("max", h) for h in range(H2)]
            order += [("turn", 0), ("turn", 1)]
            for h in range(H2 + LAG):
                if h < H2:
                    order.append(("exp", h))
                if h >= LAG and h % 2:
                    order.append(("out", (h - LAG) // 2))
            who = {"q": "A", "k": "V", "max": "V", "turn": "V", "exp": "A", "out": "V"}
            c_full, c_act, c_dve, c_e_need, c_e = (sem("c_full"), sem("c_act"), sem("c_dve"), sem("c_e_need"),
                                                   sem("c_e"))
            U = Uses(c_full, {"A": c_act, "V": c_dve}, [who[k] for k, _ in order])
            where = {k: n for n, k in enumerate(order)}
            with nc.Block() as block:
                @block.tensor
                def _(pe):
                    with pe.Fori(0, B) as b:
                        U.wait_start(pe, b)
                        xb = TR[:, bass.ds(b * L, L)]
                        for n, (kind, k) in enumerate(order):
                            bank = PS[:, n % 8, :]
                            if kind == "max" and k % 4 == 0:
                                U.wait_taken(pe, b, where[("q", k // 8)])
                                U.wait_taken(pe, b, where[("k", k // 8)])
                                for i in range(4):
                                    U.wait_empty(pe, b, n + i)
                                for f in range(2):
                                    for i in range(4):
                                        hs = slice(32 * i, 32 * i + HD2)
                                        last = nc.tensor.matmul(PS[:, (n + i) % 8, f * L:(f + 1) * L],
                                                                QF[hs, k // 4, f * P:(f + 1) * P], KF[hs, k // 4, :],
                                                                start=True, stop=True)
                                        if f:
                                            last.then_inc(c_full, 1)
                                continue
                            if kind == "max":
                                continue
                            U.wait_empty(pe, b, n)
                            if kind in "qk":
                                w = pc("wq" if kind == "q" else "wk")
                                for t in (2 * k, 2 * k + 1):
                                    last = nc.tensor.matmul(bank[:, (t % 2) * L:(t % 2 + 1) * L],
                                                            w[:, t * P:(t + 1) * P], xb, start=True, stop=True)
                            elif kind == "turn":
                                U.wait_taken(pe, b, where[("max", 8 * k + 7)])
                                for t in (2 * k, 2 * k + 1):
                                    for f in range(2):
                                        at = (t % 2) * L + f * P
                                        last = nc.tensor.transpose(bank[:, at:at + P], MX[:, f, t, :], ident)
                            elif kind == "exp":
                                if k % 8 == 0:
                                    U.wait_taken(pe, b, where[("turn", k // 8)])
                                hs = slice(32 * (k % 4), 32 * (k % 4) + HD2 + 1)
                                for c in range(2):
                                    last = nc.tensor.matmul(bank[:, c * L:(c + 1) * L],
                                                            KF[hs, k // 4, c * P:(c + 1) * P], QF[hs, k // 4, :],
                                                            start=True, stop=True)
                            else:
                                U.wait_taken(pe, b, where[("exp", 2 * k + 1)])
                                for h in (2 * k, 2 * k + 1):
                                    for f in range(2):
                                        at = ((h % 2) * 2 + f) * VX
                                        for c in range(2):
                                            v = VXT[:, bass.ds(b * 2 + c, 1), :].rearrange("p t c -> p (t c)")
                                            last = nc.tensor.matmul(bank[:, at:at + VX],
                                                                    PT[:, h % 4, c, f * P:(f + 1) * P], v,
                                                                    start=(c == 0), stop=(c == 1))
                            last.then_inc(c_full, 1)

                @block.scalar
                def _(act):
                    U.open(act, "A")
                    with act.Fori(0, B) as b:
                        for n, (kind, k) in enumerate(order):
                            bank = PS[:, n % 8, :]
                            if kind == "q":
                                U.wait_full(act, b, n)
                                for t in (2 * k, 2 * k + 1):
                                    last = nc.scalar.activation(QF[:, t, :], bank[:, (t % 2) * L:(t % 2 + 1) * L],
                                                                ACT.Identity, bias=BQS[:, t:t + 1],
                                                                scale=1.0 / math.sqrt(HD2))
                                last.then_inc(c_act, 1)
                            elif kind == "exp":
                                if k >= 4:
                                    U.wait_full(act, b, where[("out", (k - 4) // 2)])
                                U.wait_full(act, b, n)
                                nc.scalar.activation(PT[:, k % 4, :, :],
                                                     bank.rearrange("p (c q) -> p c q", c=2), ACT.Exp).then_inc(c_act, 1)
                        act.wait_ge(c_e_need, b + 1)
                        nc.scalar.activation(CM[:, :, :], CM[:, :, :], ACT.Exp).then_inc(c_e, 1)

                @block.vector
                def _(dve):
                    U.open(dve, "V")
                    with dve.Fori(0, B) as b:
                        V.enter(b, 10)
                        for n, (kind, k) in enumerate(order):
                            bank = PS[:, n % 8, :]
                            if kind in ("q", "exp"):
                                continue
                            U.wait_full(dve, b, n)
                            if kind == "k":
                                nc.vector.tensor_tensor(KF[:, 2 * k:2 * k + 2, :],
                                                        bank.rearrange("p (t q) -> p t q", t=2),
                                                        bcast(pc("bk")[:, 2 * k:2 * k + 2], L), ALU.add)\
                                    .then_inc(c_dve, 1)
                            elif kind == "max":
                                nc.vector.tensor_reduce(MX[:, :, k // 4, 32 * (k % 4) + HD2],
                                                        bank.rearrange("p (f q) -> p f q", f=2), AX.X, ALU.max,
                                                        negate=True).then_inc(c_dve, 1)
                            elif kind == "turn":
                                dst = QF[:, 2 * k:2 * k + 2, :]
                                nc.vector.tensor_tensor(dst, dst, bank.rearrange("p (t q) -> p t q", t=2), ALU.add)\
                                    .then_inc(c_dve, 1)
                            else:
                                nc.vector.tensor_copy(UB[:, 2 * k:2 * k + 2, :, :].rearrange("p h f c -> p (h f c)"),
                                                      bank[:, 0:4 * VX]).then_inc(c_dve, 1)
                        U.wait_taken(dve, b, where[("out", H2 // 2 - 1)])
                        ub = UB[:, :, :, :].rearrange("p h f c -> p (h f) c")
                        cm = CM[:, :, :]
                        V.link(nc.vector.reciprocal(RI[:, 0, :], ub[:, :, VX - 1]))
                        V.link(nc.vector.tensor_tensor(cm, ub[:, :, 64:72], bcast(RI[:, 0, :], R2), ALU.mult))
                        ct = CT[:, bass.ds(b * 2, 2), :].rearrange("p f h -> p h f").unsqueeze(3)\
                            .to_broadcast([P, H2, 2, R2])
                        V.link(nc.vector.tensor_tensor(cm.rearrange("p (h f) r -> p h f r", f=2),
                                                       cm.rearrange("p (h f) r -> p h f r", f=2), ct, ALU.add))
                        V.link(nc.vector.tensor_reduce(RI[:, 1, :], cm, AX.X, ALU.max))
                        nc.vector.tensor_tensor(cm, cm, bcast(RI[:, 1, :], R2), ALU.subtract).then_inc(c_e_need, 1)
                        dve.wait_ge(c_e, b + 1)
                        V.link(nc.vector.tensor_reduce(RI[:, 1, :], cm, AX.X, ALU.add))
                        V.link(nc.vector.reciprocal(RI[:, 1, :], RI[:, 1, :]))
                        V.link(nc.vector.tensor_tensor(RI[:, 1, :], RI[:, 1, :], RI[:, 0, :], ALU.mult))
                        V.link(nc.vector.tensor_tensor(cm, cm, bcast(RI[:, 1, :], R2), ALU.mult))
                        V.link(nc.vector.tensor_tensor(UP[:, :, :, :], ub[:, :, 0:64].rearrange("p a (r d) -> p a d r", r=R2),
                                                       cm.unsqueeze(2).to_broadcast([P, 2 * H2, HD2, R2]), ALU.mult))
                        V.link(nc.vector.tensor_reduce(
                            OC[:, bass.ds(b * 2, 2), :].rearrange("p f (h d) -> p h f d", h=H2),
                            UP[:, :, :, :].rearrange("p (h f) d r -> p h f d r", f=2), AX.X, ALU.add))
                        V.leave(B)

            c_wf, c_hid, c_relu, c_ffn = sem("c_wf"), sem("c_hid"), sem("c_relu"), sem("c_ffn")
            with nc.Block() as block:
                @block.tensor
                def _(pe):
                    p_transpose(lambda t: OC[:, t, :], ready=False)
                    p_copied()
                    for t in range(NT):
                        last = nc.tensor.matmul(PS[:, 4 + t // 4, (t % 4) * P:(t % 4 + 1) * P],
                                                TR[:, t * P:(t + 1) * P], pc("wf"), start=True, stop=True)
                    last.then_inc(c_wf, 1)
                    p_transpose(lambda t: NRM[:, t, :])
                    p_copied()
                    for j in range(4):
                        for c in range(2):
                            n = 2 * j + c
                            nc.tensor.matmul(PS[:, n, :], pc("wr1")[:, c * P:(c + 1) * P],
                                             TR[:, j * 512:(j + 1) * 512], start=True, stop=True).then_inc(c_hid, 1)
                    for j in range(4):
                        pe.wait_ge(c_relu, 2 * j + 2)
                        for t in range(4 * j, 4 * j + 4):
                            for c in range(2):
                                last = nc.tensor.matmul(PS[:, j, (t % 4) * P:(t % 4 + 1) * P],
                                                        HR[:, c, t * P:(t + 1) * P], pc("wr2")[:, c * P:(c + 1) * P],
                                                        start=(c == 0), stop=(c == 1))
                        last.then_inc(c_ffn, 1)

                @block.scalar
                def _(act):
                    a_transposed(lambda j: TR[:, j * 512:(j + 1) * 512])
                    a_sqrt(NT)
                    a_transposed(lambda j: TR[:, j * 512:(j + 1) * 512])
                    for n in range(8):
                        act.wait_ge(c_hid, n + 1)
                        nc.scalar.activation(HR[:, n % 2, (n // 2) * 512:(n // 2 + 1) * 512], PS[:, n, :], ACT.Relu,
                                             bias=pc("br1")[:, n % 2:n % 2 + 1]).then_inc(c_relu, 1)
                    a_sqrt(NT)

                @block.vector
                def _(dve):
                    V.link(nc.vector.tensor_tensor(XL[:, :, :], XL[:, :, :], rows(pc("bf"), NT), ALU.add))
                    dve.wait_ge(c_wf, 1)
                    for j in range(4):
                        last = nc.vector.tensor_tensor(XL[:, 4 * j:4 * j + 4, :], XL[:, 4 * j:4 * j + 4, :],
                                                       tile4(PS[:, 4 + j, :]), ALU.add)
                    V.link(last)
                    V.link(v_norm(lambda t: XL[:, t, :], lambda t: NRM[:, t, :]))
                    v_ready(v_affine(NRM, pc("g2"), pc("b2")))
                    V.link(nc.vector.tensor_tensor(XL[:, :, :], XL[:, :, :], rows(pc("br2"), NT), ALU.add))
                    for j in range(4):
                        dve.wait_ge(c_ffn, j + 1)
                        last = nc.vector.tensor_tensor(XL[:, 4 * j:4 * j + 4, :], XL[:, 4 * j:4 * j + 4, :],
                                                       tile4(PS[:, j, :]), ALU.add)
                    V.link(last)
                    V.link(v_norm(lambda t: XL[:, t, :], lambda t: NRM[:, t, :]))
                    V.link(nc.vector.tensor_tensor(flat(X[:, :, :]), flat(X[:, :, :]), flat(NRM[:, :, :]), ALU.add))

        sd = ExitStack()
        with sd:
            HA = sbuf(sd, "HA", [P, 2, 4, 512])
            HB = sbuf(sd, "HB", [P, 2, 4, 512])
            YT = sbuf(sd, "YT", [P, NT, D])
            with nc.Block() as block:
                @block.tensor
                def _(pe):
                    p_transpose(lambda t: NRM[:, t, :])

                @block.scalar
                def _(act):
                    a_sqrt(NT)
                    a_transposed(lambda j: TR[:, j * 512:(j + 1) * 512])

                @block.vector
                def _(dve):
                    dve.wait_ge(loadD, 16)
                    v_ready(v_norm(lambda t: X[:, t, :], lambda t: NRM[:, t, :]))

            d_full, d_act, d_dve = sem("d_full"), sem("d_act"), sem("d_dve")
            order = [(k, s_, c) for k in ("w1", "w2", "h1", "h2") for s_ in range(2) for c in range(4)]
            order += [("w3", s_, 0) for s_ in range(2)]
            U = Uses(d_full, {"A": d_act, "V": d_dve}, ["V" if k in ("w2", "w3") else "A" for k, _, _ in order])
            where = {k: n for n, k in enumerate(order)}
            with nc.Block() as block:
                @block.tensor
                def _(pe):
                    with pe.Fori(0, NG // 2) as g:
                        U.wait_start(pe, g)
                        for n, (kind, s_, c) in enumerate(order):
                            bank = PS[:, n % 8, :]
                            U.wait_empty(pe, g, n)
                            if kind in ("w1", "w2"):
                                last = nc.tensor.matmul(bank, pd(kind)[:, c * P:(c + 1) * P],
                                                        TR[:, bass.ds(g * 1024 + s_ * 512, 512)], start=True, stop=True)
                            elif kind in ("h1", "h2"):
                                src, before = (HB, "w2") if kind == "h1" else (HA, "h1")
                                for k in range(4):
                                    if c == 0:
                                        U.wait_taken(pe, g, where[(before, s_, k)])
                                    at = k * DH + c * P
                                    last = nc.tensor.matmul(bank, pd(kind)[:, at:at + P], src[:, s_, k, :],
                                                            start=(k == 0), stop=(k == 3))
                            else:
                                U.wait_taken(pe, g, where[("h2", s_, 3)])
                                for t in range(4):
                                    for k in range(4):
                                        last = nc.tensor.matmul(bank[:, t * P:(t + 1) * P],
                                                                HB[:, s_, k, t * P:(t + 1) * P],
                                                                pd("w3")[:, k * P:(k + 1) * P],
                                                                start=(k == 0), stop=(k == 3))
                            last.then_inc(d_full, 1)

                @block.scalar
                def _(act):
                    U.open(act, "A")
                    with act.Fori(0, NG // 2) as g:
                        for n, (kind, s_, c) in enumerate(order):
                            if kind in ("w2", "w3"):
                                continue
                            U.wait_full(act, g, n)
                            if kind == "h2" and c == 0:
                                U.wait_full(act, g, where[("h1", s_, 3)])
                            func, scale, dst = {"w1": (ACT.Silu, "s1", HA), "h1": (ACT.Gelu, "t1", HA),
                                                "h2": (ACT.Gelu, "t2", HB)}[kind]
                            if kind == "h1" and c == 0:
                                U.wait_taken(act, g, where[("w2", s_, 3)])
                            nc.scalar.activation(dst[:, s_, c, :], PS[:, n % 8, :], func,
                                                 scale=pd(scale)[:, c:c + 1]).then_inc(d_act, 1)

                @block.vector
                def _(dve):
                    U.open(dve, "V")
                    with dve.Fori(0, NG // 2) as g:
                        for n, (kind, s_, c) in enumerate(order):
                            if kind == "w2":
                                U.wait_taken(dve, g, where[("w1", s_, c)])
                                U.wait_full(dve, g, n)
                                nc.vector.scalar_tensor_tensor(out=HB[:, s_, c, :], in0=PS[:, n % 8, :],
                                                               scalar=pd("s2")[:, c:c + 1], in1=HA[:, s_, c, :],
                                                               op0=ALU.mult, op1=ALU.mult).then_inc(d_dve, 1)
                            elif kind == "w3":
                                U.wait_full(dve, g, n)
                                nc.vector.tensor_tensor(YT[:, bass.ds(g * 8 + s_ * 4, 4), :], tile4(PS[:, n % 8, :]),
                                                        rows(pd("s3"), 4), ALU.mult).then_inc(d_dve, 1)

            done, x_final = sem("stored"), sem("x_final")
            with nc.Block() as block:
                @block.scalar
                def _(act):
                    a_sqrt(NT)

                @block.vector
                def _(dve):
                    V.link(v_norm(lambda t: YT[:, t, :], lambda t: NRM[:, t, :]))
                    for j in range(2):
                        nc.vector.tensor_tensor(flat(X[:, 8 * j:8 * j + 8, :]), flat(X[:, 8 * j:8 * j + 8, :]),
                                                flat(NRM[:, 8 * j:8 * j + 8, :]), ALU.add).then_inc(x_final, 1)

                @block.sync
                def _(sp):
                    for j in range(2):
                        sp.wait_ge(x_final, j + 1)
                        sp.dma_start(out_dram[:, 8 * j:8 * j + 8, :], X[:, 8 * j:8 * j + 8, :]).then_inc(done, 16)
                    sp.wait_ge(done, 32)


def packed(pack, parts):
    out = np.zeros((P, offsets(pack)[1]), np.float32)
    for name, (at, width) in offsets(pack)[0].items():
        part = np.asarray(parts[name])
        assert part.shape[1] == width, (name, part.shape)
        out[:part.shape[0], at:at + width] = part
    return out


def every(v):
    v = np.asarray(v).reshape(1, -1)
    return np.broadcast_to(v, (P, v.shape[1]))


def column_chunks(v, n):
    return np.asarray(v).reshape(n, P).T


def row_chunks(w):
    n = w.shape[0] // P
    return w.reshape(n, P, -1).transpose(1, 0, 2).reshape(P, -1)


def layout(i):
    i = {k: np.asarray(v) for k, v in i.items()}
    a = {k[8:]: v for k, v in i.items() if k.startswith("L0_attn_")}
    f = {k[7:]: v for k, v in i.items() if k.startswith("L0_ffn_")}
    c = {k[8:]: v for k, v in i.items() if k.startswith("L1_attn_")}
    m = {k[7:]: v for k, v in i.items() if k.startswith("L1_ffn_")}
    r = np.arange(P)
    ident = np.eye(P, dtype=np.float32)
    later = (r[:, None] > r[None, :]).astype(np.float32)
    firs = np.zeros((P, 4), np.float32)
    firs[:, 1:] = a["firs"].reshape(P, FIRS)
    firl = np.zeros((P, 64), np.float32)
    firl[:, 1:] = a["firl"].reshape(P, FIRL)
    gw1s = np.zeros((NH, DK, NH, P), np.float32)
    for h in range(NH):
        gw1s[h, :16, h, :] = a["gW1"][D:D + 16]
    packs = {}
    packs["pa"] = packed(PACK_A, {
        "ident": ident, "low": -later, "upp": -later.T, "incl": 1 - later,
        "wqkv": np.concatenate([a["Wq"], a["Wk"], a["Wv"]], 1),
        "cwb": every(np.concatenate([a[k].T.reshape(-1) for k in ("cwq", "cwk", "cwv")])),
        "wid": a["Wid"], "wb": a["Wb"], "firs": firs, "firl": firl, "gw1h": a["gW1"][:D],
        "gw1s": gw1s.reshape(P, NH * P), "gb1": a["gb1"][:, None], "gw2": a["gW2"],
        "gb2": every(np.tile(a["gb2"], NH)), "ltemp": every(a["log_temp"]), "floor": every(a["floor_param"]),
        "crl": every(a["conv_res_logit"]), "alpha": every(a["alpha_id"]),
        "onw": np.tile(a["o_norm_w"], NH)[:, None], "wo": a["Wo"]})
    packs["pb"] = packed(PACK_B, {
        "ident": ident, "wqkv": f["Wqkv"].T, "bqkv": every(f["bqkv"]), "wo": f["Wo"].T, "bo": every(f["bo"]),
        "g1": every(f["g1"]), "be1": every(f["be1"]), "g2": every(f["g2"]), "be2": every(f["be2"]),
        "wg": f["Wg"].T, "w1": f["W1"].transpose(1, 0, 2).reshape(P, E * DF),
        "b1": f["b1"].reshape(E * 4, P).T, "w2": row_chunks(f["W2"].reshape(E * DF, D)), "b2": f["b2"],
        "iota": every(np.arange(E, dtype=np.float32) - E)})

    def by_quad(w):
        out = np.zeros((w.shape[1], H2, 32), np.float32)
        out[:, :, :HD2] = w.T.reshape(-1, H2, HD2)
        return out.reshape(w.shape[1], 4 * P)

    bk = by_quad(c["bk"][:, None]).reshape(H2, 32)
    bk[:, HD2] = 1
    mask4 = np.zeros((4, 32, 4), np.float32)
    for h in range(4):
        mask4[h, :, h] = 1
    packs["pc"] = packed(PACK_C, {
        "wq": by_quad(c["Wq"]), "wk": by_quad(c["Wk"]),
        "bq": by_quad(c["bq"][:, None]).reshape(4, P).T, "bk": bk.reshape(4, P).T,
        "wv": c["Wv"].T, "bv": every(c["bv"]), "wqv": row_chunks(c["Wqv"]), "bqv": column_chunks(c["bqv"], 4),
        "wsq": np.tile(c["Ws"][0, :QK2], 4)[:, None], "mask4": mask4.reshape(P, 4), "wso": every(c["Ws"][0, QK2:]),
        "bs": every(c["bs"]), "wf": c["Wf"].T, "bf": every(c["bf"]), "wr1": c["Wr1"].T,
        "br1": column_chunks(c["br1"], 2), "wr2": row_chunks(c["Wr2"].T), "br2": every(c["br2"]),
        "g1": every(c["g1"]), "b1": every(c["b1"]), "g2": every(c["g2"]), "b2": every(c["b2"])})
    packs["pd"] = packed(PACK_D, {
        "w1": m["w1_w"].T, "w2": m["w2_w"].T, "h1": row_chunks(m["h1_w"].T), "h2": row_chunks(m["h2_w"].T),
        "w3": row_chunks(m["w3_w"].T), "s1": column_chunks(m["w1_s"], 4), "s2": column_chunks(m["w2_s"], 4),
        "t1": column_chunks(m["h1_s"], 4), "t2": column_chunks(m["h2_s"], 4), "s3": every(m["w3_s"])})
    packs["x"] = a["hs"].reshape(NT, P, D).transpose(1, 0, 2)
    return packs


def kernel(**inputs):
    import concourse.bacc as bacc
    from concourse.bass_utils import run_bass_kernel_spmd

    nc = bacc.Bacc("TRN2", target_bir_lowering=False, num_devices=1)
    arrays, args = {}, []
    for name, a in layout(inputs).items():
        arrays[f"in_{name}"] = np.ascontiguousarray(a, dtype=np.float32)
        args.append((name, nc.dram_tensor(f"in_{name}", a.shape, F32, kind="ExternalInput").ap()))
    args = dict(args)
    out = nc.dram_tensor("out_x", (P, NT, D), F32, kind="ExternalOutput").ap()
    build(nc, args["x"], args["pa"], args["pb"], args["pc"], args["pd"], out)
    r = run_bass_kernel_spmd(nc, [arrays], core_ids=[0])
    got = np.asarray(r.results[0]["out_x"])
    return got.transpose(1, 0, 2).reshape(B, L, D)
```

```python
import math
from contextlib import ExitStack

import numpy as np

import concourse.bass as bass
from concourse import mybir

F32 = mybir.dt.float32
F32R = mybir.dt.float32r
ALU = mybir.AluOpType
ACT = mybir.ActivationFunctionType
AX = mybir.AxisListType

P = 128
B, L, D = 8, 256, 128
NT = B * L // P
NG = NT // 4
NH, DK = 4, 32
TAPS, FIRS, FIRL = 4, 3, 63
PAD = FIRL
E, DF = 8, 512
H2, HD2, R2, QK2 = 16, 8, 8, 32
VX = R2 * HD2 + R2 + 1
DH = 512
FLOOR = 0.05
LEVELS = 7


PACK_A = [("ident", 128), ("low", 128), ("upp", 128), ("incl", 128), ("wqkv", 384), ("cwb", 1536),
          ("wid", 128), ("wb", 4), ("firs", 4), ("firl", 64), ("gw1h", 128), ("gw1s", 512), ("gb1", 1),
          ("gw2", 4), ("gb2", 16), ("ltemp", 16), ("floor", 16), ("crl", 4), ("alpha", 4), ("onw", 1),
          ("wo", 128)]
PACK_B = [("ident", 128), ("wqkv", 384), ("bqkv", 384), ("wo", 128), ("bo", 128), ("g1", 128), ("be1", 128),
          ("g2", 128), ("be2", 128), ("wg", 8), ("w1", E * DF), ("b1", E * 4), ("w2", E * DF), ("b2", 128),
          ("iota", 8)]
PACK_C = [("wq", 512), ("wk", 512), ("bq", 4), ("bk", 4), ("signs", 4), ("sel", H2), ("wv", 64), ("bv", 64), ("wqv", 512),
          ("bqv", 4), ("wsq", 1), ("mask4", 4), ("wso", 8), ("bs", 1), ("wf", 128), ("bf", 128), ("wr1", 256),
          ("br1", 2), ("wr2", 256), ("br2", 128), ("g1", 128), ("b1", 128), ("g2", 128), ("b2", 128)]
PACK_D = [("w1", DH), ("w2", DH), ("h1", 4 * DH), ("h2", 4 * DH), ("w3", DH), ("s1", 4), ("s2", 4),
          ("t1", 4), ("t2", 4), ("s3", 128)]


def offsets(pack):
    at, out = 0, {}
    for name, width in pack:
        out[name] = (at, width)
        at += width
    return out, at


class Chain:

    def __init__(self, eng, sem):
        self.eng, self.sem, self.done, self.base, self.inside = eng, sem, 0, None, 0

    def enter(self, turn, per):
        self.base, self.inside, self.per = turn * per, 0, per

    def leave(self, turns):
        assert self.inside == self.per, (self.inside, self.per)
        self.done += turns * self.per
        self.base = None

    def mark(self, ins):
        ins.then_inc(self.sem, 1)
        if self.base is None:
            self.done += 1
            return self.done
        self.inside += 1
        return self.base + (self.done + self.inside)

    def link(self, ins):
        self.eng.wait_ge(self.sem, self.mark(ins))


class Uses:

    def __init__(self, full, sems, engines, first=0, ring=8):
        self.full, self.sems, self.slots, self.first, self.ring = full, sems, len(engines), first, ring
        self.per = {e: 0 for e in sems}
        self.n, self.order, self.at = 0, [], []
        for e in engines:
            if e:
                self.per[e] += 1
                self.n += 1
            self.order.append(self.n)
            self.at.append((e, self.per[e]) if e else None)

    def bank(self, n):
        return self.first + n % self.ring

    def open(self, eng, e):
        eng.sem_inc(self.sems[e], self.per[e])

    def open_full(self, pe):
        pe.sem_inc(self.full, self.n)

    def wait_start(self, pe, g):
        for e, s in self.sems.items():
            pe.wait_ge(s, g * self.per[e] + self.per[e])

    def wait_empty(self, pe, g, n):
        n -= self.ring
        while n >= 0 and not self.at[n]:
            n -= self.ring
        if n >= 0:
            self.wait_taken(pe, g, n)
        elif self.slots % self.ring == 0:
            while not self.at[n]:
                n -= self.ring
            e, k = self.at[n]
            pe.wait_ge(self.sems[e], g * self.per[e] + k)

    def wait_taken(self, pe, g, n):
        e, k = self.at[n]
        pe.wait_ge(self.sems[e], g * self.per[e] + (self.per[e] + k))

    def wait_full(self, eng, g, n, back=0):
        eng.wait_ge(self.full, g * self.n + ((1 - back) * self.n + self.order[n]))


def build(nc, x_in, pa_in, pb_in, pc_in, pd_in, out_dram):
    ctx = ExitStack()
    with ctx:
        names = {}

        def sem(name):
            if name not in names:
                names[name] = ctx.enter_context(nc.semaphore(name))
            return names[name]

        def sbuf(stack, name, shape):
            return stack.enter_context(nc.sbuf_tensor(name, shape, F32))

        def sbufr(stack, name, shape):
            return stack.enter_context(nc.sbuf_tensor(name, shape, F32R))

        X = sbuf(ctx, "X", [P, NT, D])
        NRM = sbuf(ctx, "NRM", [P, NT, D])
        TR = sbuf(ctx, "TR", [P, NT * D])
        STAT = sbuf(ctx, "STAT", [P, NT, 6])
        MV = sbuf(ctx, "MV", [P, NT, 2])
        SQA = sbuf(ctx, "SQA", [P, 256])
        SQR = sbuf(ctx, "SQR", [P, 256])
        RS = sbuf(ctx, "RS", [P, NT])
        oa, na = offsets(PACK_A)
        ob, nb = offsets(PACK_B)
        oc, ncc = offsets(PACK_C)
        od, nd = offsets(PACK_D)
        PB = sbuf(ctx, "PB", [P, nb])
        PS = ctx.enter_context(nc.psum_tensor("PS", [P, 8, 512], F32))

        def pb(name, rows=P):
            at, width = ob[name]
            return PB[0:rows, at:at + width]

        ident = pb("ident")
        loadA, loadB, loadC, loadD = sem("load_a"), sem("load_b"), sem("load_c"), sem("load_d")
        load_x = sem("load_x")
        dve_step, act_step, pool_step = sem("dve_step"), sem("act_step"), sem("pool_step")
        sqrt_asked, sqrt_given = sem("sqrt_asked"), sem("sqrt_given")
        norm_ready = sem("norm_ready")
        tr_bank, tr_copied = sem("tr_bank"), sem("tr_copied")
        V = Chain(nc.vector, dve_step)
        A = Chain(nc.scalar, act_step)
        G = Chain(nc.gpsimd, pool_step)
        count = {"sqrt_v": 0, "sqrt_a": 0, "norm_v": 0, "norm_p": 0, "tr_p": 0, "tr_a": 0, "tr_v": 0}

        def tile4(ap):
            return ap.rearrange("p (t c) -> p t c", t=4)

        def bcast(ap, n):
            return ap.unsqueeze(2).to_broadcast([P, ap.shape[1], n])

        def rows(ap, n):
            return ap.unsqueeze(1).to_broadcast([P, n, ap.shape[1]])

        def v_sqrt(arg_width):
            count["sqrt_v"] += 1
            nc.vector.wait_ge(sqrt_given, count["sqrt_v"])

        def a_sqrt(width):
            count["sqrt_a"] += 1
            nc.scalar.wait_ge(sqrt_asked, count["sqrt_a"])
            nc.scalar.activation(SQR[:, :width], SQA[:, :width], ACT.Sqrt).then_inc(sqrt_given, 1)

        def v_ask(ins):
            ins.then_inc(sqrt_asked, 1)

        def v_norm(src, dst, eps=1e-5, tiles=NT):
            for t in range(tiles):
                last = nc.vector.bn_stats(STAT[:, t, :], src(t))
            V.link(last)
            for t in range(tiles):
                last = nc.vector.bn_aggr(MV[:, t, :], STAT[:, t, :])
            V.link(last)
            v_ask(nc.vector.tensor_scalar(SQA[:, :tiles], MV[:, :tiles, 1], eps, None, ALU.add))
            v_sqrt(tiles)
            V.link(nc.vector.reciprocal(RS[:, :tiles], SQR[:, :tiles]))
            for t in range(tiles):
                last = nc.vector.tensor_scalar(dst(t), src(t), MV[:, t, 0:1], RS[:, t:t + 1],
                                               ALU.subtract, ALU.mult)
            return last

        def v_ready(last):
            last.then_inc(norm_ready, 1)
            count["norm_v"] += 1

        def p_transpose(src, banks=(0, 1, 2, 3), ready=True):
            if ready:
                count["norm_p"] += 1
                nc.tensor.wait_ge(norm_ready, count["norm_p"])
            for j, bank in enumerate(banks):
                for t in range(4):
                    last = nc.tensor.transpose(PS[:, bank, t * P:(t + 1) * P], src(4 * j + t), ident)
                last.then_inc(tr_bank, 1)
            count["tr_p"] += len(banks)

        def a_transposed(dst, banks=(0, 1, 2, 3)):
            for j, bank in enumerate(banks):
                count["tr_a"] += 1
                nc.scalar.wait_ge(tr_bank, count["tr_a"])
                nc.scalar.activation(dst(j), PS[:, bank, :], ACT.Copy).then_inc(tr_copied, 1)

        def p_copied():
            nc.tensor.wait_ge(tr_copied, count["tr_p"])

        sa = ctx.enter_context(ExitStack())
        DEL = sbuf(sa, "DEL", [P, NT, D])
        QTK = sbuf(sa, "QTK", [P, NT, D])
        KTK = sbuf(sa, "KTK", [P, NT, D])
        VTK = sbuf(sa, "VTK", [P, NT, D])
        ITK = sbuf(sa, "ITK", [P, NT, D])
        VPT = sbuf(sa, "VPT", [P, B, PAD + L])
        FS = sbuf(sa, "FS", [P, B, L])
        FL0 = sbuf(sa, "FL0", [P, B, L])
        FL1 = sbuf(sa, "FL1", [P, B, L])
        XT = sbuf(sa, "XT", [P, B, 3 + L])
        PA = sbuf(sa, "PA", [P, na])
        BETA = sbuf(sa, "BETA", [P, NT, NH])

        def pa(name):
            at, width = oa[name]
            return PA[:, at:at + width]

        s1 = ExitStack()
        with s1:
            WT = sbuf(s1, "WT", [P, 3, TAPS, D])
            ST = sbuf(s1, "ST", [P, 4, 512])
            SB = sbuf(s1, "SB", [NH, 512])
            xt_zero, wt_ready, x_turned = sem("xt_zero"), sem("wt_ready"), sem("x_turned")
            a1_proj, a1_staged, a1_turned, a1_out = (sem("a1_proj"), sem("a1_staged"), sem("a1_turned"),
                                                     sem("a1_out"))
            with nc.Block() as block:
                @block.sync
                def _(sp):
                    sp.dma_start(X[:, :, :], x_in).then_inc(load_x, 16)
                    sp.dma_start(PA[:, :], pa_in).then_inc(loadA, 16)
                    sp.dma_start(PB[:, :], pb_in).then_inc(loadB, 16)

                @block.gpsimd
                def _(pool):
                    nc.gpsimd.memset(XT[:, :, 0:3], 0.0).then_inc(xt_zero, 1)
                    nc.gpsimd.memset(VPT[:, :, 0:PAD], 0.0).then_inc(xt_zero, 1)
                    nc.gpsimd.memset(FS[:, :, :], 0.0).then_inc(xt_zero, 1)
                    nc.gpsimd.memset(FL0[:, :, :], 0.0).then_inc(xt_zero, 1)
                    nc.gpsimd.memset(FL1[:, :, :], 0.0).then_inc(xt_zero, 1)

                @block.vector
                def _(dve):
                    dve.wait_ge(load_x, 16)
                    v_ready(v_norm(lambda t: X[:, t, :], lambda t: NRM[:, t, :]))
                    dve.wait_ge(loadA, 16)
                    for p in range(3):
                        last = nc.vector.tensor_tensor(
                            WT[:, p, :, :], rows(pa("wqkv")[:, p * D:(p + 1) * D], TAPS),
                            pa("cwb")[:, p * 512:(p + 1) * 512].rearrange("p (j c) -> p j c", j=TAPS), ALU.mult)
                    last.then_inc(wt_ready, 1)
                    dve.sem_inc(a1_out, 1)
                    with dve.Fori(0, NG) as g:
                        for n, (bank, dst) in enumerate(((5, QTK), (6, KTK), (7, VTK), (5, ITK))):
                            dve.wait_ge(a1_turned, g * 5 + (n + 2))
                            nc.vector.tensor_copy(dst[:, bass.ds(g * 4, 4), :], tile4(PS[:, bank, :]))\
                                .then_inc(a1_out, 1)
                        dve.wait_ge(a1_turned, g * 5 + 6)
                        nc.vector.tensor_copy(BETA[:, bass.ds(g * 4, 4), :],
                                              PS[:, 6, 0:16].rearrange("p (t h) -> p t h", t=4)).then_inc(a1_out, 1)
                        nc.vector.tensor_copy(VPT[:, bass.ds(g * 2, 2), PAD:PAD + L],
                                              ST[:, 2, :].rearrange("p (b l) -> p b l", b=2)).then_inc(a1_out, 1)

                @block.tensor
                def _(pe):
                    pe.wait_ge(loadB, 16)
                    p_transpose(lambda t: NRM[:, t, :])
                    p_copied()
                    pe.wait_ge(wt_ready, 1)
                    pe.wait_ge(xt_zero, 1)
                    pe.sem_inc(a1_turned, 1)
                    with pe.Fori(0, NG) as g:
                        for p in range(3):
                            for j in range(TAPS):
                                last = nc.tensor.matmul(PS[:, p, :].rearrange("p (b l) -> p b l", b=2),
                                                        WT[:, p, j, :], XT[:, bass.ds(g * 2, 2), j:j + L],
                                                        start=(j == 0), stop=(j == TAPS - 1))
                            last.then_inc(a1_proj, 1)
                        now = XT[:, bass.ds(g * 2, 2), 3:3 + L]
                        nc.tensor.matmul(PS[:, 3, :].rearrange("p (b l) -> p b l", b=2), pa("wid"), now,
                                         start=True, stop=True).then_inc(a1_proj, 1)
                        nc.tensor.matmul(PS[0:NH, 4, :].rearrange("p (b l) -> p b l", b=2), pa("wb"), now,
                                         start=True, stop=True).then_inc(a1_proj, 1)
                        pe.wait_ge(a1_out, g * 6 + 1)
                        for n, bank in enumerate((5, 6, 7, 5)):
                            pe.wait_ge(a1_staged, g * 5 + (n + 1))
                            if n == 3:
                                pe.wait_ge(a1_staged, g * 5 + 5)
                                pe.wait_ge(a1_out, g * 6 + 3)
                            for t in range(4):
                                last = nc.tensor.transpose(PS[:, bank, t * P:(t + 1) * P],
                                                           ST[:, n, t * P:(t + 1) * P], ident)
                            last.then_inc(a1_turned, 1)
                        for t in range(4):
                            last = nc.tensor.transpose(PS[:, 6, t * NH:(t + 1) * NH],
                                                       SB[:, t * P:(t + 1) * P], ident[0:NH, 0:NH])
                        last.then_inc(a1_turned, 1)

                @block.scalar
                def _(act):
                    a_sqrt(NT)
                    a_transposed(lambda j: XT[:, 2 * j:2 * j + 2, 3:3 + L])
                    with act.Fori(0, NG) as g:
                        act.wait_ge(a1_turned, g * 5 + 1)
                        act.wait_ge(a1_out, g * 6 + 1)
                        for n in range(5):
                            act.wait_ge(a1_proj, g * 5 + (n + 1))
                            dst, src, func = ((ST[:, n, :], PS[:, n, :], ACT.Silu if n < 3 else ACT.Copy) if n < 4
                                              else (SB[:, :], PS[0:NH, 4, :], ACT.Sigmoid))
                            nc.scalar.activation(dst, src, func).then_inc(a1_staged, 1)

        s2 = ExitStack()
        with s2:
            RQ = sbuf(s2, "RQ", [P, NT * NH])
            RK = sbuf(s2, "RK", [P, NT * NH])
            RKB = sbuf(s2, "RKB", [P, NT * NH])
            QH = NRM[:, 0:4, :]
            KH = NRM[:, 4:8, :]
            Y = sbuf(s2, "Y", [P, 4, 2, D])
            TQ = sbuf(s2, "TQ", [P, 3, 4, P])
            PW = [sbuf(s2, f"PW{n}", [P, 16, 2, P]) for n in range(2)]
            AT = TR[:, :].rearrange("p (u c) -> p u c", u=16)
            SS = sbuf(s2, "SS", [P, 2, D])
            W1T = sbuf(s2, "W1T", [P, 2, P])
            a2_prep, a2_bank, a2_act, a2_dve = sem("a2_prep"), sem("a2_bank"), sem("a2_act"), sem("a2_dve")

            uses = [("turn", "A")] * 3 + [("mask", "V")] * 12
            for lv in range(LEVELS):
                uses += [("apply", "V")] * 2
                uses += [("square", "A")] * (8 if lv < LEVELS - 2 else 4 if lv == LEVELS - 2 else 0)
            uses += [("state", "V"), ("w1", "A"), ("ws", "V"), ("o", "V")]
            NU = len(uses)
            U = Uses(a2_bank, {"A": a2_act, "V": a2_dve}, [e for _, e in uses])

            pairs = [2 * h + b for b in range(2) for h in range(NH)]

            def bank_of(n):
                return n % 8

            ss_zero = sem("ss_zero")
            with nc.Block() as block:
                @block.gpsimd
                def _(pool):
                    nc.gpsimd.memset(SS[:, :, :], 0.0).then_inc(ss_zero, 1)

                @block.tensor
                def _(pe):
                    U.open_full(pe)
                    with pe.Fori(0, NG) as g:
                        n = 0
                        U.wait_start(pe, g)
                        for k, src in enumerate((QH, KH, None)):
                            pe.wait_ge(a2_prep, g * 4 + (k + 1))
                            for t in range(4):
                                last = nc.tensor.transpose(PS[:, bank_of(n), t * P:(t + 1) * P],
                                                           Y[:, t, 1, :] if src is None else src[:, t, :], ident)
                            last.then_inc(a2_bank, 1)
                            n += 1
                        for l, r in ((2, 1), (1, 2), (1, 0)):
                            U.wait_taken(pe, g, max(l, r))
                            for h in range(NH):
                                U.wait_empty(pe, g, n + h)
                            for t in range(4):
                                for h in range(NH):
                                    hs = slice(DK * h, DK * h + DK)
                                    last = nc.tensor.matmul(PS[:, bank_of(n + h), t * P:(t + 1) * P],
                                                            TQ[hs, l, t, :], TQ[hs, r, t, :], start=True, stop=True)
                                    if t == 3:
                                        last.then_inc(a2_bank, 1)
                            n += NH
                        ready = [10] * 16
                        y_use = None
                        pe.wait_ge(a2_prep, g * 4 + 4)
                        for lv in range(LEVELS):
                            old = PW[lv % 2]
                            new_y = []
                            for half in range(2):
                                U.wait_empty(pe, g, n)
                                U.wait_taken(pe, g, ready[4 * (NH - 1) + 2 * half])
                                if y_use is not None:
                                    U.wait_taken(pe, g, y_use[half])
                                for t in (2 * half, 2 * half + 1):
                                    for h in range(NH):
                                        o = PS[:, bank_of(n), :].rearrange("p (t k c) -> p t k c", t=2, k=2)
                                        last = nc.tensor.matmul(o[:, t % 2, :, h * DK:(h + 1) * DK],
                                                                old[:, 4 * h + t, 1, :],
                                                                Y[:, t, :, h * DK:(h + 1) * DK],
                                                                start=True, stop=True)
                                last.then_inc(a2_bank, 1)
                                new_y.append(n)
                                n += 1
                            y_use = new_y
                            if lv < LEVELS - 2:
                                for pair in pairs:
                                    U.wait_empty(pe, g, n)
                                    U.wait_taken(pe, g, ready[2 * pair + 1])
                                    for u in (2 * pair, 2 * pair + 1):
                                        at = (u % 2) * 256
                                        nc.tensor.matmul(PS[:, bank_of(n), at:at + P], old[:, u, 1, :],
                                                         old[:, u, 0, :], start=True, stop=True)
                                        last = nc.tensor.matmul(PS[:, bank_of(n), at + P:at + 2 * P],
                                                                old[:, u, 0, :], old[:, u, 1, :],
                                                                start=True, stop=True)
                                    last.then_inc(a2_bank, 1)
                                    ready[2 * pair] = ready[2 * pair + 1] = n
                                    n += 1
                            elif lv == LEVELS - 2:
                                for quad in range(4):
                                    U.wait_empty(pe, g, n)
                                    U.wait_taken(pe, g, ready[4 * quad + 3])
                                    for u in range(4 * quad, 4 * quad + 4):
                                        last = nc.tensor.matmul(PS[:, bank_of(n), (u % 4) * P:(u % 4 + 1) * P],
                                                                old[:, u, 0, :], old[:, u, 1, :],
                                                                start=True, stop=True)
                                    last.then_inc(a2_bank, 1)
                                    for u in range(4 * quad, 4 * quad + 4):
                                        ready[u] = n
                                    n += 1
                        U.wait_empty(pe, g, n)
                        U.wait_taken(pe, g, y_use[0])
                        U.wait_taken(pe, g, y_use[1])
                        n_state = n
                        for b in range(2):
                            for h in range(NH):
                                hs = slice(DK * h, DK * h + DK)
                                last = nc.tensor.matmul(PS[hs, bank_of(n), b * DK:(b + 1) * DK], KH[:, 2 * b, hs],
                                                        Y[:, 2 * b, 0, hs], start=True, stop=True)
                        last.then_inc(a2_bank, 1)
                        n += 1
                        U.wait_empty(pe, g, n)
                        n_w1 = n
                        for b in range(2):
                            last = nc.tensor.transpose(PS[:, bank_of(n), b * P:(b + 1) * P], Y[:, 2 * b + 1, 1, :],
                                                       ident)
                        last.then_inc(a2_bank, 1)
                        n += 1
                        U.wait_empty(pe, g, n)
                        U.wait_taken(pe, g, n_state)
                        U.wait_taken(pe, g, n_w1)
                        for b in range(2):
                            last = nc.tensor.matmul(PS[:, bank_of(n), b * P:(b + 1) * P], W1T[:, b, :], SS[:, b, :],
                                                    start=True, stop=True)
                        last.then_inc(a2_bank, 1)
                        n_ws = n
                        n += 1
                        U.wait_empty(pe, g, n)
                        U.wait_taken(pe, g, 14)
                        for t in (0, 2, 1, 3):
                            if t == 1:
                                U.wait_taken(pe, g, n_ws)
                            if t % 2:
                                nc.tensor.matmul(PS[:, bank_of(n), t * P:(t + 1) * P], TQ[:, 0, t, :],
                                                 SS[:, t // 2, :], start=True, stop=False)
                            for h in range(NH):
                                hs = slice(DK * h, DK * h + DK)
                                o = PS[:, bank_of(n), t * P + h * DK:t * P + (h + 1) * DK]
                                last = nc.tensor.matmul(o, AT[:, 4 * h + t, :], Y[:, t, 0, hs],
                                                        start=(t % 2 == 0), stop=(t % 2 == 0 or h == NH - 1))
                        last.then_inc(a2_bank, 1)
                        n += 1
                        assert n == NU

                @block.scalar
                def _(act):
                    a_sqrt(NT * NH)
                    a_sqrt(NT * NH)
                    U.open(act, "A")
                    with act.Fori(0, NG) as g:
                        pair = quad = 0
                        turned = 0
                        lv = -1
                        for n, (what, e) in enumerate(uses):
                            if what == "apply" and uses[n - 1][0] != "apply":
                                lv += 1
                                pair = quad = 0
                            if e != "A":
                                continue
                            U.wait_full(act, g, n)
                            src = PS[:, bank_of(n), :]
                            if what == "turn":
                                dst = TQ[:, turned, :, :]
                                src = tile4(src)
                                turned += 1
                            elif what == "square" and lv < LEVELS - 2:
                                dst = PW[(lv + 1) % 2][:, 2 * pairs[pair]:2 * pairs[pair] + 2, :, :]
                                src = src.rearrange("p (u k c) -> p u k c", u=2, k=2)
                                pair += 1
                            elif what == "square":
                                dst = PW[(lv + 1) % 2][:, 4 * quad:4 * quad + 4, 1, :]
                                src = tile4(src)
                                quad += 1
                            else:
                                dst = W1T[:, :, :]
                                src = PS[:, bank_of(n), 0:256].rearrange("p (b c) -> p b c", b=2)
                            nc.scalar.activation(dst, src, ACT.Copy).then_inc(a2_act, 1)

                @block.vector
                def _(dve):
                    heads = lambda ap: ap.rearrange("p t (h d) -> p (t h) d", h=NH)
                    for src, dst in ((QTK, RQ), (KTK, RK)):
                        V.link(nc.vector.tensor_tensor(NRM[:, :, :], src[:, :, :], src[:, :, :], ALU.mult))
                        V.link(nc.vector.tensor_reduce(RKB[:, :], heads(NRM[:, :, :]), AX.X, ALU.add))
                        v_ask(nc.vector.tensor_scalar(SQA[:, :NT * NH], RKB[:, :], 1e-6, None, ALU.add))
                        v_sqrt(NT * NH)
                        V.link(nc.vector.reciprocal(dst[:, :], SQR[:, :NT * NH]))
                    V.link(nc.vector.tensor_tensor(RKB[:, :], RK[:, :], BETA[:, :, :].rearrange("p t h -> p (t h)"),
                                                   ALU.mult))
                    dve.wait_ge(ss_zero, 1)
                    per_chain = 17
                    U.open(dve, "V")
                    with dve.Fori(0, NG) as g:
                        V.enter(g, per_chain)
                        tiles = bass.ds(g * 4, 4)
                        gh = bass.ds(g * 16, 16)
                        four = lambda ap: ap.rearrange("p (t h) d -> p t h d", t=4)
                        sc = lambda r: r[:, gh].unsqueeze(2).to_broadcast([P, 16, DK])
                        h4 = lambda ap: ap.rearrange("p t (h d) -> p (t h) d", h=NH)
                        hy = lambda k: Y[:, :, k, :].rearrange("p t (h d) -> p t h d", h=NH)
                        sc4 = lambda r: r.rearrange("p (t h) -> p t h", t=4).unsqueeze(3).to_broadcast([P, 4, NH, DK])
                        nc.vector.tensor_tensor(h4(QH[:, :, :]), h4(QTK[:, tiles, :]), sc(RQ), ALU.mult)\
                            .then_inc(a2_prep, 1)
                        nc.vector.tensor_tensor(h4(KH[:, :, :]), h4(KTK[:, tiles, :]), sc(RK), ALU.mult)\
                            .then_inc(a2_prep, 1)
                        nc.vector.tensor_tensor(hy(1), KTK[:, tiles, :].rearrange("p t (h d) -> p t h d", h=NH),
                                                sc4(RKB[:, gh]), ALU.mult).then_inc(a2_prep, 1)
                        nc.vector.tensor_tensor(hy(0), VTK[:, tiles, :].rearrange("p t (h d) -> p t h d", h=NH),
                                                BETA[:, tiles, :].unsqueeze(3).to_broadcast([P, 4, NH, DK]),
                                                ALU.mult).then_inc(a2_prep, 1)
                        taps_done = []

                        def tap(acc, filt, base, k):
                            ins = nc.vector.scalar_tensor_tensor(
                                out=acc[:, :, :], in0=VPT[:, :, bass.ds(k + base, L)],
                                scalar=pa(filt)[:, bass.ds(k, 1)], in1=acc[:, :, :], op0=ALU.mult, op1=ALU.add)
                            taps_done.append(V.mark(ins))

                        def long_tap():
                            k = len(taps_done) - 1
                            if k >= 2:
                                dve.wait_ge(dve_step, taps_done[-2])
                            tap((FL0, FL1)[k % 2], "firl", 0, g * 16 + k)

                        dve.wait_ge(dve_step, g * per_chain + V.done)
                        tap(FS, "firs", PAD - FIRS, g)
                        long_tap()
                        long_tap()
                        masks, lv = 0, 0
                        for n, (what, e) in enumerate(uses):
                            if e != "V":
                                continue
                            U.wait_full(dve, g, n)
                            src = PS[:, bank_of(n), :]
                            if what == "mask":
                                kind, h = divmod(masks, NH)
                                dst = (PW[0][:, 4 * h:4 * h + 4, 0, :], PW[0][:, 4 * h:4 * h + 4, 1, :],
                                       AT[:, 4 * h:4 * h + 4, :])[kind]
                                nc.vector.tensor_tensor(dst, tile4(src), rows(pa(("low", "upp", "incl")[kind]), 4),
                                                        ALU.mult).then_inc(a2_dve, 1)
                                masks += 1
                            elif what == "apply":
                                half = lv % 2
                                yy = Y[:, 2 * half:2 * half + 2, :, :].rearrange("p t k c -> p (t k c)")
                                nc.vector.tensor_tensor(yy, yy, src, ALU.add).then_inc(a2_dve, 1)
                                lv += 1
                                if half:
                                    long_tap()
                                    long_tap()
                            elif what == "state":
                                for h in range(NH):
                                    hs = slice(DK * h, DK * h + DK)
                                    last = nc.vector.tensor_copy(SS[hs, :, hs], PS[hs, bank_of(n), 0:2 * DK].rearrange(
                                        "p (b c) -> p b c", b=2))
                                last.then_inc(a2_dve, 1)
                            elif what == "ws":
                                yy = Y[:, 1:4:2, 0, :]
                                nc.vector.tensor_tensor(yy, yy, PS[:, bank_of(n), 0:256].rearrange(
                                    "p (b c) -> p b c", b=2), ALU.subtract).then_inc(a2_dve, 1)
                            else:
                                nc.vector.tensor_copy(DEL[:, tiles, :], tile4(src)).then_inc(a2_dve, 1)
                        assert len(taps_done) == 17
                        V.leave(NG)

        s3 = ExitStack()
        with s3:
            STK = QTK
            LTK = KTK
            SF = sbuf(s3, "SF", [P, NT, NH, DK])
            GH = sbuf(s3, "GH", [P, NH, 512])
            LG = sbuf(s3, "LG", [P, NT, 16])
            TMP = sbuf(s3, "TMP", [P, NT, D])
            SM = sbuf(s3, "SM", [P, 6, 64])
            GC = sbuf(s3, "GC", [P, 4, 16])
            WO = sbuf(s3, "WO", [P, D])
            long_ready, sf_zero, gate_const = sem("long_ready"), sem("sf_zero"), sem("gate_const")
            a3_hid, a3_gelu, a3_log, a3_lg = sem("a3_hid"), sem("a3_gelu"), sem("a3_log"), sem("a3_lg")
            a3_need, a3_exp, wo_ready, a3_out, src_ready = (sem("a3_need"), sem("a3_exp"), sem("wo_ready"),
                                                            sem("a3_out"), sem("src_ready"))
            with nc.Block() as block:
                @block.gpsimd
                def _(pool):
                    nc.gpsimd.memset(SF[:, :, :, 16:32], 0.0).then_inc(sf_zero, 1)

                @block.tensor
                def _(pe):
                    p_transpose(lambda t: FS[:, t // 2, (t % 2) * P:(t % 2 + 1) * P], ready=False)
                    pe.wait_ge(long_ready, 1)
                    p_transpose(lambda t: FL0[:, t // 2, (t % 2) * P:(t % 2 + 1) * P], (4, 5, 6, 7), ready=False)
                    p_copied()
                    pe.wait_ge(sf_zero, 1)
                    p_transpose(lambda t: SF[:, t, :, :].rearrange("p h s -> p (h s)"))
                    p_copied()
                    pe.sem_inc(a3_log, 1)
                    with pe.Fori(0, NG) as g:
                        for h in range(NH):
                            nc.tensor.matmul(PS[:, h, :].rearrange("p (b l) -> p b l", b=2), pa("gw1h"),
                                             XT[:, bass.ds(g * 2, 2), 3:3 + L], start=True, stop=False)
                            nc.tensor.matmul(PS[:, h, :], pa("gw1s")[:, h * P:(h + 1) * P],
                                             TR[:, bass.ds(g * 512, 512)], start=False, stop=True)\
                                .then_inc(a3_hid, 1)
                        pe.wait_ge(a3_lg, g + 1)
                        for h in range(NH):
                            pe.wait_ge(a3_gelu, g * NH + (h + 1))
                            for t in range(4):
                                at = t * 16 + h * 4
                                last = nc.tensor.matmul(PS[:, 4, at:at + 4], GH[:, h, t * P:(t + 1) * P],
                                                        pa("gw2"), start=True, stop=True)
                        last.then_inc(a3_log, 1)
                    p_transpose(lambda t: TMP[:, t, :])
                    p_copied()
                    pe.wait_ge(wo_ready, 1)
                    for t in range(NT):
                        last = nc.tensor.matmul(PS[:, 4 + t // 4, (t % 4) * P:(t % 4 + 1) * P],
                                                TR[:, t * P:(t + 1) * P], WO[:, :], start=True, stop=True)
                        if t % 4 == 3:
                            last.then_inc(a3_out, 1)

                @block.scalar
                def _(act):
                    a_transposed(lambda j: STK[:, 4 * j:4 * j + 4, :].rearrange("p t c -> p (t c)"))
                    a_transposed(lambda j: LTK[:, 4 * j:4 * j + 4, :].rearrange("p t c -> p (t c)"), (4, 5, 6, 7))
                    a_sqrt(256)
                    a_transposed(lambda j: TR[:, j * 512:(j + 1) * 512])
                    with act.Fori(0, NG) as g:
                        act.wait_ge(a3_log, g + 1)
                        for h in range(NH):
                            act.wait_ge(a3_hid, g * NH + (h + 1))
                            nc.scalar.activation(GH[:, h, :], PS[:, h, :], ACT.Gelu, bias=pa("gb1"))\
                                .then_inc(a3_gelu, 1)
                    nc.scalar.activation(GC[:, 3, 0:4], pa("crl"), ACT.Sigmoid).then_inc(gate_const, 1)
                    nc.scalar.activation(GC[:, 1, :], pa("floor"), ACT.Sigmoid).then_inc(gate_const, 1)
                    nc.scalar.activation(GC[:, 0, :], pa("ltemp"), ACT.Exp, scale=-1.0).then_inc(gate_const, 1)
                    act.wait_ge(a3_need, 1)
                    nc.scalar.activation(LG[:, :, :], LG[:, :, :], ACT.Exp).then_inc(a3_exp, 1)
                    a_sqrt(NT * NH)
                    a_transposed(lambda j: TR[:, j * 512:(j + 1) * 512])
                    a_sqrt(NT)

                @block.vector
                def _(dve):
                    flat = lambda ap: ap.rearrange("p t c -> p (t c)")
                    per_head = lambda ap: ap.rearrange("p t (h d) -> p (t h) d", h=NH)
                    nc.vector.tensor_tensor(FL0[:, :, :], FL0[:, :, :], FL1[:, :, :], ALU.add).then_inc(long_ready, 1)
                    nc.vector.tensor_scalar(WO[:, :], pa("wo"), pa("onw"), None, ALU.mult).then_inc(wo_ready, 1)
                    for s, src in ((3, VTK), (2, DEL), (0, STK), (1, LTK)):
                        if s == 0:
                            dve.wait_ge(tr_copied, 8)
                        if s == 1:
                            dve.wait_ge(tr_copied, 12)
                        stat = lambda k: SF[:, :, :, 4 * s + k].rearrange("p t h -> p (t h)")
                        nc.vector.tensor_reduce(SM[:, 0, :], per_head(src[:, :, :]), AX.X, ALU.add)
                        nc.vector.tensor_reduce(SM[:, 1, :], per_head(src[:, :, :]), AX.X, ALU.add,
                                                apply_absolute_value=True)
                        V.link(nc.vector.tensor_tensor(flat(TMP[:, :, :]), flat(src[:, :, :]), flat(src[:, :, :]),
                                                       ALU.mult))
                        V.link(nc.vector.tensor_reduce(SQA[:, s * 64:(s + 1) * 64], per_head(TMP[:, :, :]), AX.X,
                                                       ALU.add))
                        V.link(nc.vector.tensor_scalar(stat(0), SM[:, 0, :], 1.0 / DK, None, ALU.mult))
                        nc.vector.tensor_scalar(stat(2), SM[:, 1, :], 1.0 / DK, None, ALU.mult)
                        V.link(nc.vector.tensor_tensor(SM[:, 2, :], stat(0), stat(0), ALU.mult))
                        V.link(nc.vector.scalar_tensor_tensor(out=stat(1), in0=SQA[:, s * 64:(s + 1) * 64],
                                                              scalar=1.0 / DK, in1=SM[:, 2, :], op0=ALU.mult,
                                                              op1=ALU.subtract))
                    v_ask(nc.vector.tensor_scalar(SM[:, 3, 0:1], SM[:, 2, 0:1], 0.0, None, ALU.mult))
                    v_sqrt(256)
                    last = None
                    for s in range(4):
                        last = nc.vector.tensor_copy(SF[:, :, :, 4 * s + 3].rearrange("p t h -> p (t h)"),
                                                     SQR[:, s * 64:(s + 1) * 64])
                    v_ready(last)
                    dve.sem_inc(a3_lg, 1)
                    with dve.Fori(0, NG) as g:
                        dve.wait_ge(a3_log, g + 2)
                        nc.vector.tensor_copy(LG[:, bass.ds(g * 4, 4), :],
                                              PS[:, 4, 0:64].rearrange("p (t c) -> p t c", t=4)).then_inc(a3_lg, 1)
                    dve.wait_ge(a3_lg, NG + 1)
                    dve.wait_ge(gate_const, 3)
                    quad = lambda ap: ap.rearrange("p t (h s) -> p (t h) s", h=NH)
                    V.link(nc.vector.tensor_tensor(LG[:, :, :], LG[:, :, :], rows(pa("gb2"), NT), ALU.add))
                    V.link(nc.vector.tensor_tensor(LG[:, :, :], LG[:, :, :], rows(GC[:, 0, :], NT), ALU.mult))
                    V.link(nc.vector.tensor_reduce(SM[:, 0, :], quad(LG[:, :, :]), AX.X, ALU.max))
                    nc.vector.tensor_tensor(quad(LG[:, :, :]), quad(LG[:, :, :]), bcast(SM[:, 0, :], 4),
                                            ALU.subtract).then_inc(a3_need, 1)
                    V.link(nc.vector.tensor_scalar(GC[:, 1, :], GC[:, 1, :], FLOOR, None, ALU.mult))
                    V.link(nc.vector.tensor_reduce(GC[:, 2, 0:4], GC[:, 1, :].rearrange("p (h s) -> p h s", h=NH), AX.X,
                                                   ALU.add))
                    V.link(nc.vector.tensor_scalar(GC[:, 2, 0:4], GC[:, 2, 0:4], -1.0, 1.0, ALU.mult, ALU.add))
                    dve.wait_ge(a3_exp, 1)
                    V.link(nc.vector.tensor_reduce(SM[:, 0, :], quad(LG[:, :, :]), AX.X, ALU.add))
                    V.link(nc.vector.reciprocal(SM[:, 1, :], SM[:, 0, :]))
                    by_head = lambda k: SM[:, k, :].rearrange("p (t h) -> p t h", t=NT)
                    V.link(nc.vector.tensor_tensor(by_head(1), by_head(1), rows(GC[:, 2, 0:4], NT), ALU.mult))
                    V.link(nc.vector.tensor_tensor(quad(LG[:, :, :]), quad(LG[:, :, :]), bcast(SM[:, 1, :], 4),
                                                   ALU.mult))
                    V.link(nc.vector.tensor_tensor(LG[:, :, :], LG[:, :, :], rows(GC[:, 1, :], NT), ALU.add))
                    weight = lambda s: LG[:, :, :].rearrange("p t (h s) -> p (t h) s", h=NH)[:, :, s]
                    V.link(nc.vector.tensor_tensor(LG[:, :, 0:16:4], LG[:, :, 0:16:4], rows(GC[:, 3, 0:4], NT),
                                                   ALU.add))
                    for s, src in enumerate((STK, LTK, DEL, VTK)):
                        nc_last = nc.vector.tensor_tensor(per_head(src[:, :, :]), per_head(src[:, :, :]),
                                                          weight(s).unsqueeze(2).to_broadcast([P, NT * NH, DK]),
                                                          ALU.mult)
                    V.link(nc_last)
                    alpha_rows = pa("alpha").unsqueeze(1).unsqueeze(3).to_broadcast([P, NT, NH, DK])
                    V.link(nc.vector.tensor_tensor(ITK[:, :, :].rearrange("p t (h d) -> p t h d", h=NH),
                                                   ITK[:, :, :].rearrange("p t (h d) -> p t h d", h=NH), alpha_rows,
                                                   ALU.mult))
                    nc.vector.tensor_tensor(flat(STK[:, :, :]), flat(STK[:, :, :]), flat(LTK[:, :, :]), ALU.add)
                    V.link(nc.vector.tensor_tensor(flat(DEL[:, :, :]), flat(DEL[:, :, :]), flat(VTK[:, :, :]), ALU.add))
                    V.link(nc.vector.tensor_tensor(flat(STK[:, :, :]), flat(STK[:, :, :]), flat(DEL[:, :, :]), ALU.add))
                    V.link(nc.vector.tensor_tensor(flat(STK[:, :, :]), flat(STK[:, :, :]), flat(ITK[:, :, :]), ALU.add))
                    V.link(nc.vector.tensor_tensor(flat(TMP[:, :, :]), flat(STK[:, :, :]), flat(STK[:, :, :]), ALU.mult))
                    V.link(nc.vector.tensor_reduce(SM[:, 0, :], per_head(TMP[:, :, :]), AX.X, ALU.add))
                    v_ask(nc.vector.tensor_scalar(SQA[:, :64], SM[:, 0, :], 1.0 / DK, 1e-5, ALU.mult, ALU.add))
                    v_sqrt(64)
                    V.link(nc.vector.reciprocal(SM[:, 1, :], SQR[:, :64]))
                    v_ready(nc.vector.tensor_tensor(per_head(TMP[:, :, :]), per_head(STK[:, :, :]),
                                                    bcast(SM[:, 1, :], DK), ALU.mult))
                    dve.wait_ge(a3_out, 4)
                    V.link(v_norm(lambda t: PS[:, 4 + t // 4, (t % 4) * P:(t % 4 + 1) * P], lambda t: NRM[:, t, :]))
                    V.link(nc.vector.tensor_tensor(flat(X[:, :, :]), flat(X[:, :, :]), flat(NRM[:, :, :]), ALU.add))
        sa.close()

        PC = sbuf(ctx, "PC", [P, ncc])
        PD = sbuf(ctx, "PD", [P, nd])
        flat = lambda ap: ap.rearrange("p t c -> p (t c)")

        def pc(name, rows_=P):
            at, width = oc[name]
            return PC[0:rows_, at:at + width]

        def pd(name):
            at, width = od[name]
            return PD[:, at:at + width]

        def v_affine(dst, gain, shift):
            V.link(nc.vector.tensor_tensor(dst[:, :, :], dst[:, :, :], rows(gain, NT), ALU.mult))
            return nc.vector.tensor_tensor(dst[:, :, :], dst[:, :, :], rows(shift, NT), ALU.add)

        sb = ExitStack()
        with sb:
            QKV = sbuf(sb, "QKV", [P, NT, 384])
            PR = sbuf(sb, "PR", [P, 64, DK])
            OB = sbuf(sb, "OB", [P, NT, D])
            SC = sbuf(sb, "SC", [P, 2, NH, B, B])
            SR = sbuf(sb, "SR", [P, 64])
            MS = sbuf(sb, "MS", [P, NT, E])
            LE = sbuf(sb, "LE", [P, NT, E])
            MT = sbuf(sb, "MT", [E, NT * P])
            HID = sbuf(sb, "HID", [P, 2, 4, 512])
            b_qkv, b_qkv_out, b_exp_need, b_exp, b_wo, b_logit, b_bias = (
                sem("b_qkv"), sem("b_qkv_out"), sem("b_exp_need"), sem("b_exp"), sem("b_wo"), sem("b_logit"),
                sem("b_bias"))
            moe_full, moe_act, moe_dve = sem("moe_full"), sem("moe_act"), sem("moe_dve")
            copied0 = count["tr_p"]
            with nc.Block() as block:
                @block.sync
                def _(sp):
                    sp.dma_start(PC[:, :], pc_in).then_inc(loadC, 16)
                    sp.dma_start(PD[:, :], pd_in).then_inc(loadD, 16)

                @block.tensor
                def _(pe):
                    p_transpose(lambda t: NRM[:, t, :])
                    p_copied()
                    for t in range(NT):
                        if t >= 8:
                            pe.wait_ge(b_qkv_out, t - 7)
                        nc.tensor.matmul(PS[:, t % 8, 0:384], TR[:, t * P:(t + 1) * P], pb("wqkv"), start=True,
                                         stop=True).then_inc(b_qkv, 1)
                    pe.wait_ge(b_qkv_out, NT)
                    p_transpose(lambda t: OB[:, t, :])
                    p_copied()
                    for t in range(NT):
                        last = nc.tensor.matmul(PS[:, 4 + t // 4, (t % 4) * P:(t % 4 + 1) * P],
                                                TR[:, t * P:(t + 1) * P], pb("wo"), start=True, stop=True)
                    last.then_inc(b_wo, 1)
                    p_transpose(lambda t: NRM[:, t, :])
                    p_copied()
                    for t in range(NT):
                        last = nc.tensor.matmul(PS[:, 4, t * E:(t + 1) * E], TR[:, t * P:(t + 1) * P], pb("wg"),
                                                start=True, stop=True)
                    last.then_inc(b_logit, 1)
                    count["norm_p"] += 1
                    pe.wait_ge(norm_ready, count["norm_p"])
                    for j in range(4):
                        for t in range(4):
                            last = nc.tensor.transpose(PS[0:E, j, t * P:(t + 1) * P], MS[:, 4 * j + t, :], ident)
                        last.then_inc(tr_bank, 1)
                    count["tr_p"] += 4
                    p_copied()
                    for t in range(NT):
                        last = nc.tensor.matmul(PS[:, 4 + t // 4, (t % 4) * P:(t % 4 + 1) * P],
                                                MT[:, t * P:(t + 1) * P], pb("b2", E), start=True, stop=True)
                    last.then_inc(b_bias, 1)

                @block.scalar
                def _(act):
                    a_sqrt(NT)
                    a_transposed(lambda j: TR[:, j * 512:(j + 1) * 512])
                    act.wait_ge(b_exp_need, 1)
                    nc.scalar.activation(SC[:, :, :, :, :].rearrange("p f h q k -> p (f h q k)"),
                                         SC[:, :, :, :, :].rearrange("p f h q k -> p (f h q k)"), ACT.Exp)\
                        .then_inc(b_exp, 1)
                    a_transposed(lambda j: TR[:, j * 512:(j + 1) * 512])
                    a_sqrt(NT)
                    a_transposed(lambda j: TR[:, j * 512:(j + 1) * 512])
                    for j in range(4):
                        count["tr_a"] += 1
                        act.wait_ge(tr_bank, count["tr_a"])
                        nc.scalar.activation(MT[:, j * 512:(j + 1) * 512], PS[0:E, j, :], ACT.Copy)\
                            .then_inc(tr_copied, 1)

                @block.vector
                def _(dve):
                    v_ready(v_norm(lambda t: X[:, t, :], lambda t: NRM[:, t, :]))
                    for t in range(NT):
                        dve.wait_ge(b_qkv, t + 1)
                        nc.vector.tensor_tensor(QKV[:, t, :], PS[:, t % 8, 0:384], pb("bqkv"), ALU.add)\
                            .then_inc(b_qkv_out, 1)
                    dve.wait_ge(b_qkv_out, NT)
                    part = lambda f, h, k: QKV[:, f:NT:2, k * D + h * DK:k * D + (h + 1) * DK]
                    for f in range(2):
                        for h in range(NH):
                            q = part(f, h, 0).unsqueeze(2).to_broadcast([P, B, B, DK])
                            k = part(f, h, 1).unsqueeze(1).to_broadcast([P, B, B, DK])
                            V.link(nc.vector.tensor_tensor(PR[:, :, :].rearrange("p (a b) d -> p a b d", a=B), q, k,
                                                           ALU.mult))
                            V.link(nc.vector.tensor_reduce(SC[:, f, h, :, :].rearrange("p q k -> p (q k)"),
                                                           PR[:, :, :], AX.X, ALU.add))
                    scores = SC[:, :, :, :, :].rearrange("p f h q k -> p (f h q) k")
                    V.link(nc.vector.tensor_scalar(scores, scores, 1.0 / math.sqrt(DK), None, ALU.mult))
                    V.link(nc.vector.tensor_reduce(SR[:, :], scores, AX.X, ALU.max))
                    nc.vector.tensor_tensor(scores, scores, bcast(SR[:, :], B), ALU.subtract).then_inc(b_exp_need, 1)
                    dve.wait_ge(b_exp, 1)
                    V.link(nc.vector.tensor_reduce(SR[:, :], scores, AX.X, ALU.add))
                    V.link(nc.vector.reciprocal(SR[:, :], SR[:, :]))
                    V.link(nc.vector.tensor_tensor(scores, scores, bcast(SR[:, :], B), ALU.mult))
                    for f in range(2):
                        for h in range(NH):
                            a = SC[:, f, h, :, :].unsqueeze(2).to_broadcast([P, B, DK, B])
                            v = part(f, h, 2).rearrange("p b d -> p d b").unsqueeze(1).to_broadcast([P, B, DK, B])
                            pr = PR[:, :, :].rearrange("p (a x) (y b) -> p a (x y) b", a=B, b=B)
                            V.link(nc.vector.tensor_tensor(pr, a, v, ALU.mult))
                            last = nc.vector.tensor_reduce(OB[:, f:NT:2, h * DK:(h + 1) * DK], pr, AX.X, ALU.add)
                            if f < 1 or h < NH - 1:
                                V.link(last)
                    v_ready(last)
                    dve.wait_ge(b_wo, 1)
                    V.link(nc.vector.tensor_tensor(NRM[:, :, :], NRM[:, :, :], rows(pb("bo"), NT), ALU.add))
                    for j in range(4):
                        last = nc.vector.tensor_tensor(NRM[:, 4 * j:4 * j + 4, :], NRM[:, 4 * j:4 * j + 4, :],
                                                       tile4(PS[:, 4 + j, :]), ALU.add)
                    V.link(last)
                    V.link(v_norm(lambda t: NRM[:, t, :], lambda t: NRM[:, t, :]))
                    v_ready(v_affine(NRM, pb("g1"), pb("be1")))
                    dve.wait_ge(b_logit, 1)
                    V.link(nc.vector.tensor_copy(LE[:, :, :], PS[:, 4, 0:NT * E].rearrange("p (t e) -> p t e", t=NT)))
                    V.link(nc.vector.tensor_reduce(SR[:, 0:NT], LE[:, :, :], AX.X, ALU.max))
                    V.link(nc.vector.tensor_tensor(LE[:, :, :], LE[:, :, :], bcast(SR[:, 0:NT], E), ALU.is_equal))
                    V.link(nc.vector.tensor_tensor(LE[:, :, :], LE[:, :, :], rows(pb("iota"), NT), ALU.mult))
                    V.link(nc.vector.tensor_reduce(SR[:, 0:NT], LE[:, :, :], AX.X, ALU.min))
                    v_ready(nc.vector.tensor_tensor(MS[:, :, :], rows(pb("iota"), NT), bcast(SR[:, 0:NT], E),
                                                    ALU.is_equal))
                    dve.wait_ge(b_bias, 1)
                    for j in range(4):
                        nc.vector.tensor_tensor(OB[:, 4 * j:4 * j + 4, :], NRM[:, 4 * j:4 * j + 4, :],
                                                tile4(PS[:, 4 + j, :]), ALU.add)

            engines, order = [], []
            for e in range(E + 1):
                if e < E:
                    order += [("up", e, c) for c in range(4)]
                if e >= 1:
                    order.append(("down", e - 1, 0))
            engines = ["A" if k == "up" else "V" for k, _, _ in order]
            U = Uses(moe_full, {"A": moe_act, "V": moe_dve}, engines)
            where = {k: n for n, k in enumerate(order)}
            with nc.Block() as block:
                @block.tensor
                def _(pe):
                    U.open_full(pe)
                    with pe.Fori(0, NG) as g:
                        U.wait_start(pe, g)
                        for n, (kind, e, c) in enumerate(order):
                            U.wait_empty(pe, g, n)
                            if kind == "up":
                                at = e * DF + c * P
                                last = nc.tensor.matmul(PS[:, n % 8, :], pb("w1")[:, at:at + P],
                                                        TR[:, bass.ds(g * 512, 512)], start=True, stop=True)
                            else:
                                U.wait_taken(pe, g, where[("up", e, 3)])
                                for t in range(4):
                                    for k in range(4):
                                        last = nc.tensor.matmul(PS[:, n % 8, t * P:(t + 1) * P],
                                                                HID[:, e % 2, k, t * P:(t + 1) * P],
                                                                pb("w2")[:, (4 * e + k) * P:(4 * e + k + 1) * P],
                                                                start=(k == 0), stop=(k == 3))
                            last.then_inc(moe_full, 1)

                @block.scalar
                def _(act):
                    U.open(act, "A")
                    with act.Fori(0, NG) as g:
                        for n, (kind, e, c) in enumerate(order):
                            if kind == "up":
                                if e >= 2:
                                    U.wait_full(act, g, where[("down", e - 2, 0)])
                                U.wait_full(act, g, n)
                                at = 4 * e + c
                                nc.scalar.activation(HID[:, e % 2, c, :], PS[:, n % 8, :], ACT.Relu,
                                                     bias=pb("b1")[:, at:at + 1]).then_inc(moe_act, 1)

                @block.vector
                def _(dve):
                    U.open(dve, "V")
                    with dve.Fori(0, NG) as g:
                        for n, (kind, e, c) in enumerate(order):
                            if kind == "down":
                                U.wait_full(dve, g, n)
                                if e:
                                    U.wait_taken(dve, g, where[("down", e - 1, 0)])
                                for t in range(4):
                                    acc = OB[:, bass.ds(g * 4 + t, 1), :].rearrange("p t c -> p (t c)")
                                    last = nc.vector.scalar_tensor_tensor(
                                        out=acc, in0=PS[:, n % 8, t * P:(t + 1) * P],
                                        scalar=MS[:, bass.ds(g * 4 + t, 1), e], in1=acc, op0=ALU.mult, op1=ALU.add)
                                last.then_inc(moe_dve, 1)

            with nc.Block() as block:
                @block.scalar
                def _(act):
                    a_sqrt(NT)
                    a_sqrt(NT)

                @block.vector
                def _(dve):
                    V.link(v_norm(lambda t: OB[:, t, :], lambda t: NRM[:, t, :]))
                    V.link(v_affine(NRM, pb("g2"), pb("be2")))
                    V.link(v_norm(lambda t: NRM[:, t, :], lambda t: NRM[:, t, :]))
                    V.link(nc.vector.tensor_tensor(flat(X[:, :, :]), flat(X[:, :, :]), flat(NRM[:, :, :]), ALU.add))

        sc_ = ExitStack()
        with sc_:
            XL = sbuf(sc_, "XL", [P, NT, D])
            VXT = sbuf(sc_, "VXT", [P, NT, VX])
            CT = sbuf(sc_, "CT", [P, NT, H2])
            BD = sbuf(sc_, "BD", [P, 4, H2])
            WEF = sbuf(sc_, "WEF", [P, H2])
            CRW = sbuf(sc_, "CRW", [P, H2])
            OC = sbuf(sc_, "OC", [P, NT, D])
            s5 = sc_.enter_context(ExitStack())
            BS = sbuf(s5, "BS", [P, 4, 4])
            QK = [sbufr(s5, f"QK{n}", [P, 2, 4, L]) for n in range(2)]
            HI = sbufr(s5, "HI", [P, 4, 2, L])
            LO = sbuf(s5, "LO", [P, 4, 2, L])
            MX = sbuf(s5, "MX", [P, 2, H2])
            MH = sbufr(s5, "MH", [P, 2, H2])
            M4 = sbuf(s5, "M4", [P, 2, 4, 2, H2])
            MR = [sbufr(s5, f"MR{n}", [P, L]) for n in range(2)]
            SEL = sbufr(s5, "SEL", [P, H2])
            PT = sbuf(s5, "PT", [P, 4, 2, L])
            UB = [sbuf(s5, f"UB{n}", [P, H2, 2, VX]) for n in range(2)]
            CM = sbuf(s5, "CM", [P, 2 * H2, R2])
            RI = sbuf(s5, "RI", [P, 3, 2 * H2])
            UP = sbuf(s5, "UP", [P, 2 * H2, HD2, R2])
            c_zero, c_bd, c_w, c_wef, c_v, c_vout, c_ct = (sem("c_zero"), sem("c_bd"), sem("c_w"), sem("c_wef"),
                                                           sem("c_v"), sem("c_vout"), sem("c_ct"))
            with nc.Block() as block:
                @block.gpsimd
                def _(pool):
                    nc.gpsimd.memset(BD[:, :, :], 0.0).then_inc(c_zero, 1)
                    nc.gpsimd.memset(VXT[:, :, VX - 1:VX], 1.0).then_inc(c_zero, 1)

                @block.tensor
                def _(pe):
                    pe.wait_ge(c_bd, 1)
                    for c in range(4):
                        nc.tensor.matmul(PS[:, 6, 0:H2], pc("wqv")[:, c * P:(c + 1) * P], BD[:, c, :],
                                         start=(c == 0), stop=(c == 3))
                    for c in range(4):
                        last = nc.tensor.matmul(PS[:, 7, 0:H2], pc("bqv")[:, c:c + 1].to_broadcast([P, P]),
                                                BD[:, c, :], start=(c == 0), stop=(c == 3))
                    last.then_inc(c_w, 1)
                    p_transpose(lambda t: NRM[:, t, :])
                    p_copied()
                    for t in range(NT):
                        last = nc.tensor.matmul(PS[:, 4 + t // 8, (t % 8) * 64:(t % 8 + 1) * 64],
                                                TR[:, t * P:(t + 1) * P], pc("wv"), start=True, stop=True)
                    last.then_inc(c_v, 1)
                    pe.wait_ge(c_wef, 1)
                    for t in range(NT):
                        last = nc.tensor.matmul(PS[:, 6, t * H2:(t + 1) * H2], TR[:, t * P:(t + 1) * P], WEF[:, :],
                                                start=True, stop=True)
                    last.then_inc(c_ct, 1)

                @block.scalar
                def _(act):
                    a_sqrt(NT)
                    a_sqrt(NT)
                    a_transposed(lambda j: TR[:, j * 512:(j + 1) * 512])

                @block.vector
                def _(dve):
                    dve.wait_ge(loadC, 16)
                    dve.wait_ge(c_zero, 1)
                    for c in range(4):
                        last = nc.vector.tensor_scalar(BD[:, c, 4 * c:4 * c + 4], pc("mask4"), pc("wsq"), None,
                                                       ALU.mult)
                    last.then_inc(c_bd, 1)
                    V.link(nc.vector.tensor_scalar(BS[:, 0, :], pc("bq"), 1.0 / math.sqrt(HD2), None, ALU.mult))
                    nc.vector.tensor_scalar(BS[:, 1, :], BS[:, 0, :], pc("signs")[:, 0:1], None, ALU.mult)
                    nc.vector.tensor_scalar(BS[:, 2, :], pc("bk"), pc("signs")[:, 2:3], None, ALU.mult)
                    nc.vector.tensor_scalar(BS[:, 3, 0:1], pc("signs")[:, 0:1], 1.0 / math.sqrt(HD2), None, ALU.mult)
                    nc.vector.tensor_copy(SEL[:, :], pc("sel"))
                    V.link(v_norm(lambda t: X[:, t, :], lambda t: XL[:, t, :]))
                    V.link(v_norm(lambda t: XL[:, t, :], lambda t: NRM[:, t, :]))
                    v_ready(v_affine(NRM, pc("g1"), pc("b1")))
                    dve.wait_ge(c_w, 1)
                    nc.vector.tensor_scalar(CRW[:, :], PS[:, 7, 0:H2], 1.0 / math.sqrt(QK2), pc("bs"), ALU.mult,
                                            ALU.add)
                    nc.vector.tensor_scalar(WEF[:, :], PS[:, 6, 0:H2], 1.0 / math.sqrt(QK2), None, ALU.mult)\
                        .then_inc(c_wef, 1)
                    dve.wait_ge(c_v, 1)
                    for j in range(2):
                        last = nc.vector.tensor_tensor(VXT[:, 8 * j:8 * j + 8, 0:64],
                                                       PS[:, 4 + j, :].rearrange("p (t c) -> p t c", t=8),
                                                       rows(pc("bv"), 8), ALU.add)
                    V.link(last)
                    prod = UP[:, :, :, :].rearrange("p a b c -> p (a b c)")[:, 0:NT * 64]
                    V.link(nc.vector.tensor_tensor(prod.rearrange("p (t r d) -> p t r d", t=NT, r=R2),
                                                   VXT[:, :, 0:64].rearrange("p t (r d) -> p t r d", r=R2),
                                                   pc("wso").unsqueeze(1).unsqueeze(1).to_broadcast([P, NT, R2, HD2]),
                                                   ALU.mult))
                    nc.vector.tensor_reduce(VXT[:, :, 64:72], prod.rearrange("p (t r d) -> p t r d", t=NT, r=R2), AX.X,
                                            ALU.add)
                    dve.wait_ge(c_ct, 1)
                    V.link(nc.vector.tensor_tensor(CT[:, :, :], PS[:, 6, 0:NT * H2].rearrange("p (t h) -> p t h", t=NT),
                                                   rows(CRW[:, :], NT), ALU.add))

            prep = [("q", 0), ("k", 0), ("q", 1), ("k", 1)] + [("max", h) for h in range(H2)] + [("turn", 0)]
            LAG = 2
            main = []
            for h in range(H2 + LAG):
                if h < H2:
                    main.append(("exp", h))
                if h >= LAG and h % 2:
                    main.append(("out", (h - LAG) // 2))
            merged, todo = [], [("p",) + u for u in prep]
            for k, u in enumerate(main):
                merged.append(("m",) + u)
                if k == 1:
                    merged.append(("f", "start", 0))
                if k == 7:
                    merged.append(("f", "end", 0))
                for _ in range(2 if k < 8 else 1):
                    if todo:
                        merged.append(todo.pop(0))
            assert not todo
            c_full, c_act = sem("c_full"), sem("c_act")
            p_full, p_act, p_dve = sem("p_full"), sem("p_act"), sem("p_dve")
            c_split, c_e_need, c_e, c_done = sem("c_split"), sem("c_e_need"), sem("c_e"), sem("c_done")
            UP_ = Uses(p_full, {"A": p_act, "V": p_dve}, ["A" if k in "qk" else "V" for k, _ in prep] + [None] * (-len(prep) % 4), 0, 4)
            UM = Uses(c_full, {"A": c_act}, ["A" for _ in main], 4, 4)
            c_own, c_mh, c_m4 = sem("c_own"), sem("c_mh"), sem("c_m4")
            at_p = {k: n for n, k in enumerate(prep)}
            at_m = {k: n for n, k in enumerate(main)}

            def batches(eng, step):
                for u in prep:
                    step(("p",) + u, 0, 0)

                def turn(b, odd, first=False, last=False):
                    for kind, *u in merged:
                        if kind == "m":
                            step(("m", *u), b, odd)
                        elif kind == "f" and not first:
                            step(("f", *u), b - 1, 1 - odd)
                        elif kind == "p" and not last:
                            step(("p", *u), b + 1, 1 - odd)

                turn(0, 0, first=True)
                with eng.Fori(0, (B - 2) // 2) as i:
                    turn(i * 2 + 1, 1)
                    turn(i * 2 + 2, 0)
                turn(B - 1, 1, last=True)
                step(("f", "start", 0), B - 1, 1)
                step(("f", "end", 0), B - 1, 1)

            def wait_split(eng, b, s_, back=0):
                eng.wait_ge(c_split, b * 4 + (4 * (1 - back) + s_ + 1))

            with nc.Block() as block:
                @block.tensor
                def _(pe):
                    def step(what, b, odd):
                        group, kind, k = what
                        q, kk = QK[odd][:, 0, :, :], QK[odd][:, 1, :, :]
                        if group == "f":
                            return
                        U, at = (UP_, at_p) if group == "p" else (UM, at_m)
                        n = at[(kind, k)]
                        bank = PS[:, U.bank(n), :]
                        U.wait_empty(pe, b, n)
                        if kind in "qk":
                            w = pc("wq" if kind == "q" else "wk")
                            for t in (2 * k, 2 * k + 1):
                                last = nc.tensor.matmul(bank[:, (t % 2) * L:(t % 2 + 1) * L], w[:, t * P:(t + 1) * P],
                                                        TR[:, bass.ds(b * L, L)], start=True, stop=True)
                        elif kind == "max":
                            hs = slice(32 * (k % 4), 32 * (k % 4) + 32)
                            wait_split(pe, b, 2 * (k // 8) + 1)
                            for f in range(2):
                                last = nc.tensor.matmul(bank[:, f * L:(f + 1) * L], q[hs, k // 4, f * P:(f + 1) * P],
                                                        kk[hs, k // 4, :], start=True, stop=True)
                        elif kind == "turn":
                            pe.wait_ge(c_m4, b + 1)
                            for f in range(2):
                                last = nc.tensor.transpose(bank[:, f * P:(f + 1) * P],
                                                           M4[:, f, :, :, :].rearrange("p r a h -> p (r a h)"), ident)
                        elif kind == "exp":
                            hs = slice(32 * (k % 4), 32 * (k % 4) + 32)
                            UP_.wait_taken(pe, b, at_p[("turn", 0)])
                            for c in range(2):
                                o = bank[:, c * L:(c + 1) * L]
                                nc.tensor.matmul(o, kk[hs, k // 4, c * P:(c + 1) * P], q[hs, k // 4, :], start=True,
                                                 stop=False)
                                last = nc.tensor.matmul(o, SEL[hs, k:k + 1].to_broadcast([32, P]), MR[odd][hs, :],
                                                        start=False, stop=True)
                        else:
                            UM.wait_taken(pe, b, at_m[("exp", 2 * k + 1)])
                            for h in (2 * k, 2 * k + 1):
                                for f in range(2):
                                    col = ((h % 2) * 2 + f) * VX
                                    for c in range(2):
                                        v = VXT[:, bass.ds(b * 2 + c, 1), :].rearrange("p t c -> p (t c)")
                                        last = nc.tensor.matmul(bank[:, col:col + VX],
                                                                PT[:, h % 4, c, f * P:(f + 1) * P], v,
                                                                start=(c == 0), stop=(c == 1))
                        last.then_inc(U.full, 1)

                    UP_.open_full(pe)
                    UM.open_full(pe)
                    batches(pe, step)

                @block.scalar
                def _(act):
                    def step(what, b, odd):
                        group, kind, k = what
                        if group == "f":
                            if kind == "end":
                                act.wait_ge(c_e_need, b + 1)
                                nc.scalar.activation(CM[:, :, :], CM[:, :, :], ACT.Exp).then_inc(c_e, 1)
                            return
                        U, at = (UP_, at_p) if group == "p" else (UM, at_m)
                        n = at[(kind, k)]
                        if U.at[n][0] != "A":
                            return
                        bank = PS[:, U.bank(n), :]
                        if kind in "qk":
                            s_ = 2 * k + (kind == "k")
                            wait_split(act, b, s_, back=1)
                            U.wait_full(act, b, n)
                            for t in (2 * k, 2 * k + 1):
                                src = bank[:, (t % 2) * L:(t % 2 + 1) * L]
                                bias, low, scale, lows = ((BS[:, 0, t:t + 1], BS[:, 1, t:t + 1], 1.0 / math.sqrt(HD2),
                                                           BS[:, 3, 0:1]) if kind == "q" else
                                                          (pc("bk")[:, t:t + 1], BS[:, 2, t:t + 1], 1.0,
                                                           pc("signs")[:, 2:3]))
                                nc.scalar.activation(HI[:, s_, t % 2, :], src, ACT.Identity, bias=bias, scale=scale)
                                last = nc.scalar.activation(LO[:, s_, t % 2, :], src, ACT.Identity, bias=low,
                                                            scale=lows)
                        elif kind == "exp":
                            if k >= 4:
                                U.wait_full(act, b, at_m[("out", (k - 4) // 2)])
                            else:
                                U.wait_full(act, b, at_m[("out", (k + 12) // 2)], back=1)
                            U.wait_full(act, b, n)
                            last = nc.scalar.activation(PT[:, k % 4, :, :], bank.rearrange("p (c q) -> p c q", c=2),
                                                        ACT.Exp)
                        else:
                            if k == 0:
                                act.wait_ge(c_done, b + 1)
                            U.wait_full(act, b, n)
                            last = nc.scalar.activation(UB[odd][:, 2 * k:2 * k + 2, :, :].rearrange(
                                "p h f c -> p (h f c)"), bank[:, 0:4 * VX], ACT.Copy)
                        last.then_inc(U.sems["A"], 1)

                    UP_.open(act, "A")
                    UM.open(act, "A")
                    batches(act, step)

                @block.vector
                def _(dve):
                    def own(b, k):
                        dve.wait_ge(c_own, b * OWN + k)

                    OWN = 9

                    def step(what, b, odd):
                        group, kind, k = what
                        if group == "f":
                            ub = UB[odd][:, :, :, :].rearrange("p h f c -> p (h f) c")
                            cm = CM[:, :, :]
                            if kind == "start":
                                UM.wait_taken(dve, b, at_m[("out", H2 // 2 - 1)])
                                nc.vector.reciprocal(RI[:, 0, :], ub[:, :, VX - 1]).then_inc(c_own, 1)
                                own(b, 1)
                                nc.vector.tensor_tensor(cm, ub[:, :, 64:72], bcast(RI[:, 0, :], R2), ALU.mult)\
                                    .then_inc(c_own, 1)
                                ct = CT[:, bass.ds(b * 2, 2), :].rearrange("p f h -> p h f").unsqueeze(3)\
                                    .to_broadcast([P, H2, 2, R2])
                                cm4 = cm.rearrange("p (h f) r -> p h f r", f=2)
                                own(b, 2)
                                nc.vector.tensor_tensor(cm4, cm4, ct, ALU.add).then_inc(c_own, 1)
                                own(b, 3)
                                nc.vector.tensor_reduce(RI[:, 1, :], cm, AX.X, ALU.max).then_inc(c_own, 1)
                                own(b, 4)
                                nc.vector.tensor_tensor(cm, cm, bcast(RI[:, 1, :], R2), ALU.subtract)\
                                    .then_inc(c_e_need, 1)
                            else:
                                dve.wait_ge(c_e, b + 1)
                                nc.vector.tensor_reduce(RI[:, 1, :], cm, AX.X, ALU.add).then_inc(c_own, 1)
                                own(b, 5)
                                nc.vector.reciprocal(RI[:, 1, :], RI[:, 1, :]).then_inc(c_own, 1)
                                own(b, 6)
                                nc.vector.tensor_tensor(RI[:, 1, :], RI[:, 1, :], RI[:, 0, :], ALU.mult)\
                                    .then_inc(c_own, 1)
                                own(b, 7)
                                nc.vector.tensor_tensor(cm, cm, bcast(RI[:, 1, :], R2), ALU.mult).then_inc(c_own, 1)
                                own(b, 8)
                                nc.vector.tensor_tensor(UP[:, :, :, :],
                                                        ub[:, :, 0:64].rearrange("p a (r d) -> p a d r", r=R2),
                                                        cm.unsqueeze(2).to_broadcast([P, 2 * H2, HD2, R2]),
                                                        ALU.mult).then_inc(c_own, 1)
                                own(b, 9)
                                nc.vector.tensor_reduce(
                                    OC[:, bass.ds(b * 2, 2), :].rearrange("p f (h d) -> p h f d", h=H2),
                                    UP[:, :, :, :].rearrange("p (h f) d r -> p h f d r", f=2), AX.X,
                                    ALU.add).then_inc(c_done, 1)
                            return
                        if group == "m":
                            return
                        n = at_p[(kind, k)]
                        bank = PS[:, UP_.bank(n), :]
                        if kind in "qk":
                            UP_.wait_taken(dve, b, n)
                            s_ = 2 * k + (kind == "k")
                            sign = pc("signs")[:, 1:2] if kind == "q" else pc("signs")[:, 3:4]
                            nc.vector.scalar_tensor_tensor(out=QK[odd][:, s_ % 2, 2 * k:2 * k + 2, :],
                                                           in0=HI[:, s_, :, :], scalar=sign, in1=LO[:, s_, :, :],
                                                           op0=ALU.mult, op1=ALU.add).then_inc(c_split, 1)
                            return
                        UP_.wait_full(dve, b, n)
                        if kind == "max":
                            nc.vector.tensor_reduce(MX[:, :, k], bank.rearrange("p (f q) -> p f q", f=2), AX.X,
                                                    ALU.max, negate=True).then_inc(p_dve, 1)
                            if k == H2 - 1:
                                UP_.wait_taken(dve, b, n)
                                nc.vector.tensor_copy(MH[:, :, :], MX[:, :, :]).then_inc(c_mh, 1)
                                dve.wait_ge(c_mh, b + 1)
                                quad = lambda ap: ap.unsqueeze(2).to_broadcast([P, 2, 4, H2])
                                nc.vector.tensor_copy(M4[:, :, :, 0, :], quad(MH[:, :, :]))
                                nc.vector.tensor_tensor(M4[:, :, :, 1, :], quad(MX[:, :, :]), quad(MH[:, :, :]),
                                                        ALU.subtract).then_inc(c_m4, 1)
                        else:
                            nc.vector.tensor_copy(MR[odd][:, :], bank[:, 0:L]).then_inc(p_dve, 1)

                    UP_.open(dve, "V")
                    dve.sem_inc(c_split, 4)
                    dve.sem_inc(c_done, 2)
                    batches(dve, step)

            s5.close()
            HR = sbuf(sc_, "HR", [P, 2, NT * P])
            c_wf, c_hid, c_relu, c_ffn = sem("c_wf"), sem("c_hid"), sem("c_relu"), sem("c_ffn")
            with nc.Block() as block:
                @block.tensor
                def _(pe):
                    p_transpose(lambda t: OC[:, t, :], ready=False)
                    p_copied()
                    for t in range(NT):
                        last = nc.tensor.matmul(PS[:, 4 + t // 4, (t % 4) * P:(t % 4 + 1) * P],
                                                TR[:, t * P:(t + 1) * P], pc("wf"), start=True, stop=True)
                    last.then_inc(c_wf, 1)
                    p_transpose(lambda t: NRM[:, t, :])
                    p_copied()
                    for j in range(4):
                        for c in range(2):
                            n = 2 * j + c
                            nc.tensor.matmul(PS[:, n, :], pc("wr1")[:, c * P:(c + 1) * P],
                                             TR[:, j * 512:(j + 1) * 512], start=True, stop=True).then_inc(c_hid, 1)
                    for j in range(4):
                        pe.wait_ge(c_relu, 2 * j + 2)
                        for t in range(4 * j, 4 * j + 4):
                            for c in range(2):
                                last = nc.tensor.matmul(PS[:, j, (t % 4) * P:(t % 4 + 1) * P],
                                                        HR[:, c, t * P:(t + 1) * P], pc("wr2")[:, c * P:(c + 1) * P],
                                                        start=(c == 0), stop=(c == 1))
                        last.then_inc(c_ffn, 1)

                @block.scalar
                def _(act):
                    a_transposed(lambda j: TR[:, j * 512:(j + 1) * 512])
                    a_sqrt(NT)
                    a_transposed(lambda j: TR[:, j * 512:(j + 1) * 512])
                    for n in range(8):
                        act.wait_ge(c_hid, n + 1)
                        nc.scalar.activation(HR[:, n % 2, (n // 2) * 512:(n // 2 + 1) * 512], PS[:, n, :], ACT.Relu,
                                             bias=pc("br1")[:, n % 2:n % 2 + 1]).then_inc(c_relu, 1)
                    a_sqrt(NT)

                @block.vector
                def _(dve):
                    V.link(nc.vector.tensor_tensor(XL[:, :, :], XL[:, :, :], rows(pc("bf"), NT), ALU.add))
                    dve.wait_ge(c_wf, 1)
                    for j in range(4):
                        last = nc.vector.tensor_tensor(XL[:, 4 * j:4 * j + 4, :], XL[:, 4 * j:4 * j + 4, :],
                                                       tile4(PS[:, 4 + j, :]), ALU.add)
                    V.link(last)
                    V.link(v_norm(lambda t: XL[:, t, :], lambda t: NRM[:, t, :]))
                    v_ready(v_affine(NRM, pc("g2"), pc("b2")))
                    V.link(nc.vector.tensor_tensor(XL[:, :, :], XL[:, :, :], rows(pc("br2"), NT), ALU.add))
                    for j in range(4):
                        dve.wait_ge(c_ffn, j + 1)
                        last = nc.vector.tensor_tensor(XL[:, 4 * j:4 * j + 4, :], XL[:, 4 * j:4 * j + 4, :],
                                                       tile4(PS[:, j, :]), ALU.add)
                    V.link(last)
                    V.link(v_norm(lambda t: XL[:, t, :], lambda t: NRM[:, t, :]))
                    V.link(nc.vector.tensor_tensor(flat(X[:, :, :]), flat(X[:, :, :]), flat(NRM[:, :, :]), ALU.add))

        sd = ExitStack()
        with sd:
            HA = sbuf(sd, "HA", [P, 2, 4, 512])
            HB = sbuf(sd, "HB", [P, 2, 4, 512])
            YT = sbuf(sd, "YT", [P, NT, D])
            with nc.Block() as block:
                @block.tensor
                def _(pe):
                    p_transpose(lambda t: NRM[:, t, :])

                @block.scalar
                def _(act):
                    a_sqrt(NT)
                    a_transposed(lambda j: TR[:, j * 512:(j + 1) * 512])

                @block.vector
                def _(dve):
                    dve.wait_ge(loadD, 16)
                    v_ready(v_norm(lambda t: X[:, t, :], lambda t: NRM[:, t, :]))

            d_full, d_act, d_dve = sem("d_full"), sem("d_act"), sem("d_dve")
            order = [(k, s_, c) for k in ("w1", "w2", "h1", "h2") for s_ in range(2) for c in range(4)]
            order += [("w3", s_, 0) for s_ in range(2)]
            U = Uses(d_full, {"A": d_act, "V": d_dve}, ["V" if k in ("w2", "w3") else "A" for k, _, _ in order])
            where = {k: n for n, k in enumerate(order)}
            with nc.Block() as block:
                @block.tensor
                def _(pe):
                    U.open_full(pe)
                    with pe.Fori(0, NG // 2) as g:
                        U.wait_start(pe, g)
                        for n, (kind, s_, c) in enumerate(order):
                            bank = PS[:, n % 8, :]
                            U.wait_empty(pe, g, n)
                            if kind in ("w1", "w2"):
                                last = nc.tensor.matmul(bank, pd(kind)[:, c * P:(c + 1) * P],
                                                        TR[:, bass.ds(g * 1024 + s_ * 512, 512)], start=True, stop=True)
                            elif kind in ("h1", "h2"):
                                src, before = (HB, "w2") if kind == "h1" else (HA, "h1")
                                for k in range(4):
                                    if c == 0:
                                        U.wait_taken(pe, g, where[(before, s_, k)])
                                    at = k * DH + c * P
                                    last = nc.tensor.matmul(bank, pd(kind)[:, at:at + P], src[:, s_, k, :],
                                                            start=(k == 0), stop=(k == 3))
                            else:
                                U.wait_taken(pe, g, where[("h2", s_, 3)])
                                for t in range(4):
                                    for k in range(4):
                                        last = nc.tensor.matmul(bank[:, t * P:(t + 1) * P],
                                                                HB[:, s_, k, t * P:(t + 1) * P],
                                                                pd("w3")[:, k * P:(k + 1) * P],
                                                                start=(k == 0), stop=(k == 3))
                            last.then_inc(d_full, 1)

                @block.scalar
                def _(act):
                    U.open(act, "A")
                    with act.Fori(0, NG // 2) as g:
                        for n, (kind, s_, c) in enumerate(order):
                            if kind in ("w2", "w3"):
                                continue
                            U.wait_full(act, g, n)
                            if kind == "h2" and c == 0:
                                U.wait_full(act, g, where[("h1", s_, 3)])
                            func, scale, dst = {"w1": (ACT.Silu, "s1", HA), "h1": (ACT.Gelu, "t1", HA),
                                                "h2": (ACT.Gelu, "t2", HB)}[kind]
                            if kind == "h1" and c == 0:
                                U.wait_taken(act, g, where[("w2", s_, 3)])
                            nc.scalar.activation(dst[:, s_, c, :], PS[:, n % 8, :], func,
                                                 scale=pd(scale)[:, c:c + 1]).then_inc(d_act, 1)

                @block.vector
                def _(dve):
                    U.open(dve, "V")
                    with dve.Fori(0, NG // 2) as g:
                        for n, (kind, s_, c) in enumerate(order):
                            if kind == "w2":
                                U.wait_taken(dve, g, where[("w1", s_, c)])
                                U.wait_full(dve, g, n)
                                nc.vector.scalar_tensor_tensor(out=HB[:, s_, c, :], in0=PS[:, n % 8, :],
                                                               scalar=pd("s2")[:, c:c + 1], in1=HA[:, s_, c, :],
                                                               op0=ALU.mult, op1=ALU.mult).then_inc(d_dve, 1)
                            elif kind == "w3":
                                U.wait_full(dve, g, n)
                                nc.vector.tensor_tensor(YT[:, bass.ds(g * 8 + s_ * 4, 4), :], tile4(PS[:, n % 8, :]),
                                                        rows(pd("s3"), 4), ALU.mult).then_inc(d_dve, 1)

            done, x_final = sem("stored"), sem("x_final")
            with nc.Block() as block:
                @block.scalar
                def _(act):
                    a_sqrt(NT)

                @block.vector
                def _(dve):
                    V.link(v_norm(lambda t: YT[:, t, :], lambda t: NRM[:, t, :]))
                    for j in range(2):
                        nc.vector.tensor_tensor(flat(X[:, 8 * j:8 * j + 8, :]), flat(X[:, 8 * j:8 * j + 8, :]),
                                                flat(NRM[:, 8 * j:8 * j + 8, :]), ALU.add).then_inc(x_final, 1)

                @block.sync
                def _(sp):
                    for j in range(2):
                        sp.wait_ge(x_final, j + 1)
                        sp.dma_start(out_dram[:, 8 * j:8 * j + 8, :], X[:, 8 * j:8 * j + 8, :]).then_inc(done, 16)
                    sp.wait_ge(done, 32)


def packed(pack, parts):
    out = np.zeros((P, offsets(pack)[1]), np.float32)
    for name, (at, width) in offsets(pack)[0].items():
        part = np.asarray(parts[name])
        assert part.shape[1] == width, (name, part.shape)
        out[:part.shape[0], at:at + width] = part
    return out


def every(v):
    v = np.asarray(v).reshape(1, -1)
    return np.broadcast_to(v, (P, v.shape[1]))


def column_chunks(v, n):
    return np.asarray(v).reshape(n, P).T


def row_chunks(w):
    n = w.shape[0] // P
    return w.reshape(n, P, -1).transpose(1, 0, 2).reshape(P, -1)


def layout(i):
    i = {k: np.asarray(v) for k, v in i.items()}
    a = {k[8:]: v for k, v in i.items() if k.startswith("L0_attn_")}
    f = {k[7:]: v for k, v in i.items() if k.startswith("L0_ffn_")}
    c = {k[8:]: v for k, v in i.items() if k.startswith("L1_attn_")}
    m = {k[7:]: v for k, v in i.items() if k.startswith("L1_ffn_")}
    r = np.arange(P)
    ident = np.eye(P, dtype=np.float32)
    later = (r[:, None] > r[None, :]).astype(np.float32)
    firs = np.zeros((P, 4), np.float32)
    firs[:, 1:] = a["firs"].reshape(P, FIRS)
    firl = np.zeros((P, 64), np.float32)
    firl[:, 1:] = a["firl"].reshape(P, FIRL)
    gw1s = np.zeros((NH, DK, NH, P), np.float32)
    for h in range(NH):
        gw1s[h, :16, h, :] = a["gW1"][D:D + 16]
    packs = {}
    packs["pa"] = packed(PACK_A, {
        "ident": ident, "low": -later, "upp": -later.T, "incl": 1 - later,
        "wqkv": np.concatenate([a["Wq"], a["Wk"], a["Wv"]], 1),
        "cwb": every(np.concatenate([a[k].T.reshape(-1) for k in ("cwq", "cwk", "cwv")])),
        "wid": a["Wid"], "wb": a["Wb"], "firs": firs, "firl": firl, "gw1h": a["gW1"][:D],
        "gw1s": gw1s.reshape(P, NH * P), "gb1": a["gb1"][:, None], "gw2": a["gW2"],
        "gb2": every(np.tile(a["gb2"], NH)), "ltemp": every(a["log_temp"]), "floor": every(a["floor_param"]),
        "crl": every(a["conv_res_logit"]), "alpha": every(a["alpha_id"]),
        "onw": np.tile(a["o_norm_w"], NH)[:, None], "wo": a["Wo"]})
    packs["pb"] = packed(PACK_B, {
        "ident": ident, "wqkv": f["Wqkv"].T, "bqkv": every(f["bqkv"]), "wo": f["Wo"].T, "bo": every(f["bo"]),
        "g1": every(f["g1"]), "be1": every(f["be1"]), "g2": every(f["g2"]), "be2": every(f["be2"]),
        "wg": f["Wg"].T, "w1": f["W1"].transpose(1, 0, 2).reshape(P, E * DF),
        "b1": f["b1"].reshape(E * 4, P).T, "w2": row_chunks(f["W2"].reshape(E * DF, D)), "b2": f["b2"],
        "iota": every(np.arange(E, dtype=np.float32) - E)})

    def by_quad(w):
        return np.tile(w.T.reshape(-1, H2, 1, HD2), (1, 1, 4, 1)).reshape(w.shape[1], 4 * P)

    part = r % 32 // HD2
    qlow, klow = (part >= 2).astype(np.float32), (part % 2).astype(np.float32)
    signs = np.stack([qlow, 1 - 2 * qlow, klow, 1 - 2 * klow], 1)
    mask4 = np.zeros((4, 32, 4), np.float32)
    for h in range(4):
        mask4[h, :, h] = 1
    packs["pc"] = packed(PACK_C, {
        "wq": by_quad(c["Wq"]), "wk": by_quad(c["Wk"]),
        "bq": by_quad(c["bq"][:, None]).reshape(4, P).T, "bk": by_quad(c["bk"][:, None]).reshape(4, P).T,
        "signs": signs, "sel": (r[:, None] % H2 == np.arange(H2)).astype(np.float32),
        "wv": c["Wv"].T, "bv": every(c["bv"]), "wqv": row_chunks(c["Wqv"]), "bqv": column_chunks(c["bqv"], 4),
        "wsq": np.tile(c["Ws"][0, :QK2], 4)[:, None], "mask4": mask4.reshape(P, 4), "wso": every(c["Ws"][0, QK2:]),
        "bs": every(c["bs"]), "wf": c["Wf"].T, "bf": every(c["bf"]), "wr1": c["Wr1"].T,
        "br1": column_chunks(c["br1"], 2), "wr2": row_chunks(c["Wr2"].T), "br2": every(c["br2"]),
        "g1": every(c["g1"]), "b1": every(c["b1"]), "g2": every(c["g2"]), "b2": every(c["b2"])})
    packs["pd"] = packed(PACK_D, {
        "w1": m["w1_w"].T, "w2": m["w2_w"].T, "h1": row_chunks(m["h1_w"].T), "h2": row_chunks(m["h2_w"].T),
        "w3": row_chunks(m["w3_w"].T), "s1": column_chunks(m["w1_s"], 4), "s2": column_chunks(m["w2_s"], 4),
        "t1": column_chunks(m["h1_s"], 4), "t2": column_chunks(m["h2_s"], 4), "s3": every(m["w3_s"])})
    packs["x"] = a["hs"].reshape(NT, P, D).transpose(1, 0, 2)
    return packs


def kernel(**inputs):
    import concourse.bacc as bacc
    from concourse.bass_utils import run_bass_kernel_spmd

    nc = bacc.Bacc("TRN2", target_bir_lowering=False, num_devices=1)
    arrays, args = {}, []
    for name, a in layout(inputs).items():
        arrays[f"in_{name}"] = np.ascontiguousarray(a, dtype=np.float32)
        args.append((name, nc.dram_tensor(f"in_{name}", a.shape, F32, kind="ExternalInput").ap()))
    args = dict(args)
    out = nc.dram_tensor("out_x", (P, NT, D), F32, kind="ExternalOutput").ap()
    build(nc, args["x"], args["pa"], args["pb"], args["pc"], args["pd"], out)
    r = run_bass_kernel_spmd(nc, [arrays], core_ids=[0])
    got = np.asarray(r.results[0]["out_x"])
    return got.transpose(1, 0, 2).reshape(B, L, D)
```

```python
import math
from contextlib import ExitStack

import numpy as np

import concourse.bass as bass
from concourse import mybir

F32 = mybir.dt.float32
F32R = mybir.dt.float32r
ALU = mybir.AluOpType
ACT = mybir.ActivationFunctionType
AX = mybir.AxisListType

P = 128
B, L, D = 8, 256, 128
NT = B * L // P
NG = NT // 4
NH, DK = 4, 32
TAPS, FIRS, FIRL = 4, 3, 63
PAD = FIRL
E, DF = 8, 512
H2, HD2, R2, QK2 = 16, 8, 8, 32
VX = R2 * HD2 + R2 + 1
DH = 512
FLOOR = 0.05
LEVELS = 7


PACK_A = [("ident", 128), ("low", 128), ("upp", 128), ("incl", 128), ("wqkv", 384), ("cwb", 1536),
          ("wid", 128), ("wb", 4), ("firs", 4), ("firl", 64), ("gw1h", 128), ("gw1s", 512), ("gb1", 1),
          ("gw2", 4), ("gb2", 16), ("ltemp", 16), ("floor", 16), ("crl", 4), ("alpha", 4), ("onw", 1),
          ("wo", 128)]
PACK_B = [("ident", 128), ("wqkv", 384), ("bqkv", 384), ("wo", 128), ("bo", 128), ("g1", 128), ("be1", 128),
          ("g2", 128), ("be2", 128), ("wg", 8), ("w1", E * DF), ("b1", E * 4), ("w2", E * DF), ("b2", 128),
          ("iota", 8)]
PACK_C = [("wq", 512), ("wk", 512), ("bq", 4), ("bk", 4), ("signs", 4), ("sel", H2), ("wv", 64), ("bv", 64), ("wqv", 512),
          ("bqv", 4), ("wsq", 1), ("mask4", 4), ("wso", 8), ("bs", 1), ("wf", 128), ("bf", 128), ("wr1", 256),
          ("br1", 2), ("wr2", 256), ("br2", 128), ("g1", 128), ("b1", 128), ("g2", 128), ("b2", 128)]
PACK_D = [("w1", DH), ("w2", DH), ("h1", 4 * DH), ("h2", 4 * DH), ("w3", DH), ("s1", 4), ("s2", 4),
          ("t1", 4), ("t2", 4), ("s3", 128)]


def offsets(pack):
    at, out = 0, {}
    for name, width in pack:
        out[name] = (at, width)
        at += width
    return out, at


class Chain:

    def __init__(self, eng, sem):
        self.eng, self.sem, self.done, self.base, self.inside = eng, sem, 0, None, 0

    def enter(self, turn, per):
        self.base, self.inside, self.per = turn * per, 0, per

    def leave(self, turns):
        assert self.inside == self.per, (self.inside, self.per)
        self.done += turns * self.per
        self.base = None

    def mark(self, ins):
        ins.then_inc(self.sem, 1)
        if self.base is None:
            self.done += 1
            return self.done
        self.inside += 1
        return self.base + (self.done + self.inside)

    def link(self, ins):
        self.eng.wait_ge(self.sem, self.mark(ins))


class Uses:

    def __init__(self, full, sems, engines, first=0, ring=8):
        self.full, self.sems, self.slots, self.first, self.ring = full, sems, len(engines), first, ring
        self.per = {e: 0 for e in sems}
        self.n, self.order, self.at = 0, [], []
        for e in engines:
            if e:
                self.per[e] += 1
                self.n += 1
            self.order.append(self.n)
            self.at.append((e, self.per[e]) if e else None)

    def bank(self, n):
        return self.first + n % self.ring

    def open(self, eng, e):
        eng.sem_inc(self.sems[e], self.per[e])

    def open_full(self, pe):
        pe.sem_inc(self.full, self.n)

    def wait_start(self, pe, g):
        for e, s in self.sems.items():
            pe.wait_ge(s, g * self.per[e] + self.per[e])

    def wait_empty(self, pe, g, n):
        n -= self.ring
        while n >= 0 and not self.at[n]:
            n -= self.ring
        if n >= 0:
            self.wait_taken(pe, g, n)
        elif self.slots % self.ring == 0:
            while not self.at[n]:
                n -= self.ring
            e, k = self.at[n]
            pe.wait_ge(self.sems[e], g * self.per[e] + k)

    def wait_taken(self, pe, g, n):
        e, k = self.at[n]
        pe.wait_ge(self.sems[e], g * self.per[e] + (self.per[e] + k))

    def wait_full(self, eng, g, n, back=0):
        eng.wait_ge(self.full, g * self.n + ((1 - back) * self.n + self.order[n]))


def build(nc, x_in, pa_in, pb_in, pc_in, pd_in, out_dram):
    ctx = ExitStack()
    with ctx:
        names = {}

        def sem(name):
            if name not in names:
                names[name] = ctx.enter_context(nc.semaphore(name))
            return names[name]

        def sbuf(stack, name, shape):
            return stack.enter_context(nc.sbuf_tensor(name, shape, F32))

        def sbufr(stack, name, shape):
            return stack.enter_context(nc.sbuf_tensor(name, shape, F32R))

        X = sbuf(ctx, "X", [P, NT, D])
        NRM = sbuf(ctx, "NRM", [P, NT, D])
        TR = sbuf(ctx, "TR", [P, NT * D])
        STAT = sbuf(ctx, "STAT", [P, NT, 6])
        MV = sbuf(ctx, "MV", [P, NT, 2])
        SQA = sbuf(ctx, "SQA", [P, 256])
        SQR = sbuf(ctx, "SQR", [P, 256])
        RS = sbuf(ctx, "RS", [P, NT])
        oa, na = offsets(PACK_A)
        ob, nb = offsets(PACK_B)
        oc, ncc = offsets(PACK_C)
        od, nd = offsets(PACK_D)
        ndr = od["s1"][0]
        PB = sbuf(ctx, "PB", [P, nb])
        PS = ctx.enter_context(nc.psum_tensor("PS", [P, 8, 512], F32))

        def pb(name, rows=P):
            at, width = ob[name]
            return PB[0:rows, at:at + width]

        loadA, loadB, loadC, loadD = sem("load_a"), sem("load_b"), sem("load_c"), sem("load_d")
        load_x = sem("load_x")
        dve_step, act_step, pool_step = sem("dve_step"), sem("act_step"), sem("pool_step")
        sqrt_asked, sqrt_given = sem("sqrt_asked"), sem("sqrt_given")
        norm_ready = sem("norm_ready")
        tr_bank, tr_copied = sem("tr_bank"), sem("tr_copied")
        V = Chain(nc.vector, dve_step)
        A = Chain(nc.scalar, act_step)
        G = Chain(nc.gpsimd, pool_step)
        count = {"sqrt_v": 0, "sqrt_a": 0, "norm_v": 0, "norm_p": 0, "tr_p": 0, "tr_a": 0, "tr_v": 0}

        def tile4(ap):
            return ap.rearrange("p (t c) -> p t c", t=4)

        def bcast(ap, n):
            return ap.unsqueeze(2).to_broadcast([P, ap.shape[1], n])

        def rows(ap, n):
            return ap.unsqueeze(1).to_broadcast([P, n, ap.shape[1]])

        def v_sqrt(arg_width):
            count["sqrt_v"] += 1
            nc.vector.wait_ge(sqrt_given, count["sqrt_v"])

        def a_sqrt(width):
            count["sqrt_a"] += 1
            nc.scalar.wait_ge(sqrt_asked, count["sqrt_a"])
            nc.scalar.activation(SQR[:, :width], SQA[:, :width], ACT.Sqrt).then_inc(sqrt_given, 1)

        def v_ask(ins):
            ins.then_inc(sqrt_asked, 1)

        def v_norm(src, dst, eps=1e-5, tiles=NT):
            for t in range(tiles):
                last = nc.vector.bn_stats(STAT[:, t, :], src(t))
            V.link(last)
            for t in range(tiles):
                last = nc.vector.bn_aggr(MV[:, t, :], STAT[:, t, :])
            V.link(last)
            v_ask(nc.vector.tensor_scalar(SQA[:, :tiles], MV[:, :tiles, 1], eps, None, ALU.add))
            v_sqrt(tiles)
            V.link(nc.vector.reciprocal(RS[:, :tiles], SQR[:, :tiles]))
            for t in range(tiles):
                last = nc.vector.tensor_scalar(dst(t), src(t), MV[:, t, 0:1], RS[:, t:t + 1],
                                               ALU.subtract, ALU.mult)
            return last

        def v_ready(last):
            last.then_inc(norm_ready, 1)
            count["norm_v"] += 1

        def p_transpose(src, banks=(0, 1, 2, 3), ready=True):
            if ready:
                count["norm_p"] += 1
                nc.tensor.wait_ge(norm_ready, count["norm_p"])
            for j, bank in enumerate(banks):
                for t in range(4):
                    last = nc.tensor.transpose(PS[:, bank, t * P:(t + 1) * P], src(4 * j + t), ident)
                last.then_inc(tr_bank, 1)
            count["tr_p"] += len(banks)

        def a_transposed(dst, banks=(0, 1, 2, 3)):
            for j, bank in enumerate(banks):
                count["tr_a"] += 1
                nc.scalar.wait_ge(tr_bank, count["tr_a"])
                nc.scalar.activation(dst(j), PS[:, bank, :], ACT.Copy).then_inc(tr_copied, 1)

        def p_copied():
            nc.tensor.wait_ge(tr_copied, count["tr_p"])

        sa = ctx.enter_context(ExitStack())
        DEL = sbuf(sa, "DEL", [P, NT, D])
        QTK = sbuf(sa, "QTK", [P, NT, D])
        KTK = sbuf(sa, "KTK", [P, NT, D])
        VTK = sbuf(sa, "VTK", [P, NT, D])
        ITK = sbuf(sa, "ITK", [P, NT, D])
        VPT = sbuf(sa, "VPT", [P, B, PAD + L])
        FS = sbuf(sa, "FS", [P, B, L])
        FL0 = sbuf(sa, "FL0", [P, B, L])
        FL1 = sbuf(sa, "FL1", [P, B, L])
        XT = sbuf(sa, "XT", [P, B, 3 + L])
        PA = sbuf(sa, "PA", [P, na])
        BETA = sbuf(sa, "BETA", [P, NT, NH])

        def pa(name):
            at, width = oa[name]
            return PA[:, at:at + width]

        ident = pa("ident")

        s1 = ExitStack()
        with s1:
            WT = sbuf(s1, "WT", [P, 3, TAPS, D])
            ST = sbuf(s1, "ST", [P, 4, 512])
            SB = sbuf(s1, "SB", [NH, 512])
            xt_zero, wt_ready, x_turned = sem("xt_zero"), sem("wt_ready"), sem("x_turned")
            a1_proj, a1_staged, a1_turned, a1_out = (sem("a1_proj"), sem("a1_staged"), sem("a1_turned"),
                                                     sem("a1_out"))
            with nc.Block() as block:
                @block.sync
                def _(sp):
                    sp.dma_start(X[:, :, :], x_in).then_inc(load_x, 16)
                    sp.dma_start(PA[:, :], pa_in).then_inc(loadA, 16)

                @block.gpsimd
                def _(pool):
                    nc.gpsimd.memset(XT[:, :, 0:3], 0.0).then_inc(xt_zero, 1)
                    nc.gpsimd.memset(VPT[:, :, 0:PAD], 0.0).then_inc(xt_zero, 1)
                    nc.gpsimd.memset(FS[:, :, :], 0.0).then_inc(xt_zero, 1)
                    nc.gpsimd.memset(FL0[:, :, :], 0.0).then_inc(xt_zero, 1)
                    nc.gpsimd.memset(FL1[:, :, :], 0.0).then_inc(xt_zero, 1)

                @block.vector
                def _(dve):
                    dve.wait_ge(load_x, 16)
                    v_ready(v_norm(lambda t: X[:, t, :], lambda t: NRM[:, t, :]))
                    dve.wait_ge(loadA, 16)
                    for p in range(3):
                        last = nc.vector.tensor_tensor(
                            WT[:, p, :, :], rows(pa("wqkv")[:, p * D:(p + 1) * D], TAPS),
                            pa("cwb")[:, p * 512:(p + 1) * 512].rearrange("p (j c) -> p j c", j=TAPS), ALU.mult)
                    last.then_inc(wt_ready, 1)
                    dve.sem_inc(a1_out, 1)
                    with dve.Fori(0, NG) as g:
                        for n, (bank, dst) in enumerate(((5, QTK), (6, KTK), (7, VTK), (5, ITK))):
                            dve.wait_ge(a1_turned, g * 5 + (n + 2))
                            nc.vector.tensor_copy(dst[:, bass.ds(g * 4, 4), :], tile4(PS[:, bank, :]))\
                                .then_inc(a1_out, 1)
                        dve.wait_ge(a1_turned, g * 5 + 6)
                        nc.vector.tensor_copy(BETA[:, bass.ds(g * 4, 4), :],
                                              PS[:, 6, 0:16].rearrange("p (t h) -> p t h", t=4)).then_inc(a1_out, 1)
                        nc.vector.tensor_copy(VPT[:, bass.ds(g * 2, 2), PAD:PAD + L],
                                              ST[:, 2, :].rearrange("p (b l) -> p b l", b=2)).then_inc(a1_out, 1)

                @block.tensor
                def _(pe):
                    pe.wait_ge(loadA, 16)
                    p_transpose(lambda t: NRM[:, t, :])
                    p_copied()
                    pe.wait_ge(wt_ready, 1)
                    pe.wait_ge(xt_zero, 1)
                    pe.sem_inc(a1_turned, 1)
                    with pe.Fori(0, NG) as g:
                        for p in range(3):
                            for j in range(TAPS):
                                last = nc.tensor.matmul(PS[:, p, :].rearrange("p (b l) -> p b l", b=2),
                                                        WT[:, p, j, :], XT[:, bass.ds(g * 2, 2), j:j + L],
                                                        start=(j == 0), stop=(j == TAPS - 1))
                            last.then_inc(a1_proj, 1)
                        now = XT[:, bass.ds(g * 2, 2), 3:3 + L]
                        nc.tensor.matmul(PS[:, 3, :].rearrange("p (b l) -> p b l", b=2), pa("wid"), now,
                                         start=True, stop=True).then_inc(a1_proj, 1)
                        nc.tensor.matmul(PS[0:NH, 4, :].rearrange("p (b l) -> p b l", b=2), pa("wb"), now,
                                         start=True, stop=True).then_inc(a1_proj, 1)
                        pe.wait_ge(a1_out, g * 6 + 1)
                        for n, bank in enumerate((5, 6, 7, 5)):
                            pe.wait_ge(a1_staged, g * 5 + (n + 1))
                            if n == 3:
                                pe.wait_ge(a1_staged, g * 5 + 5)
                                pe.wait_ge(a1_out, g * 6 + 3)
                            for t in range(4):
                                last = nc.tensor.transpose(PS[:, bank, t * P:(t + 1) * P],
                                                           ST[:, n, t * P:(t + 1) * P], ident)
                            last.then_inc(a1_turned, 1)
                        for t in range(4):
                            last = nc.tensor.transpose(PS[:, 6, t * NH:(t + 1) * NH],
                                                       SB[:, t * P:(t + 1) * P], ident[0:NH, 0:NH])
                        last.then_inc(a1_turned, 1)

                @block.scalar
                def _(act):
                    a_sqrt(NT)
                    a_transposed(lambda j: XT[:, 2 * j:2 * j + 2, 3:3 + L])
                    with act.Fori(0, NG) as g:
                        act.wait_ge(a1_turned, g * 5 + 1)
                        act.wait_ge(a1_out, g * 6 + 1)
                        for n in range(5):
                            act.wait_ge(a1_proj, g * 5 + (n + 1))
                            dst, src, func = ((ST[:, n, :], PS[:, n, :], ACT.Silu if n < 3 else ACT.Copy) if n < 4
                                              else (SB[:, :], PS[0:NH, 4, :], ACT.Sigmoid))
                            nc.scalar.activation(dst, src, func).then_inc(a1_staged, 1)

        s2 = ExitStack()
        with s2:
            RQ = sbuf(s2, "RQ", [P, NT * NH])
            RK = sbuf(s2, "RK", [P, NT * NH])
            RKB = sbuf(s2, "RKB", [P, NT * NH])
            QH = NRM[:, 0:4, :]
            KH = NRM[:, 4:8, :]
            Y = sbuf(s2, "Y", [P, 4, 2, D])
            TQ = sbuf(s2, "TQ", [P, 3, 4, P])
            TZ = PB[:, 0:3 * 4 * NH * P].rearrange("p (s t h c) -> p s t h c", s=3, t=4, h=NH)
            PW = [sbuf(s2, f"PW{n}", [P, 16, 2, P]) for n in range(2)]
            AT = TR[:, :].rearrange("p (u c) -> p u c", u=16)
            SS = sbuf(s2, "SS", [P, 2, D])
            W1T = sbuf(s2, "W1T", [P, 2, P])
            a2_prep, a2_bank, a2_act, a2_dve = sem("a2_prep"), sem("a2_bank"), sem("a2_act"), sem("a2_dve")

            uses = [("turn", "A")] * 3 + [("mask", "V")] * 12
            for lv in range(LEVELS):
                uses += [("apply", "V")] * 2
                uses += [("square", "A")] * (8 if lv < LEVELS - 2 else 4 if lv == LEVELS - 2 else 0)
            uses += [("state", "V"), ("w1", "A"), ("ws", "V"), ("o", "V")]
            NU = len(uses)
            U = Uses(a2_bank, {"A": a2_act, "V": a2_dve}, [e for _, e in uses])

            pairs = [2 * h + b for b in range(2) for h in range(NH)]

            def bank_of(n):
                return n % 8

            TAPS_AFTER = (3, 3, 2, 2, 2, 2, 0)
            ss_zero, a2_zeros = sem("ss_zero"), sem("a2_zeros")
            with nc.Block() as block:
                @block.gpsimd
                def _(pool):
                    nc.gpsimd.memset(SS[:, :, :], 0.0).then_inc(ss_zero, 1)
                    nc.gpsimd.memset(TZ[:, :, :, :, :], 0.0).then_inc(ss_zero, 1)

                @block.tensor
                def _(pe):
                    U.open_full(pe)
                    with pe.Fori(0, NG) as g:
                        n = 0
                        U.wait_start(pe, g)
                        for k, src in enumerate((KH, None, QH)):
                            pe.wait_ge(a2_prep, g * 4 + (k + 1))
                            for t in range(4):
                                last = nc.tensor.transpose(PS[:, bank_of(n), t * P:(t + 1) * P],
                                                           Y[:, t, 1, :] if src is None else src[:, t, :], ident)
                            last.then_inc(a2_bank, 1)
                            n += 1
                        for l, r in ((2, 1), (1, 2), (1, 0)):
                            if (l, r) == (1, 0):
                                U.wait_taken(pe, g, 2)
                            else:
                                U.wait_taken(pe, g, 1)
                                pe.wait_ge(a2_zeros, g * 2 + r)
                            for t in range(4):
                                U.wait_empty(pe, g, n)
                                nc.tensor.matmul(PS[:, bank_of(n), :], TQ[:, l, t, :],
                                                 TZ[:, r, t, :, :].rearrange("p h c -> p (h c)"),
                                                 start=True, stop=True).then_inc(a2_bank, 1)
                                n += 1
                        ready = [10] * 16
                        y_use = None
                        pe.wait_ge(a2_prep, g * 4 + 4)
                        for lv in range(LEVELS):
                            old = PW[lv % 2]
                            new_y = []
                            for half in range(2):
                                U.wait_empty(pe, g, n)
                                U.wait_taken(pe, g, ready[4 * (NH - 1) + 2 * half])
                                if y_use is not None:
                                    U.wait_taken(pe, g, y_use[half])
                                for t in (2 * half, 2 * half + 1):
                                    for h in range(NH):
                                        o = PS[:, bank_of(n), :].rearrange("p (t k c) -> p t k c", t=2, k=2)
                                        last = nc.tensor.matmul(o[:, t % 2, :, h * DK:(h + 1) * DK],
                                                                old[:, 4 * h + t, 1, :],
                                                                Y[:, t, :, h * DK:(h + 1) * DK],
                                                                start=True, stop=True)
                                last.then_inc(a2_bank, 1)
                                new_y.append(n)
                                n += 1
                            y_use = new_y
                            if lv < LEVELS - 2:
                                for pair in pairs:
                                    U.wait_empty(pe, g, n)
                                    U.wait_taken(pe, g, ready[2 * pair + 1])
                                    for u in (2 * pair, 2 * pair + 1):
                                        at = (u % 2) * 256
                                        nc.tensor.matmul(PS[:, bank_of(n), at:at + P], old[:, u, 1, :],
                                                         old[:, u, 0, :], start=True, stop=True)
                                        last = nc.tensor.matmul(PS[:, bank_of(n), at + P:at + 2 * P],
                                                                old[:, u, 0, :], old[:, u, 1, :],
                                                                start=True, stop=True)
                                    last.then_inc(a2_bank, 1)
                                    ready[2 * pair] = ready[2 * pair + 1] = n
                                    n += 1
                            elif lv == LEVELS - 2:
                                for quad in range(4):
                                    U.wait_empty(pe, g, n)
                                    U.wait_taken(pe, g, ready[4 * quad + 3])
                                    for u in range(4 * quad, 4 * quad + 4):
                                        last = nc.tensor.matmul(PS[:, bank_of(n), (u % 4) * P:(u % 4 + 1) * P],
                                                                old[:, u, 0, :], old[:, u, 1, :],
                                                                start=True, stop=True)
                                    last.then_inc(a2_bank, 1)
                                    for u in range(4 * quad, 4 * quad + 4):
                                        ready[u] = n
                                    n += 1
                        U.wait_empty(pe, g, n)
                        U.wait_taken(pe, g, y_use[0])
                        U.wait_taken(pe, g, y_use[1])
                        n_state = n
                        for b in range(2):
                            for h in range(NH):
                                hs = slice(DK * h, DK * h + DK)
                                last = nc.tensor.matmul(PS[hs, bank_of(n), b * DK:(b + 1) * DK], KH[:, 2 * b, hs],
                                                        Y[:, 2 * b, 0, hs], start=True, stop=True)
                        last.then_inc(a2_bank, 1)
                        n += 1
                        U.wait_empty(pe, g, n)
                        n_w1 = n
                        for b in range(2):
                            last = nc.tensor.transpose(PS[:, bank_of(n), b * P:(b + 1) * P], Y[:, 2 * b + 1, 1, :],
                                                       ident)
                        last.then_inc(a2_bank, 1)
                        n += 1
                        U.wait_empty(pe, g, n)
                        U.wait_taken(pe, g, n_state)
                        U.wait_taken(pe, g, n_w1)
                        for b in range(2):
                            last = nc.tensor.matmul(PS[:, bank_of(n), b * P:(b + 1) * P], W1T[:, b, :], SS[:, b, :],
                                                    start=True, stop=True)
                        last.then_inc(a2_bank, 1)
                        n_ws = n
                        n += 1
                        U.wait_empty(pe, g, n)
                        U.wait_taken(pe, g, 14)
                        for t in (0, 2, 1, 3):
                            if t == 1:
                                U.wait_taken(pe, g, n_ws)
                            if t % 2:
                                nc.tensor.matmul(PS[:, bank_of(n), t * P:(t + 1) * P], TQ[:, 0, t, :],
                                                 SS[:, t // 2, :], start=True, stop=False)
                            for h in range(NH):
                                hs = slice(DK * h, DK * h + DK)
                                o = PS[:, bank_of(n), t * P + h * DK:t * P + (h + 1) * DK]
                                last = nc.tensor.matmul(o, AT[:, 4 * h + t, :], Y[:, t, 0, hs],
                                                        start=(t % 2 == 0), stop=(t % 2 == 0 or h == NH - 1))
                        last.then_inc(a2_bank, 1)
                        n += 1
                        assert n == NU

                @block.scalar
                def _(act):
                    a_sqrt(NT * NH)
                    a_sqrt(NT * NH)
                    U.open(act, "A")
                    act.wait_ge(ss_zero, 2)
                    with act.Fori(0, NG) as g:
                        pair = quad = 0
                        turned = 0
                        lv = -1
                        for n, (what, e) in enumerate(uses):
                            if what == "apply" and uses[n - 1][0] != "apply":
                                lv += 1
                                pair = quad = 0
                            if e != "A":
                                continue
                            U.wait_full(act, g, n)
                            src = PS[:, bank_of(n), :]
                            if what == "turn":
                                dst = TQ[:, (1, 2, 0)[turned], :, :]
                                src = tile4(src)
                                if turned == 2:
                                    for h in range(NH):
                                        hs = slice(DK * h, DK * h + DK)
                                        nc.scalar.activation(TZ[hs, 0, :, h, :], tile4(PS[hs, bank_of(n), :]),
                                                             ACT.Copy)
                                turned += 1
                            elif what == "square" and lv < LEVELS - 2:
                                dst = PW[(lv + 1) % 2][:, 2 * pairs[pair]:2 * pairs[pair] + 2, :, :]
                                src = src.rearrange("p (u k c) -> p u k c", u=2, k=2)
                                pair += 1
                            elif what == "square":
                                dst = PW[(lv + 1) % 2][:, 4 * quad:4 * quad + 4, 1, :]
                                src = tile4(src)
                                quad += 1
                            else:
                                dst = W1T[:, :, :]
                                src = PS[:, bank_of(n), 0:256].rearrange("p (b c) -> p b c", b=2)
                            nc.scalar.activation(dst, src, ACT.Copy).then_inc(a2_act, 1)

                @block.vector
                def _(dve):
                    heads = lambda ap: ap.rearrange("p t (h d) -> p (t h) d", h=NH)
                    for src, dst in ((QTK, RQ), (KTK, RK)):
                        V.link(nc.vector.tensor_tensor(NRM[:, :, :], src[:, :, :], src[:, :, :], ALU.mult))
                        V.link(nc.vector.tensor_reduce(RKB[:, :], heads(NRM[:, :, :]), AX.X, ALU.add))
                        v_ask(nc.vector.tensor_scalar(SQA[:, :NT * NH], RKB[:, :], 1e-6, None, ALU.add))
                        v_sqrt(NT * NH)
                        V.link(nc.vector.reciprocal(dst[:, :], SQR[:, :NT * NH]))
                    V.link(nc.vector.tensor_tensor(RKB[:, :], RK[:, :], BETA[:, :, :].rearrange("p t h -> p (t h)"),
                                                   ALU.mult))
                    dve.wait_ge(ss_zero, 2)
                    per_chain = 17
                    U.open(dve, "V")
                    with dve.Fori(0, NG) as g:
                        V.enter(g, per_chain)
                        tiles = bass.ds(g * 4, 4)
                        gh = bass.ds(g * 16, 16)
                        four = lambda ap: ap.rearrange("p (t h) d -> p t h d", t=4)
                        sc = lambda r: r[:, gh].unsqueeze(2).to_broadcast([P, 16, DK])
                        h4 = lambda ap: ap.rearrange("p t (h d) -> p (t h) d", h=NH)
                        hy = lambda k: Y[:, :, k, :].rearrange("p t (h d) -> p t h d", h=NH)
                        sc4 = lambda r: r.rearrange("p (t h) -> p t h", t=4).unsqueeze(3).to_broadcast([P, 4, NH, DK])
                        nc.vector.tensor_tensor(h4(KH[:, :, :]), h4(KTK[:, tiles, :]), sc(RK), ALU.mult)\
                            .then_inc(a2_prep, 1)
                        nc.vector.tensor_tensor(hy(1), KTK[:, tiles, :].rearrange("p t (h d) -> p t h d", h=NH),
                                                sc4(RKB[:, gh]), ALU.mult).then_inc(a2_prep, 1)
                        nc.vector.tensor_tensor(h4(QH[:, :, :]), h4(QTK[:, tiles, :]), sc(RQ), ALU.mult)\
                            .then_inc(a2_prep, 1)
                        nc.vector.tensor_tensor(hy(0), VTK[:, tiles, :].rearrange("p t (h d) -> p t h d", h=NH),
                                                BETA[:, tiles, :].unsqueeze(3).to_broadcast([P, 4, NH, DK]),
                                                ALU.mult).then_inc(a2_prep, 1)
                        for s_ in (1, 2):
                            U.wait_taken(dve, g, s_ - 1)
                            for h in range(NH):
                                hs = slice(DK * h, DK * h + DK)
                                last = nc.vector.tensor_copy(TZ[hs, s_, :, h, :], TQ[hs, s_, :, :])
                            last.then_inc(a2_zeros, 1)
                        taps_done = []

                        def tap(acc, filt, base, k):
                            ins = nc.vector.scalar_tensor_tensor(
                                out=acc[:, :, :], in0=VPT[:, :, bass.ds(k + base, L)],
                                scalar=pa(filt)[:, bass.ds(k, 1)], in1=acc[:, :, :], op0=ALU.mult, op1=ALU.add)
                            taps_done.append(V.mark(ins))

                        def long_tap():
                            k = len(taps_done) - 1
                            if k >= 2:
                                dve.wait_ge(dve_step, taps_done[-2])
                            tap((FL0, FL1)[k % 2], "firl", 0, g * 16 + k)

                        dve.wait_ge(dve_step, g * per_chain + V.done)
                        tap(FS, "firs", PAD - FIRS, g)
                        long_tap()
                        long_tap()
                        masks, lv = 0, 0
                        for n, (what, e) in enumerate(uses):
                            if e != "V":
                                continue
                            U.wait_full(dve, g, n)
                            src = PS[:, bank_of(n), :]
                            if what == "mask":
                                kind, t = divmod(masks, 4)
                                dst = (PW[0][:, t:16:4, 0, :], PW[0][:, t:16:4, 1, :], AT[:, t:16:4, :])[kind]
                                nc.vector.tensor_tensor(dst, tile4(src), rows(pa(("low", "upp", "incl")[kind]), 4),
                                                        ALU.mult).then_inc(a2_dve, 1)
                                masks += 1
                            elif what == "apply":
                                half = lv % 2
                                yy = Y[:, 2 * half:2 * half + 2, :, :].rearrange("p t k c -> p (t k c)")
                                nc.vector.tensor_tensor(yy, yy, src, ALU.add).then_inc(a2_dve, 1)
                                lv += 1
                                if half:
                                    for _ in range(TAPS_AFTER[lv // 2 - 1]):
                                        long_tap()
                            elif what == "state":
                                for h in range(NH):
                                    hs = slice(DK * h, DK * h + DK)
                                    last = nc.vector.tensor_copy(SS[hs, :, hs], PS[hs, bank_of(n), 0:2 * DK].rearrange(
                                        "p (b c) -> p b c", b=2))
                                last.then_inc(a2_dve, 1)
                            elif what == "ws":
                                yy = Y[:, 1:4:2, 0, :]
                                nc.vector.tensor_tensor(yy, yy, PS[:, bank_of(n), 0:256].rearrange(
                                    "p (b c) -> p b c", b=2), ALU.subtract).then_inc(a2_dve, 1)
                            else:
                                nc.vector.tensor_copy(DEL[:, tiles, :], tile4(src)).then_inc(a2_dve, 1)
                        assert len(taps_done) == 17
                        V.leave(NG)

        s3 = ExitStack()
        with s3:
            STK = QTK
            LTK = KTK
            SF = sbuf(s3, "SF", [P, NT, NH, DK])
            GH = sbuf(s3, "GH", [P, NH, 512])
            LG = sbuf(s3, "LG", [P, 4, 16])
            TMP = sbuf(s3, "TMP", [P, NT, D])
            SM = sbuf(s3, "SM", [P, 6, 64])
            GC = sbuf(s3, "GC", [P, 4, 16])
            WO = sbuf(s3, "WO", [P, D])
            long_ready, sf_zero, gate_const = sem("long_ready"), sem("sf_zero"), sem("gate_const")
            a3_hid, a3_gelu, a3_log, a3_lg = sem("a3_hid"), sem("a3_gelu"), sem("a3_log"), sem("a3_lg")
            a3_need, a3_exp, wo_ready, a3_out, src_ready = (sem("a3_need"), sem("a3_exp"), sem("wo_ready"),
                                                            sem("a3_out"), sem("src_ready"))
            with nc.Block() as block:
                @block.sync
                def _(sp):
                    sp.dma_start(PB[:, :], pb_in).then_inc(loadB, 16)

                @block.gpsimd
                def _(pool):
                    nc.gpsimd.memset(SF[:, :, :, 16:32], 0.0).then_inc(sf_zero, 1)

                @block.tensor
                def _(pe):
                    p_transpose(lambda t: FS[:, t // 2, (t % 2) * P:(t % 2 + 1) * P], ready=False)
                    pe.wait_ge(long_ready, 1)
                    p_transpose(lambda t: FL0[:, t // 2, (t % 2) * P:(t % 2 + 1) * P], (4, 5, 6, 7), ready=False)
                    p_copied()
                    pe.wait_ge(sf_zero, 1)
                    p_transpose(lambda t: SF[:, t, :, :].rearrange("p h s -> p (h s)"))
                    p_copied()
                    pe.sem_inc(a3_log, 1)
                    with pe.Fori(0, NG) as g:
                        for h in range(NH):
                            nc.tensor.matmul(PS[:, h, :].rearrange("p (b l) -> p b l", b=2), pa("gw1h"),
                                             XT[:, bass.ds(g * 2, 2), 3:3 + L], start=True, stop=False)
                            nc.tensor.matmul(PS[:, h, :], pa("gw1s")[:, h * P:(h + 1) * P],
                                             TR[:, bass.ds(g * 512, 512)], start=False, stop=True)\
                                .then_inc(a3_hid, 1)
                        pe.wait_ge(a3_lg, g + 1)
                        for h in range(NH):
                            pe.wait_ge(a3_gelu, g * NH + (h + 1))
                            for t in range(4):
                                at = t * 16 + h * 4
                                last = nc.tensor.matmul(PS[:, 4, at:at + 4], GH[:, h, t * P:(t + 1) * P],
                                                        pa("gw2"), start=True, stop=True)
                        last.then_inc(a3_log, 1)
                    p_transpose(lambda t: TMP[:, t, :])
                    p_copied()
                    pe.wait_ge(wo_ready, 1)
                    for t in range(NT):
                        last = nc.tensor.matmul(PS[:, 4 + t // 4, (t % 4) * P:(t % 4 + 1) * P],
                                                TR[:, t * P:(t + 1) * P], WO[:, :], start=True, stop=True)
                        if t % 4 == 3:
                            last.then_inc(a3_out, 1)

                @block.scalar
                def _(act):
                    a_transposed(lambda j: STK[:, 4 * j:4 * j + 4, :].rearrange("p t c -> p (t c)"))
                    nc.scalar.activation(GC[:, 3, 0:4], pa("crl"), ACT.Sigmoid).then_inc(gate_const, 1)
                    nc.scalar.activation(GC[:, 1, :], pa("floor"), ACT.Sigmoid).then_inc(gate_const, 1)
                    nc.scalar.activation(GC[:, 0, :], pa("ltemp"), ACT.Exp, scale=-1.0).then_inc(gate_const, 1)
                    a_transposed(lambda j: LTK[:, 4 * j:4 * j + 4, :].rearrange("p t c -> p (t c)"), (4, 5, 6, 7))
                    a_sqrt(256)
                    a_transposed(lambda j: TR[:, j * 512:(j + 1) * 512])
                    with act.Fori(0, NG) as g:
                        act.wait_ge(a3_log, g + 1)
                        for h in range(NH):
                            act.wait_ge(a3_hid, g * NH + (h + 1))
                            nc.scalar.activation(GH[:, h, :], PS[:, h, :], ACT.Gelu, bias=pa("gb1"))\
                                .then_inc(a3_gelu, 1)
                        act.wait_ge(a3_need, g + 1)
                        nc.scalar.activation(LG[:, :, :], LG[:, :, :], ACT.Exp)\
                            .then_inc(a3_exp, 1)
                    a_sqrt(NT * NH)
                    a_transposed(lambda j: TR[:, j * 512:(j + 1) * 512])
                    a_sqrt(NT)

                @block.vector
                def _(dve):
                    flat = lambda ap: ap.rearrange("p t c -> p (t c)")
                    per_head = lambda ap: ap.rearrange("p t (h d) -> p (t h) d", h=NH)
                    nc.vector.tensor_tensor(FL0[:, :, :], FL0[:, :, :], FL1[:, :, :], ALU.add).then_inc(long_ready, 1)
                    nc.vector.tensor_scalar(WO[:, :], pa("wo"), pa("onw"), None, ALU.mult).then_inc(wo_ready, 1)
                    for s, src in ((3, VTK), (2, DEL), (0, STK), (1, LTK)):
                        if s == 0:
                            dve.wait_ge(tr_copied, 8)
                        if s == 1:
                            dve.wait_ge(tr_copied, 12)
                        stat = lambda k: SF[:, :, :, 4 * s + k].rearrange("p t h -> p (t h)")
                        nc.vector.tensor_reduce(SM[:, 0, :], per_head(src[:, :, :]), AX.X, ALU.add)
                        nc.vector.tensor_reduce(SM[:, 1, :], per_head(src[:, :, :]), AX.X, ALU.add,
                                                apply_absolute_value=True)
                        V.link(nc.vector.tensor_tensor(flat(TMP[:, :, :]), flat(src[:, :, :]), flat(src[:, :, :]),
                                                       ALU.mult))
                        V.link(nc.vector.tensor_reduce(SQA[:, s * 64:(s + 1) * 64], per_head(TMP[:, :, :]), AX.X,
                                                       ALU.add))
                        V.link(nc.vector.tensor_scalar(stat(0), SM[:, 0, :], 1.0 / DK, None, ALU.mult))
                        nc.vector.tensor_scalar(stat(2), SM[:, 1, :], 1.0 / DK, None, ALU.mult)
                        V.link(nc.vector.tensor_tensor(SM[:, 2, :], stat(0), stat(0), ALU.mult))
                        V.link(nc.vector.scalar_tensor_tensor(out=stat(1), in0=SQA[:, s * 64:(s + 1) * 64],
                                                              scalar=1.0 / DK, in1=SM[:, 2, :], op0=ALU.mult,
                                                              op1=ALU.subtract))
                    v_ask(nc.vector.tensor_scalar(SM[:, 3, 0:1], SM[:, 2, 0:1], 0.0, None, ALU.mult))
                    v_sqrt(256)
                    last = None
                    for s in range(4):
                        last = nc.vector.tensor_copy(SF[:, :, :, 4 * s + 3].rearrange("p t h -> p (t h)"),
                                                     SQR[:, s * 64:(s + 1) * 64])
                    v_ready(last)
                    dve.wait_ge(gate_const, 3)
                    V.link(nc.vector.tensor_scalar(GC[:, 1, :], GC[:, 1, :], FLOOR, None, ALU.mult))
                    V.link(nc.vector.tensor_reduce(GC[:, 2, 0:4], GC[:, 1, :].rearrange("p (h s) -> p h s", h=NH), AX.X,
                                                   ALU.add))
                    V.link(nc.vector.tensor_scalar(GC[:, 2, 0:4], GC[:, 2, 0:4], -1.0, 1.0, ALU.mult, ALU.add))
                    alpha_rows = pa("alpha").unsqueeze(1).unsqueeze(3).to_broadcast([P, NT, NH, DK])
                    V.link(nc.vector.tensor_tensor(ITK[:, :, :].rearrange("p t (h d) -> p t h d", h=NH),
                                                   ITK[:, :, :].rearrange("p t (h d) -> p t h d", h=NH), alpha_rows,
                                                   ALU.mult))
                    dve.sem_inc(a3_lg, 1)
                    with dve.Fori(0, NG) as g:
                        V.enter(g, 13)
                        tiles = bass.ds(g * 4, 4)
                        lg = LG[:, :, :]
                        quad = lg.rearrange("p t (h s) -> p (t h) s", h=NH)
                        small = lambda k: SM[:, k, 0:4 * NH]
                        dve.wait_ge(a3_log, g + 2)
                        nc.vector.tensor_tensor(lg, PS[:, 4, 0:64].rearrange("p (t c) -> p t c", t=4),
                                                rows(pa("gb2"), 4), ALU.add).then_inc(a3_lg, 1)
                        dve.wait_ge(a3_lg, g + 2)
                        V.link(nc.vector.tensor_tensor(lg, lg, rows(GC[:, 0, :], 4), ALU.mult))
                        V.link(nc.vector.tensor_reduce(small(0), quad, AX.X, ALU.max))
                        nc.vector.tensor_tensor(quad, quad, bcast(small(0), 4), ALU.subtract).then_inc(a3_need, 1)
                        dve.wait_ge(a3_exp, g + 1)
                        V.link(nc.vector.tensor_reduce(small(0), quad, AX.X, ALU.add))
                        V.link(nc.vector.reciprocal(small(1), small(0)))
                        by_head = small(1).rearrange("p (t h) -> p t h", t=4)
                        V.link(nc.vector.tensor_tensor(by_head, by_head, rows(GC[:, 2, 0:4], 4), ALU.mult))
                        V.link(nc.vector.tensor_tensor(quad, quad, bcast(small(1), 4), ALU.mult))
                        V.link(nc.vector.tensor_tensor(lg, lg, rows(GC[:, 1, :], 4), ALU.add))
                        first = LG[:, :, 0:16:4]
                        V.link(nc.vector.tensor_tensor(first, first, rows(GC[:, 3, 0:4], 4), ALU.add))
                        for s, src in enumerate((STK, LTK, DEL, VTK)):
                            last = nc.vector.tensor_tensor(per_head(src[:, tiles, :]), per_head(src[:, tiles, :]),
                                                           quad[:, :, s].unsqueeze(2).to_broadcast([P, 4 * NH, DK]),
                                                           ALU.mult)
                        V.link(last)
                        part = lambda src: flat(src[:, tiles, :])
                        nc.vector.tensor_tensor(part(STK), part(STK), part(LTK), ALU.add)
                        V.link(nc.vector.tensor_tensor(part(DEL), part(DEL), part(VTK), ALU.add))
                        V.link(nc.vector.tensor_tensor(part(STK), part(STK), part(DEL), ALU.add))
                        V.link(nc.vector.tensor_tensor(part(STK), part(STK), part(ITK), ALU.add))
                        V.link(nc.vector.tensor_tensor(part(TMP), part(STK), part(STK), ALU.mult))
                        V.leave(NG)
                    V.link(nc.vector.tensor_reduce(SM[:, 0, :], per_head(TMP[:, :, :]), AX.X, ALU.add))
                    v_ask(nc.vector.tensor_scalar(SQA[:, :64], SM[:, 0, :], 1.0 / DK, 1e-5, ALU.mult, ALU.add))
                    v_sqrt(64)
                    V.link(nc.vector.reciprocal(SM[:, 1, :], SQR[:, :64]))
                    v_ready(nc.vector.tensor_tensor(per_head(TMP[:, :, :]), per_head(STK[:, :, :]),
                                                    bcast(SM[:, 1, :], DK), ALU.mult))
                    dve.wait_ge(a3_out, 4)
                    V.link(v_norm(lambda t: PS[:, 4 + t // 4, (t % 4) * P:(t % 4 + 1) * P], lambda t: NRM[:, t, :]))
                    V.link(nc.vector.tensor_tensor(flat(X[:, :, :]), flat(X[:, :, :]), flat(NRM[:, :, :]), ALU.add))
        sa.close()

        PC = sbuf(ctx, "PC", [P, ncc])
        PD = PB[:, P:P + nd]
        WR = sbufr(ctx, "WR", [P, ndr])
        flat = lambda ap: ap.rearrange("p t c -> p (t c)")

        ident = pb("ident")

        def pc(name, rows_=P):
            at, width = oc[name]
            return PC[0:rows_, at:at + width]

        def pd(name):
            at, width = od[name]
            return PD[:, at:at + width]

        def pdr(name):
            at, width = od[name]
            return WR[:, at:at + width]

        def v_affine(dst, gain, shift):
            V.link(nc.vector.tensor_tensor(dst[:, :, :], dst[:, :, :], rows(gain, NT), ALU.mult))
            return nc.vector.tensor_tensor(dst[:, :, :], dst[:, :, :], rows(shift, NT), ALU.add)

        OB = sbuf(ctx, "OB", [P, NT, D])
        sb = ExitStack()
        with sb:
            SR = sbuf(sb, "SR", [P, 64])
            MS = sbuf(sb, "MS", [P, NT, E])
            LE = sbuf(sb, "LE", [P, NT, E])
            W1H, W1L = (sbufr(sb, n, [P, E * DF]) for n in ("W1H", "W1L"))
            sba = sb.enter_context(ExitStack())
            MT = sbuf(sba, "MT", [E, NT * P])
            QKV = sbuf(sba, "QKV", [P, NT, 384])
            PR = sbuf(sba, "PR", [P, 64, DK])
            PRP = sbuf(sba, "PRP", [P, 2, 64, DK])
            SC = sbuf(sba, "SC", [P, 2, NH, B, B])
            products, summed, b_probs, w1_split = sem("products"), sem("summed"), sem("b_probs"), sem("w1_split")
            STEPS = [(f, h) for f in range(2) for h in range(NH)]
            part = lambda f, h, k: QKV[:, f:NT:2, k * D + h * DK:k * D + (h + 1) * DK]

            def score_products(eng, f, h, buf):
                q = part(f, h, 0).unsqueeze(2).to_broadcast([P, B, B, DK])
                k = part(f, h, 1).unsqueeze(1).to_broadcast([P, B, B, DK])
                return eng.tensor_tensor(buf.rearrange("p (a b) d -> p a b d", a=B), q, k, ALU.mult)

            def by_batch(buf):
                return buf.rearrange("p (a x) (y b) -> p a (x y) b", a=B, b=B)

            def value_products(eng, f, h, buf):
                a = SC[:, f, h, :, :].unsqueeze(2).to_broadcast([P, B, DK, B])
                v = part(f, h, 2).rearrange("p b d -> p d b").unsqueeze(1).to_broadcast([P, B, DK, B])
                return eng.tensor_tensor(by_batch(buf), a, v, ALU.mult)

            b_qkv, b_qkv_out, b_exp_need, b_exp, b_wo, b_logit, b_bias = (
                sem("b_qkv"), sem("b_qkv_out"), sem("b_exp_need"), sem("b_exp"), sem("b_wo"), sem("b_logit"),
                sem("b_bias"))
            moe_full, moe_act, moe_dve = sem("moe_full"), sem("moe_act"), sem("moe_dve")
            copied0 = count["tr_p"]
            with nc.Block() as block:
                @block.sync
                def _(sp):
                    sp.dma_start(PC[:, :], pc_in).then_inc(loadC, 16)

                @block.gpsimd
                def _(pool):
                    pool.wait_ge(loadB, 16)
                    for e in range(E):
                        cols = slice(e * DF, (e + 1) * DF)
                        G.link(nc.gpsimd.tensor_copy(W1H[:, cols], pb("w1")[:, cols]))
                        nc.gpsimd.tensor_tensor(W1L[:, cols], pb("w1")[:, cols], W1H[:, cols], ALU.subtract)\
                            .then_inc(w1_split, 1)
                    done = 0
                    for stage in range(2):
                        if stage == 0:
                            pool.wait_ge(b_qkv_out, NT)
                        else:
                            pool.wait_ge(b_probs, 1)
                        for f, h in STEPS[1::2]:
                            if done >= 2:
                                pool.wait_ge(summed, done - 1)
                            (score_products if stage == 0 else value_products)(
                                nc.gpsimd, f, h, PRP[:, done % 2, :, :]).then_inc(products, 1)
                            done += 1

                @block.tensor
                def _(pe):
                    pe.wait_ge(loadB, 16)
                    p_transpose(lambda t: NRM[:, t, :])
                    p_copied()
                    for t in range(NT):
                        if t >= 8:
                            pe.wait_ge(b_qkv_out, t - 7)
                        nc.tensor.matmul(PS[:, t % 8, 0:384], TR[:, t * P:(t + 1) * P], pb("wqkv"), start=True,
                                         stop=True).then_inc(b_qkv, 1)
                    pe.wait_ge(b_qkv_out, NT)
                    p_transpose(lambda t: OB[:, t, :])
                    p_copied()
                    for t in range(NT):
                        last = nc.tensor.matmul(PS[:, 4 + t // 4, (t % 4) * P:(t % 4 + 1) * P],
                                                TR[:, t * P:(t + 1) * P], pb("wo"), start=True, stop=True)
                    last.then_inc(b_wo, 1)
                    p_transpose(lambda t: NRM[:, t, :])
                    p_copied()
                    for t in range(NT):
                        last = nc.tensor.matmul(PS[:, 4, t * E:(t + 1) * E], TR[:, t * P:(t + 1) * P], pb("wg"),
                                                start=True, stop=True)
                    last.then_inc(b_logit, 1)
                    count["norm_p"] += 1
                    pe.wait_ge(norm_ready, count["norm_p"])
                    for j in range(4):
                        for t in range(4):
                            last = nc.tensor.transpose(PS[0:E, j, t * P:(t + 1) * P], MS[:, 4 * j + t, :], ident)
                        last.then_inc(tr_bank, 1)
                    count["tr_p"] += 4
                    p_copied()
                    for t in range(NT):
                        last = nc.tensor.matmul(PS[:, 4 + t // 4, (t % 4) * P:(t % 4 + 1) * P],
                                                MT[:, t * P:(t + 1) * P], pb("b2", E), start=True, stop=True)
                    last.then_inc(b_bias, 1)

                @block.scalar
                def _(act):
                    a_sqrt(NT)
                    a_transposed(lambda j: TR[:, j * 512:(j + 1) * 512])
                    act.wait_ge(b_exp_need, 1)
                    nc.scalar.activation(SC[:, :, :, :, :].rearrange("p f h q k -> p (f h q k)"),
                                         SC[:, :, :, :, :].rearrange("p f h q k -> p (f h q k)"), ACT.Exp)\
                        .then_inc(b_exp, 1)
                    a_transposed(lambda j: TR[:, j * 512:(j + 1) * 512])
                    a_sqrt(NT)
                    a_transposed(lambda j: TR[:, j * 512:(j + 1) * 512])
                    for j in range(4):
                        count["tr_a"] += 1
                        act.wait_ge(tr_bank, count["tr_a"])
                        nc.scalar.activation(MT[:, j * 512:(j + 1) * 512], PS[0:E, j, :], ACT.Copy)\
                            .then_inc(tr_copied, 1)

                @block.vector
                def _(dve):
                    dve.wait_ge(loadB, 16)
                    v_ready(v_norm(lambda t: X[:, t, :], lambda t: NRM[:, t, :]))
                    for t in range(NT):
                        dve.wait_ge(b_qkv, t + 1)
                        nc.vector.tensor_tensor(QKV[:, t, :], PS[:, t % 8, 0:384], pb("bqkv"), ALU.add)\
                            .then_inc(b_qkv_out, 1)
                    dve.wait_ge(b_qkv_out, NT)
                    done = 0
                    for n, (f, h) in enumerate(STEPS):
                        to = SC[:, f, h, :, :].rearrange("p q k -> p (q k)")
                        if n % 2 == 0:
                            V.link(score_products(nc.vector, f, h, PR[:, :, :]))
                            V.link(nc.vector.tensor_reduce(to, PR[:, :, :], AX.X, ALU.add))
                        else:
                            done += 1
                            dve.wait_ge(products, done)
                            nc.vector.tensor_reduce(to, PRP[:, (done - 1) % 2, :, :], AX.X, ALU.add)\
                                .then_inc(summed, 1)
                    dve.wait_ge(summed, done)
                    scores = SC[:, :, :, :, :].rearrange("p f h q k -> p (f h q) k")
                    V.link(nc.vector.tensor_scalar(scores, scores, 1.0 / math.sqrt(DK), None, ALU.mult))
                    V.link(nc.vector.tensor_reduce(SR[:, :], scores, AX.X, ALU.max))
                    nc.vector.tensor_tensor(scores, scores, bcast(SR[:, :], B), ALU.subtract).then_inc(b_exp_need, 1)
                    dve.wait_ge(b_exp, 1)
                    V.link(nc.vector.tensor_reduce(SR[:, :], scores, AX.X, ALU.add))
                    V.link(nc.vector.reciprocal(SR[:, :], SR[:, :]))
                    V.mark(nc.vector.tensor_tensor(scores, scores, bcast(SR[:, :], B), ALU.mult))
                    dve.wait_ge(dve_step, V.done)
                    dve.sem_inc(b_probs, 1)
                    for n, (f, h) in enumerate(STEPS):
                        to = OB[:, f:NT:2, h * DK:(h + 1) * DK]
                        if n % 2 == 0:
                            V.link(value_products(nc.vector, f, h, PR[:, :, :]))
                            V.link(nc.vector.tensor_reduce(to, by_batch(PR[:, :, :]), AX.X, ALU.add))
                        else:
                            done += 1
                            dve.wait_ge(products, done)
                            last = nc.vector.tensor_reduce(to, by_batch(PRP[:, (done - 1) % 2, :, :]), AX.X, ALU.add)
                            if n < len(STEPS) - 1:
                                last.then_inc(summed, 1)
                    v_ready(last)
                    dve.wait_ge(b_wo, 1)
                    V.link(nc.vector.tensor_tensor(NRM[:, :, :], NRM[:, :, :], rows(pb("bo"), NT), ALU.add))
                    for j in range(4):
                        last = nc.vector.tensor_tensor(NRM[:, 4 * j:4 * j + 4, :], NRM[:, 4 * j:4 * j + 4, :],
                                                       tile4(PS[:, 4 + j, :]), ALU.add)
                    V.link(last)
                    V.link(v_norm(lambda t: NRM[:, t, :], lambda t: NRM[:, t, :]))
                    v_ready(v_affine(NRM, pb("g1"), pb("be1")))
                    dve.wait_ge(b_logit, 1)
                    V.link(nc.vector.tensor_copy(LE[:, :, :], PS[:, 4, 0:NT * E].rearrange("p (t e) -> p t e", t=NT)))
                    V.link(nc.vector.tensor_reduce(SR[:, 0:NT], LE[:, :, :], AX.X, ALU.max))
                    V.link(nc.vector.tensor_tensor(LE[:, :, :], LE[:, :, :], bcast(SR[:, 0:NT], E), ALU.is_equal))
                    V.link(nc.vector.tensor_tensor(LE[:, :, :], LE[:, :, :], rows(pb("iota"), NT), ALU.mult))
                    V.link(nc.vector.tensor_reduce(SR[:, 0:NT], LE[:, :, :], AX.X, ALU.min))
                    v_ready(nc.vector.tensor_tensor(MS[:, :, :], rows(pb("iota"), NT), bcast(SR[:, 0:NT], E),
                                                    ALU.is_equal))
                    dve.wait_ge(b_bias, 1)
                    for j in range(4):
                        nc.vector.tensor_tensor(OB[:, 4 * j:4 * j + 4, :], NRM[:, 4 * j:4 * j + 4, :],
                                                tile4(PS[:, 4 + j, :]), ALU.add)

            sba.close()
            HID = sbuf(sb, "HID", [P, 2, 4, 512])
            XBH, XBL = (sbufr(sb, n, [P, NT * P]) for n in ("XBH", "XBL"))
            xb_high, xb_low = sem("xb_high"), sem("xb_low")
            engines, order = [], []
            for e in range(E + 1):
                if e < E:
                    order += [("up", e, c) for c in range(4)]
                if e >= 1:
                    order.append(("down", e - 1, 0))
            engines = ["A" if k == "up" else "V" for k, _, _ in order]
            U = Uses(moe_full, {"A": moe_act, "V": moe_dve}, engines)
            where = {k: n for n, k in enumerate(order)}
            m_asked, m_given = sem("m_asked"), sem("m_given")
            NORMS = 4

            def turns(eng, turn):
                turn(0, None)
                with eng.Fori(0, NG - 1) as i:
                    turn(i + 1, i)

            with nc.Block() as block:
                @block.tensor
                def _(pe):
                    U.open_full(pe)
                    pe.wait_ge(w1_split, E)
                    pe.wait_ge(xb_low, 4)
                    with pe.Fori(0, NG) as g:
                        U.wait_start(pe, g)
                        for n, (kind, e, c) in enumerate(order):
                            U.wait_empty(pe, g, n)
                            if kind == "up":
                                at = e * DF + c * P
                                for m, (w, x_) in enumerate(((W1H, XBH), (W1H, XBL), (W1L, XBH))):
                                    last = nc.tensor.matmul(PS[:, n % 8, :], w[:, at:at + P],
                                                            x_[:, bass.ds(g * 512, 512)], start=(m == 0),
                                                            stop=(m == 2))
                            else:
                                U.wait_taken(pe, g, where[("up", e, 3)])
                                for t in range(4):
                                    for k in range(4):
                                        last = nc.tensor.matmul(PS[:, n % 8, t * P:(t + 1) * P],
                                                                HID[:, e % 2, k, t * P:(t + 1) * P],
                                                                pb("w2")[:, (4 * e + k) * P:(4 * e + k + 1) * P],
                                                                start=(k == 0), stop=(k == 3))
                            last.then_inc(moe_full, 1)

                @block.scalar
                def _(act):
                    def root(before, k):
                        act.wait_ge(m_asked, before * NORMS + (k + 1))
                        nc.scalar.activation(SQR[:, 0:4], SQA[:, 0:4], ACT.Sqrt).then_inc(m_given, 1)

                    def turn(g, before):
                        for n, (kind, e, c) in enumerate(order):
                            if kind == "up":
                                if e >= 2:
                                    U.wait_full(act, g, where[("down", e - 2, 0)])
                                U.wait_full(act, g, n)
                                at = 4 * e + c
                                nc.scalar.activation(HID[:, e % 2, c, :], PS[:, n % 8, :], ACT.Relu,
                                                     bias=pb("b1")[:, at:at + 1]).then_inc(moe_act, 1)
                                if before is not None and c == 3 and 0 <= e - 2 < NORMS:
                                    root(before, e - 2)

                    U.open(act, "A")
                    for j in range(4):
                        cols = slice(j * 512, (j + 1) * 512)
                        nc.scalar.activation(XBH[:, cols], TR[:, cols], ACT.Copy).then_inc(xb_high, 1)
                    turns(act, turn)
                    for k in range(NORMS):
                        root(NG - 1, k)

                @block.vector
                def _(dve):
                    def take_wait():
                        nc.vector.tensor_copy(RS[:, 8:9], pb("iota")[:, 0:1])

                    def begin(before, k):
                        src = (OB, NRM, X, OB)[k][:, bass.ds(before * 4, 4), :]
                        take_wait()
                        for t in range(4):
                            last = nc.vector.bn_stats(STAT[:, t, :], src[:, t, :])
                        V.link(last)
                        take_wait()
                        for t in range(4):
                            last = nc.vector.bn_aggr(MV[:, t, :], STAT[:, t, :])
                        V.link(last)
                        nc.vector.tensor_scalar(SQA[:, 0:4], MV[:, 0:4, 1], 1e-5, None, ALU.add).then_inc(m_asked, 1)

                    def end(before, k):
                        tiles = bass.ds(before * 4, 4)
                        src, dst = ((OB, NRM), (NRM, NRM), (X, OB), (OB, NRM))[k]
                        src, dst, x_ = src[:, tiles, :], dst[:, tiles, :], X[:, tiles, :]
                        dve.wait_ge(m_given, before * NORMS + (k + 1))
                        V.link(nc.vector.reciprocal(RS[:, 0:4], SQR[:, 0:4]))
                        for t in range(4):
                            last = nc.vector.tensor_scalar(dst[:, t, :], src[:, t, :], MV[:, t, 0:1], RS[:, t:t + 1],
                                                           ALU.subtract, ALU.mult)
                        V.link(last)
                        if k == 1:
                            V.link(nc.vector.tensor_tensor(x_, x_, dst, ALU.add))
                        elif k != 2:
                            gain, shift = (pb("g2"), pb("be2")) if k == 0 else (pc("g1"), pc("b1"))
                            V.link(nc.vector.tensor_tensor(dst, dst, rows(gain, 4), ALU.mult))
                            V.link(nc.vector.tensor_tensor(dst, dst, rows(shift, 4), ALU.add))

                    def post(before, step):
                        if step > 0:
                            end(before, step - 1)
                        if step < NORMS:
                            begin(before, step)

                    LINKS = 2 * NORMS + 2 * NORMS + 1 + 2 * 2

                    def turn(g, before):
                        if before is not None:
                            V.enter(before, LINKS)
                        for n, (kind, e, c) in enumerate(order):
                            if kind == "down":
                                U.wait_full(dve, g, n)
                                if e:
                                    U.wait_taken(dve, g, where[("down", e - 1, 0)])
                                for t in range(4):
                                    acc = OB[:, bass.ds(g * 4 + t, 1), :].rearrange("p t c -> p (t c)")
                                    last = nc.vector.scalar_tensor_tensor(
                                        out=acc, in0=PS[:, n % 8, t * P:(t + 1) * P],
                                        scalar=MS[:, bass.ds(g * 4 + t, 1), e], in1=acc, op0=ALU.mult, op1=ALU.add)
                                last.then_inc(moe_dve, 1)
                                if before is not None and e <= NORMS:
                                    post(before, e)
                        if before is not None:
                            V.leave(NG - 1)

                    U.open(dve, "V")
                    dve.wait_ge(loadC, 16)
                    for j in range(4):
                        cols = slice(j * 512, (j + 1) * 512)
                        dve.wait_ge(xb_high, j + 1)
                        nc.vector.tensor_tensor(XBL[:, cols], TR[:, cols], XBH[:, cols], ALU.subtract)\
                            .then_inc(xb_low, 1)
                    turns(dve, turn)
                    U.wait_taken(dve, NG - 1, where[("down", E - 1, 0)])
                    for step in range(NORMS + 1):
                        post(NG - 1, step)

        sc_ = ExitStack()
        with sc_:
            XL = OB
            VXT = sbuf(sc_, "VXT", [P, NT, VX])
            CT = sbuf(sc_, "CT", [P, NT, H2])
            BD = sbuf(sc_, "BD", [P, 4, H2])
            WEF = sbuf(sc_, "WEF", [P, H2])
            CRW = sbuf(sc_, "CRW", [P, H2])
            OC = sbuf(sc_, "OC", [P, NT, D])
            s5 = sc_.enter_context(ExitStack())
            BS = sbuf(s5, "BS", [P, 4, 4])
            QK = [sbufr(s5, f"QK{n}", [P, 2, 4, L]) for n in range(2)]
            HI = sbufr(s5, "HI", [P, 4, 2, L])
            LO = sbuf(s5, "LO", [P, 4, 2, L])
            MX = sbuf(s5, "MX", [P, 2, H2])
            MH = sbufr(s5, "MH", [P, 2, H2])
            M4 = sbuf(s5, "M4", [P, 2, 4, 2, H2])
            MR = [sbufr(s5, f"MR{n}", [P, L]) for n in range(2)]
            SEL = sbufr(s5, "SEL", [P, H2])
            PT = sbuf(s5, "PT", [P, 4, 2, L])
            UB = [sbuf(s5, f"UB{n}", [P, H2, 2, VX]) for n in range(2)]
            CM = sbuf(s5, "CM", [P, 2 * H2, R2])
            RI = sbuf(s5, "RI", [P, 3, 2 * H2])
            UP = sbuf(s5, "UP", [P, 2 * H2, HD2, R2])
            c_zero, c_bd, c_w, c_wef, c_v, c_vout, c_ct = (sem("c_zero"), sem("c_bd"), sem("c_w"), sem("c_wef"),
                                                           sem("c_v"), sem("c_vout"), sem("c_ct"))
            with nc.Block() as block:
                @block.sync
                def _(sp):
                    sp.dma_start(PD, pd_in).then_inc(loadD, 16)

                @block.gpsimd
                def _(pool):
                    nc.gpsimd.memset(BD[:, :, :], 0.0).then_inc(c_zero, 1)
                    nc.gpsimd.memset(VXT[:, :, VX - 1:VX], 1.0).then_inc(c_zero, 1)

                @block.tensor
                def _(pe):
                    pe.wait_ge(c_bd, 1)
                    for c in range(4):
                        nc.tensor.matmul(PS[:, 6, 0:H2], pc("wqv")[:, c * P:(c + 1) * P], BD[:, c, :],
                                         start=(c == 0), stop=(c == 3))
                    for c in range(4):
                        last = nc.tensor.matmul(PS[:, 7, 0:H2], pc("bqv")[:, c:c + 1].to_broadcast([P, P]),
                                                BD[:, c, :], start=(c == 0), stop=(c == 3))
                    last.then_inc(c_w, 1)
                    p_transpose(lambda t: NRM[:, t, :], ready=False)
                    p_copied()
                    for t in range(NT):
                        last = nc.tensor.matmul(PS[:, 4 + t // 8, (t % 8) * 64:(t % 8 + 1) * 64],
                                                TR[:, t * P:(t + 1) * P], pc("wv"), start=True, stop=True)
                    last.then_inc(c_v, 1)
                    pe.wait_ge(c_wef, 1)
                    for t in range(NT):
                        last = nc.tensor.matmul(PS[:, 6, t * H2:(t + 1) * H2], TR[:, t * P:(t + 1) * P], WEF[:, :],
                                                start=True, stop=True)
                    last.then_inc(c_ct, 1)

                @block.scalar
                def _(act):
                    a_transposed(lambda j: TR[:, j * 512:(j + 1) * 512])

                @block.vector
                def _(dve):
                    dve.wait_ge(loadC, 16)
                    dve.wait_ge(c_zero, 1)
                    for c in range(4):
                        last = nc.vector.tensor_scalar(BD[:, c, 4 * c:4 * c + 4], pc("mask4"), pc("wsq"), None,
                                                       ALU.mult)
                    last.then_inc(c_bd, 1)
                    V.link(nc.vector.tensor_scalar(BS[:, 0, :], pc("bq"), 1.0 / math.sqrt(HD2), None, ALU.mult))
                    nc.vector.tensor_scalar(BS[:, 1, :], BS[:, 0, :], pc("signs")[:, 0:1], None, ALU.mult)
                    nc.vector.tensor_scalar(BS[:, 2, :], pc("bk"), pc("signs")[:, 2:3], None, ALU.mult)
                    nc.vector.tensor_scalar(BS[:, 3, 0:1], pc("signs")[:, 0:1], 1.0 / math.sqrt(HD2), None, ALU.mult)
                    nc.vector.tensor_copy(SEL[:, :], pc("sel"))
                    dve.wait_ge(c_w, 1)
                    nc.vector.tensor_scalar(CRW[:, :], PS[:, 7, 0:H2], 1.0 / math.sqrt(QK2), pc("bs"), ALU.mult,
                                            ALU.add)
                    nc.vector.tensor_scalar(WEF[:, :], PS[:, 6, 0:H2], 1.0 / math.sqrt(QK2), None, ALU.mult)\
                        .then_inc(c_wef, 1)
                    dve.wait_ge(c_v, 1)
                    for j in range(2):
                        last = nc.vector.tensor_tensor(VXT[:, 8 * j:8 * j + 8, 0:64],
                                                       PS[:, 4 + j, :].rearrange("p (t c) -> p t c", t=8),
                                                       rows(pc("bv"), 8), ALU.add)
                    V.link(last)
                    prod = UP[:, :, :, :].rearrange("p a b c -> p (a b c)")[:, 0:NT * 64]
                    V.link(nc.vector.tensor_tensor(prod.rearrange("p (t r d) -> p t r d", t=NT, r=R2),
                                                   VXT[:, :, 0:64].rearrange("p t (r d) -> p t r d", r=R2),
                                                   pc("wso").unsqueeze(1).unsqueeze(1).to_broadcast([P, NT, R2, HD2]),
                                                   ALU.mult))
                    nc.vector.tensor_reduce(VXT[:, :, 64:72], prod.rearrange("p (t r d) -> p t r d", t=NT, r=R2), AX.X,
                                            ALU.add)
                    dve.wait_ge(c_ct, 1)
                    V.link(nc.vector.tensor_tensor(CT[:, :, :], PS[:, 6, 0:NT * H2].rearrange("p (t h) -> p t h", t=NT),
                                                   rows(CRW[:, :], NT), ALU.add))

            prep = [("q", 0), ("k", 0), ("q", 1), ("max", 0), ("max", 1), ("k", 1)]
            prep += [("max", h) for h in range(2, H2)] + [("turn", 0)]
            LAG = 2
            main = []
            for h in range(H2 + LAG):
                if h < H2:
                    main.append(("exp", h))
                if h >= LAG and h % 2:
                    main.append(("out", (h - LAG) // 2))
            spread = [2, 0, 0, 1] + [1] * 17 + [0, 0, 1, 0]
            finish = {2: ("start", 0), 9: ("end", 0), 12: ("weigh", 0), 13: ("weigh", 1), 14: ("sum", 0), 16: ("sum", 1)}
            merged, todo = [], [("p",) + u for u in prep]
            for k, n in enumerate(spread):
                if k:
                    merged.append(("m",) + main[k - 1])
                if k in finish:
                    merged.append(("f",) + finish[k])
                merged += todo[:n]
                todo = todo[n:]
            assert not todo and len(spread) == len(main) + 1
            c_full, c_act = sem("c_full"), sem("c_act")
            p_full, p_act, p_dve = sem("p_full"), sem("p_act"), sem("p_dve")
            c_split, c_e_need, c_e, c_done = sem("c_split"), sem("c_e_need"), sem("c_e"), sem("c_done")
            UP_ = Uses(p_full, {"A": p_act, "V": p_dve}, ["A" if k in "qk" else "V" for k, _ in prep] + [None] * (-len(prep) % 4), 0, 4)
            UM = Uses(c_full, {"A": c_act}, ["A" for _ in main], 4, 4)
            c_own, c_mh, c_m4 = sem("c_own"), sem("c_mh"), sem("c_m4")
            at_p = {k: n for n, k in enumerate(prep)}
            at_m = {k: n for n, k in enumerate(main)}

            def batches(eng, step):
                for u in prep:
                    step(("p",) + u, 0, 0)

                def turn(b, odd, first=False, last=False):
                    for kind, *u in merged:
                        if kind == "m":
                            step(("m", *u), b, odd)
                        elif kind == "f" and not first:
                            step(("f", *u), b - 1, 1 - odd)
                        elif kind == "p" and not last:
                            step(("p", *u), b + 1, 1 - odd)

                turn(0, 0, first=True)
                with eng.Fori(0, (B - 2) // 2) as i:
                    turn(i * 2 + 1, 1)
                    turn(i * 2 + 2, 0)
                turn(B - 1, 1, last=True)
                for u in finish.values():
                    step(("f",) + u, B - 1, 1)

            def wait_split(eng, b, s_, back=0):
                eng.wait_ge(c_split, b * 4 + (4 * (1 - back) + s_ + 1))

            with nc.Block() as block:
                @block.tensor
                def _(pe):
                    def step(what, b, odd):
                        group, kind, k = what
                        q, kk = QK[odd][:, 0, :, :], QK[odd][:, 1, :, :]
                        if group == "f":
                            return
                        U, at = (UP_, at_p) if group == "p" else (UM, at_m)
                        n = at[(kind, k)]
                        bank = PS[:, U.bank(n), :]
                        U.wait_empty(pe, b, n)
                        if kind in "qk":
                            w = pc("wq" if kind == "q" else "wk")
                            for t in (2 * k, 2 * k + 1):
                                last = nc.tensor.matmul(bank[:, (t % 2) * L:(t % 2 + 1) * L], w[:, t * P:(t + 1) * P],
                                                        TR[:, bass.ds(b * L, L)], start=True, stop=True)
                        elif kind == "max":
                            hs = slice(32 * (k % 4), 32 * (k % 4) + 32)
                            wait_split(pe, b, 2 * (k // 8) + 1)
                            for f in range(2):
                                last = nc.tensor.matmul(bank[:, f * L:(f + 1) * L], q[hs, k // 4, f * P:(f + 1) * P],
                                                        kk[hs, k // 4, :], start=True, stop=True)
                        elif kind == "turn":
                            pe.wait_ge(c_m4, b + 1)
                            for f in range(2):
                                last = nc.tensor.transpose(bank[:, f * P:(f + 1) * P],
                                                           M4[:, f, :, :, :].rearrange("p r a h -> p (r a h)"), ident)
                        elif kind == "exp":
                            hs = slice(32 * (k % 4), 32 * (k % 4) + 32)
                            UP_.wait_taken(pe, b, at_p[("turn", 0)])
                            for c in range(2):
                                o = bank[:, c * L:(c + 1) * L]
                                nc.tensor.matmul(o, kk[hs, k // 4, c * P:(c + 1) * P], q[hs, k // 4, :], start=True,
                                                 stop=False)
                                last = nc.tensor.matmul(o, SEL[:, k:k + 1].to_broadcast([P, P]), MR[odd][:, :],
                                                        start=False, stop=True)
                        else:
                            UM.wait_taken(pe, b, at_m[("exp", 2 * k + 1)])
                            for h in (2 * k, 2 * k + 1):
                                for f in range(2):
                                    col = ((h % 2) * 2 + f) * VX
                                    for c in range(2):
                                        v = VXT[:, bass.ds(b * 2 + c, 1), :].rearrange("p t c -> p (t c)")
                                        last = nc.tensor.matmul(bank[:, col:col + VX],
                                                                PT[:, h % 4, c, f * P:(f + 1) * P], v,
                                                                start=(c == 0), stop=(c == 1))
                        last.then_inc(U.full, 1)

                    UP_.open_full(pe)
                    UM.open_full(pe)
                    batches(pe, step)

                @block.scalar
                def _(act):
                    def step(what, b, odd):
                        group, kind, k = what
                        if group == "f":
                            if kind == "end":
                                act.wait_ge(c_e_need, b + 1)
                                nc.scalar.activation(CM[:, :, :], CM[:, :, :], ACT.Exp).then_inc(c_e, 1)
                            return
                        U, at = (UP_, at_p) if group == "p" else (UM, at_m)
                        n = at[(kind, k)]
                        if U.at[n][0] != "A":
                            return
                        bank = PS[:, U.bank(n), :]
                        if kind in "qk":
                            s_ = 2 * k + (kind == "k")
                            wait_split(act, b, s_, back=1)
                            U.wait_full(act, b, n)
                            for t in (2 * k, 2 * k + 1):
                                src = bank[:, (t % 2) * L:(t % 2 + 1) * L]
                                bias, low, scale, lows = ((BS[:, 0, t:t + 1], BS[:, 1, t:t + 1], 1.0 / math.sqrt(HD2),
                                                           BS[:, 3, 0:1]) if kind == "q" else
                                                          (pc("bk")[:, t:t + 1], BS[:, 2, t:t + 1], 1.0,
                                                           pc("signs")[:, 2:3]))
                                nc.scalar.activation(HI[:, s_, t % 2, :], src, ACT.Identity, bias=bias, scale=scale)
                                last = nc.scalar.activation(LO[:, s_, t % 2, :], src, ACT.Identity, bias=low,
                                                            scale=lows)
                        elif kind == "exp":
                            if k >= 4:
                                U.wait_full(act, b, at_m[("out", (k - 4) // 2)])
                            else:
                                U.wait_full(act, b, at_m[("out", (k + 12) // 2)], back=1)
                            U.wait_full(act, b, n)
                            last = nc.scalar.activation(PT[:, k % 4, :, :], bank.rearrange("p (c q) -> p c q", c=2),
                                                        ACT.Exp)
                        else:
                            if k == 0:
                                act.wait_ge(c_done, b * 2 + 2)
                            U.wait_full(act, b, n)
                            last = nc.scalar.activation(UB[odd][:, 2 * k:2 * k + 2, :, :].rearrange(
                                "p h f c -> p (h f c)"), bank[:, 0:4 * VX], ACT.Copy)
                        last.then_inc(U.sems["A"], 1)

                    UP_.open(act, "A")
                    UM.open(act, "A")
                    batches(act, step)

                @block.vector
                def _(dve):
                    def own(b, k):
                        dve.wait_ge(c_own, b * OWN + k)

                    OWN = 10

                    def step(what, b, odd):
                        group, kind, k = what
                        if group == "f":
                            ub = UB[odd][:, :, :, :].rearrange("p h f c -> p (h f) c")
                            cm = CM[:, :, :]
                            if kind == "start":
                                UM.wait_taken(dve, b, at_m[("out", H2 // 2 - 1)])
                                nc.vector.reciprocal(RI[:, 0, :], ub[:, :, VX - 1]).then_inc(c_own, 1)
                                own(b, 1)
                                nc.vector.tensor_tensor(cm, ub[:, :, 64:72], bcast(RI[:, 0, :], R2), ALU.mult)\
                                    .then_inc(c_own, 1)
                                ct = CT[:, bass.ds(b * 2, 2), :].rearrange("p f h -> p h f").unsqueeze(3)\
                                    .to_broadcast([P, H2, 2, R2])
                                cm4 = cm.rearrange("p (h f) r -> p h f r", f=2)
                                own(b, 2)
                                nc.vector.tensor_tensor(cm4, cm4, ct, ALU.add).then_inc(c_own, 1)
                                own(b, 3)
                                nc.vector.tensor_reduce(RI[:, 1, :], cm, AX.X, ALU.max).then_inc(c_own, 1)
                                own(b, 4)
                                nc.vector.tensor_tensor(cm, cm, bcast(RI[:, 1, :], R2), ALU.subtract)\
                                    .then_inc(c_e_need, 1)
                            elif kind == "end":
                                dve.wait_ge(c_e, b + 1)
                                nc.vector.tensor_reduce(RI[:, 1, :], cm, AX.X, ALU.add).then_inc(c_own, 1)
                                own(b, 5)
                                nc.vector.reciprocal(RI[:, 1, :], RI[:, 1, :]).then_inc(c_own, 1)
                                own(b, 6)
                                nc.vector.tensor_tensor(RI[:, 1, :], RI[:, 1, :], RI[:, 0, :], ALU.mult)\
                                    .then_inc(c_own, 1)
                                own(b, 7)
                                nc.vector.tensor_tensor(cm, cm, bcast(RI[:, 1, :], R2), ALU.mult).then_inc(c_own, 1)
                            elif kind == "weigh":
                                own(b, 8)
                                half = slice(H2 * k, H2 * k + H2)
                                nc.vector.tensor_tensor(
                                    UP[:, half, :, :], ub[:, half, 0:64].rearrange("p a (r d) -> p a d r", r=R2),
                                    cm[:, half, :].unsqueeze(2).to_broadcast([P, H2, HD2, R2]),
                                    ALU.mult).then_inc(c_own, 1)
                            else:
                                own(b, 9 + k)
                                nc.vector.tensor_reduce(
                                    OC[:, bass.ds(b * 2, 2), 64 * k:64 * k + 64].rearrange(
                                        "p f (h d) -> p h f d", h=H2 // 2),
                                    UP[:, H2 * k:H2 * k + H2, :, :].rearrange("p (h f) d r -> p h f d r", f=2), AX.X,
                                    ALU.add).then_inc(c_done, 1)
                            return
                        if group == "m":
                            return
                        n = at_p[(kind, k)]
                        bank = PS[:, UP_.bank(n), :]
                        if kind in "qk":
                            UP_.wait_taken(dve, b, n)
                            s_ = 2 * k + (kind == "k")
                            sign = pc("signs")[:, 1:2] if kind == "q" else pc("signs")[:, 3:4]
                            nc.vector.scalar_tensor_tensor(out=QK[odd][:, s_ % 2, 2 * k:2 * k + 2, :],
                                                           in0=HI[:, s_, :, :], scalar=sign, in1=LO[:, s_, :, :],
                                                           op0=ALU.mult, op1=ALU.add).then_inc(c_split, 1)
                            return
                        UP_.wait_full(dve, b, n)
                        if kind == "max":
                            nc.vector.tensor_reduce(MX[:, :, k], bank.rearrange("p (f q) -> p f q", f=2), AX.X,
                                                    ALU.max, negate=True).then_inc(p_dve, 1)
                            if k == H2 - 1:
                                UP_.wait_taken(dve, b, n)
                                nc.vector.tensor_copy(MH[:, :, :], MX[:, :, :]).then_inc(c_mh, 1)
                                dve.wait_ge(c_mh, b + 1)
                                quad = lambda ap: ap.unsqueeze(2).to_broadcast([P, 2, 4, H2])
                                nc.vector.tensor_copy(M4[:, :, :, 0, :], quad(MH[:, :, :]))
                                nc.vector.tensor_tensor(M4[:, :, :, 1, :], quad(MX[:, :, :]), quad(MH[:, :, :]),
                                                        ALU.subtract).then_inc(c_m4, 1)
                        else:
                            nc.vector.tensor_copy(MR[odd][:, :], bank[:, 0:L]).then_inc(p_dve, 1)

                    UP_.open(dve, "V")
                    dve.sem_inc(c_split, 4)
                    dve.sem_inc(c_done, 4)
                    batches(dve, step)

            s5.close()
            HR = sbuf(sc_, "HR", [P, 2, NT * P])
            c_wf, c_hid, c_relu, c_ffn = sem("c_wf"), sem("c_hid"), sem("c_relu"), sem("c_ffn")
            d_weights = sem("d_weights")
            with nc.Block() as block:
                @block.gpsimd
                def _(pool):
                    pool.wait_ge(loadD, 16)
                    for name in ("w1", "w2", "h1", "h2", "w3"):
                        nc.gpsimd.tensor_copy(pdr(name), pd(name)).then_inc(d_weights, 1)

                @block.tensor
                def _(pe):
                    p_transpose(lambda t: OC[:, t, :], ready=False)
                    p_copied()
                    for t in range(NT):
                        last = nc.tensor.matmul(PS[:, 4 + t // 4, (t % 4) * P:(t % 4 + 1) * P],
                                                TR[:, t * P:(t + 1) * P], pc("wf"), start=True, stop=True)
                    last.then_inc(c_wf, 1)
                    p_transpose(lambda t: NRM[:, t, :])
                    p_copied()
                    for j in range(4):
                        for c in range(2):
                            n = 2 * j + c
                            nc.tensor.matmul(PS[:, n, :], pc("wr1")[:, c * P:(c + 1) * P],
                                             TR[:, j * 512:(j + 1) * 512], start=True, stop=True).then_inc(c_hid, 1)
                    for j in range(4):
                        pe.wait_ge(c_relu, 2 * j + 2)
                        for t in range(4 * j, 4 * j + 4):
                            for c in range(2):
                                last = nc.tensor.matmul(PS[:, j, (t % 4) * P:(t % 4 + 1) * P],
                                                        HR[:, c, t * P:(t + 1) * P], pc("wr2")[:, c * P:(c + 1) * P],
                                                        start=(c == 0), stop=(c == 1))
                        last.then_inc(c_ffn, 1)

                @block.scalar
                def _(act):
                    a_transposed(lambda j: TR[:, j * 512:(j + 1) * 512])
                    a_sqrt(NT)
                    a_transposed(lambda j: TR[:, j * 512:(j + 1) * 512])
                    for n in range(8):
                        act.wait_ge(c_hid, n + 1)
                        nc.scalar.activation(HR[:, n % 2, (n // 2) * 512:(n // 2 + 1) * 512], PS[:, n, :], ACT.Relu,
                                             bias=pc("br1")[:, n % 2:n % 2 + 1]).then_inc(c_relu, 1)
                    a_sqrt(NT)

                @block.vector
                def _(dve):
                    V.link(nc.vector.tensor_tensor(XL[:, :, :], XL[:, :, :], rows(pc("bf"), NT), ALU.add))
                    dve.wait_ge(c_wf, 1)
                    for j in range(4):
                        last = nc.vector.tensor_tensor(XL[:, 4 * j:4 * j + 4, :], XL[:, 4 * j:4 * j + 4, :],
                                                       tile4(PS[:, 4 + j, :]), ALU.add)
                    V.link(last)
                    V.link(v_norm(lambda t: XL[:, t, :], lambda t: NRM[:, t, :]))
                    v_ready(v_affine(NRM, pc("g2"), pc("b2")))
                    V.link(nc.vector.tensor_tensor(XL[:, :, :], XL[:, :, :], rows(pc("br2"), NT), ALU.add))
                    for j in range(4):
                        dve.wait_ge(c_ffn, j + 1)
                        last = nc.vector.tensor_tensor(XL[:, 4 * j:4 * j + 4, :], XL[:, 4 * j:4 * j + 4, :],
                                                       tile4(PS[:, j, :]), ALU.add)
                    V.link(last)
                    V.link(v_norm(lambda t: XL[:, t, :], lambda t: NRM[:, t, :]))
                    V.link(nc.vector.tensor_tensor(flat(X[:, :, :]), flat(X[:, :, :]), flat(NRM[:, :, :]), ALU.add))

        sd = ExitStack()
        with sd:
            XH, XLO = (sbufr(sd, n, [P, NT * P]) for n in ("XH", "XLO"))
            F = PB[:, P + nd:P + nd + 2 * 4 * 512].rearrange("p (s k c) -> p s k c", s=2, k=4)
            HAH, HAL, HBH, HBL = (sbufr(sd, n, [P, 2, 4, 512]) for n in ("HAH", "HAL", "HBH", "HBL"))
            YT = OB
            x_split = sem("x_split")
            with nc.Block() as block:
                @block.tensor
                def _(pe):
                    p_transpose(lambda t: NRM[:, t, :])

                @block.scalar
                def _(act):
                    a_sqrt(NT)
                    for j in range(4):
                        count["tr_a"] += 1
                        act.wait_ge(tr_bank, count["tr_a"])
                        cols = slice(j * 512, (j + 1) * 512)
                        nc.scalar.activation(XH[:, cols], PS[:, j, :], ACT.Copy)
                        nc.scalar.activation(TR[:, cols], PS[:, j, :], ACT.Copy).then_inc(tr_copied, 1)

                @block.vector
                def _(dve):
                    v_ready(v_norm(lambda t: X[:, t, :], lambda t: NRM[:, t, :]))
                    for j in range(4):
                        dve.wait_ge(tr_copied, count["tr_p"] - 3 + j)
                        cols = slice(j * 512, (j + 1) * 512)
                        nc.vector.tensor_tensor(XLO[:, cols], TR[:, cols], XH[:, cols], ALU.subtract)\
                            .then_inc(x_split, 1)

            d_full, d_act, d_dve, d_split = sem("d_full"), sem("d_act"), sem("d_dve"), sem("d_split")
            order = [(k, s_, c) for k in ("w1", "w2", "h1", "h2") for s_ in range(2) for c in range(4)]
            order += [("w3", s_, 0) for s_ in range(2)]
            U = Uses(d_full, {"A": d_act, "V": d_dve}, ["V" if k in ("w2", "w3") else "A" for k, _, _ in order])
            where = {k: n for n, k in enumerate(order)}
            splits = [k for k in order if k[0] in ("w2", "h1", "h2")]

            def wait_split(eng, g, use, back=0):
                eng.wait_ge(d_split, g * len(splits) + ((1 - back) * len(splits) + splits.index(use) + 1))

            with nc.Block() as block:
                @block.tensor
                def _(pe):
                    U.open_full(pe)
                    pe.wait_ge(d_weights, 5)
                    pe.wait_ge(x_split, 4)
                    with pe.Fori(0, NG // 2) as g:
                        U.wait_start(pe, g)
                        for n, (kind, s_, c) in enumerate(order):
                            bank = PS[:, n % 8, :]
                            U.wait_empty(pe, g, n)
                            if kind in ("w1", "w2"):
                                for m, src in enumerate((XH, XLO)):
                                    last = nc.tensor.matmul(bank, pdr(kind)[:, c * P:(c + 1) * P],
                                                            src[:, bass.ds(g * 1024 + s_ * 512, 512)],
                                                            start=(m == 0), stop=(m == 1))
                            elif kind in ("h1", "h2"):
                                parts, before = ((HBH, HBL), "w2") if kind == "h1" else ((HAH, HAL), "h1")
                                for k in range(4):
                                    if c == 0:
                                        wait_split(pe, g, (before, s_, k))
                                    at = k * DH + c * P
                                    for m, src in enumerate(parts):
                                        last = nc.tensor.matmul(bank, pdr(kind)[:, at:at + P], src[:, s_, k, :],
                                                                start=(k == 0 and m == 0), stop=(k == 3 and m == 1))
                            else:
                                wait_split(pe, g, ("h2", s_, 3))
                                for t in range(4):
                                    for k in range(4):
                                        for m, src in enumerate((HBH, HBL)):
                                            last = nc.tensor.matmul(bank[:, t * P:(t + 1) * P],
                                                                    src[:, s_, k, t * P:(t + 1) * P],
                                                                    pdr("w3")[:, k * P:(k + 1) * P],
                                                                    start=(k == 0 and m == 0),
                                                                    stop=(k == 3 and m == 1))
                            last.then_inc(d_full, 1)

                @block.scalar
                def _(act):
                    U.open(act, "A")
                    with act.Fori(0, NG // 2) as g:
                        for n, (kind, s_, c) in enumerate(order):
                            if kind in ("w2", "w3"):
                                continue
                            U.wait_full(act, g, n)
                            func, scale, high = {"w1": (ACT.Silu, "s1", None), "h1": (ACT.Gelu, "t1", HAH),
                                                 "h2": (ACT.Gelu, "t2", HBH)}[kind]
                            before = {"h1": "w2", "h2": "h1"}.get(kind)
                            if kind == "h2" and c == 0:
                                U.wait_full(act, g, where[("h1", s_, 3)])
                            if before:
                                wait_split(act, g, (before, s_, c))
                            else:
                                wait_split(act, g, ("h2", s_, c), back=1)
                            if high is not None:
                                nc.scalar.activation(high[:, s_, c, :], PS[:, n % 8, :], func,
                                                     scale=pd(scale)[:, c:c + 1])
                            nc.scalar.activation(F[:, s_, c, :], PS[:, n % 8, :], func,
                                                 scale=pd(scale)[:, c:c + 1]).then_inc(d_act, 1)

                @block.vector
                def _(dve):
                    U.open(dve, "V")
                    dve.sem_inc(d_split, len(splits))
                    with dve.Fori(0, NG // 2) as g:
                        for n, (kind, s_, c) in enumerate(order):
                            if kind == "w2":
                                U.wait_taken(dve, g, where[("w1", s_, c)])
                                U.wait_full(dve, g, n)
                                for dst in (HBH, F):
                                    last = nc.vector.scalar_tensor_tensor(
                                        out=dst[:, s_, c, :], in0=PS[:, n % 8, :], scalar=pd("s2")[:, c:c + 1],
                                        in1=F[:, s_, c, :], op0=ALU.mult, op1=ALU.mult)
                                last.then_inc(d_dve, 1)
                            elif kind == "w3":
                                U.wait_full(dve, g, n)
                                nc.vector.tensor_tensor(YT[:, bass.ds(g * 8 + s_ * 4, 4), :], tile4(PS[:, n % 8, :]),
                                                        rows(pd("s3"), 4), ALU.mult).then_inc(d_dve, 1)
                            if kind in ("w2", "h1", "h2"):
                                U.wait_taken(dve, g, n)
                                high, low = (HAH, HAL) if kind == "h1" else (HBH, HBL)
                                nc.vector.tensor_tensor(low[:, s_, c, :], F[:, s_, c, :], high[:, s_, c, :],
                                                        ALU.subtract).then_inc(d_split, 1)

            done, x_final = sem("stored"), sem("x_final")
            with nc.Block() as block:
                @block.scalar
                def _(act):
                    a_sqrt(NT)

                @block.vector
                def _(dve):
                    V.link(v_norm(lambda t: YT[:, t, :], lambda t: NRM[:, t, :]))
                    for j in range(2):
                        nc.vector.tensor_tensor(flat(X[:, 8 * j:8 * j + 8, :]), flat(X[:, 8 * j:8 * j + 8, :]),
                                                flat(NRM[:, 8 * j:8 * j + 8, :]), ALU.add).then_inc(x_final, 1)

                @block.sync
                def _(sp):
                    for j in range(2):
                        sp.wait_ge(x_final, j + 1)
                        sp.dma_start(out_dram[:, 8 * j:8 * j + 8, :], X[:, 8 * j:8 * j + 8, :]).then_inc(done, 16)
                    sp.wait_ge(done, 32)


def packed(pack, parts):
    out = np.zeros((P, offsets(pack)[1]), np.float32)
    for name, (at, width) in offsets(pack)[0].items():
        part = np.asarray(parts[name])
        assert part.shape[1] == width, (name, part.shape)
        out[:part.shape[0], at:at + width] = part
    return out


def every(v):
    v = np.asarray(v).reshape(1, -1)
    return np.broadcast_to(v, (P, v.shape[1]))


def column_chunks(v, n):
    return np.asarray(v).reshape(n, P).T


def row_chunks(w):
    n = w.shape[0] // P
    return w.reshape(n, P, -1).transpose(1, 0, 2).reshape(P, -1)


def layout(i):
    i = {k: np.asarray(v) for k, v in i.items()}
    a = {k[8:]: v for k, v in i.items() if k.startswith("L0_attn_")}
    f = {k[7:]: v for k, v in i.items() if k.startswith("L0_ffn_")}
    c = {k[8:]: v for k, v in i.items() if k.startswith("L1_attn_")}
    m = {k[7:]: v for k, v in i.items() if k.startswith("L1_ffn_")}
    r = np.arange(P)
    ident = np.eye(P, dtype=np.float32)
    later = (r[:, None] > r[None, :]).astype(np.float32)
    firs = np.zeros((P, 4), np.float32)
    firs[:, 1:] = a["firs"].reshape(P, FIRS)
    firl = np.zeros((P, 64), np.float32)
    firl[:, 1:] = a["firl"].reshape(P, FIRL)
    gw1s = np.zeros((NH, DK, NH, P), np.float32)
    for h in range(NH):
        gw1s[h, :16, h, :] = a["gW1"][D:D + 16]
    packs = {}
    packs["pa"] = packed(PACK_A, {
        "ident": ident, "low": -later, "upp": -later.T, "incl": 1 - later,
        "wqkv": np.concatenate([a["Wq"], a["Wk"], a["Wv"]], 1),
        "cwb": every(np.concatenate([a[k].T.reshape(-1) for k in ("cwq", "cwk", "cwv")])),
        "wid": a["Wid"], "wb": a["Wb"], "firs": firs, "firl": firl, "gw1h": a["gW1"][:D],
        "gw1s": gw1s.reshape(P, NH * P), "gb1": a["gb1"][:, None], "gw2": a["gW2"],
        "gb2": every(np.tile(a["gb2"], NH)), "ltemp": every(a["log_temp"]), "floor": every(a["floor_param"]),
        "crl": every(a["conv_res_logit"]), "alpha": every(a["alpha_id"]),
        "onw": np.tile(a["o_norm_w"], NH)[:, None], "wo": a["Wo"]})
    packs["pb"] = packed(PACK_B, {
        "ident": ident, "wqkv": f["Wqkv"].T, "bqkv": every(f["bqkv"]), "wo": f["Wo"].T, "bo": every(f["bo"]),
        "g1": every(f["g1"]), "be1": every(f["be1"]), "g2": every(f["g2"]), "be2": every(f["be2"]),
        "wg": f["Wg"].T, "w1": f["W1"].transpose(1, 0, 2).reshape(P, E * DF),
        "b1": f["b1"].reshape(E * 4, P).T, "w2": row_chunks(f["W2"].reshape(E * DF, D)), "b2": f["b2"],
        "iota": every(np.arange(E, dtype=np.float32) - E)})

    def by_quad(w):
        return np.tile(w.T.reshape(-1, H2, 1, HD2), (1, 1, 4, 1)).reshape(w.shape[1], 4 * P)

    part = r % 32 // HD2
    qlow, klow = (part >= 2).astype(np.float32), (part % 2).astype(np.float32)
    signs = np.stack([qlow, 1 - 2 * qlow, klow, 1 - 2 * klow], 1)
    mask4 = np.zeros((4, 32, 4), np.float32)
    for h in range(4):
        mask4[h, :, h] = 1
    packs["pc"] = packed(PACK_C, {
        "wq": by_quad(c["Wq"]), "wk": by_quad(c["Wk"]),
        "bq": by_quad(c["bq"][:, None]).reshape(4, P).T, "bk": by_quad(c["bk"][:, None]).reshape(4, P).T,
        "signs": signs, "sel": ((r[:, None] % H2 == np.arange(H2)) & (r[:, None] < 2 * H2)).astype(np.float32),
        "wv": c["Wv"].T, "bv": every(c["bv"]), "wqv": row_chunks(c["Wqv"]), "bqv": column_chunks(c["bqv"], 4),
        "wsq": np.tile(c["Ws"][0, :QK2], 4)[:, None], "mask4": mask4.reshape(P, 4), "wso": every(c["Ws"][0, QK2:]),
        "bs": every(c["bs"]), "wf": c["Wf"].T, "bf": every(c["bf"]), "wr1": c["Wr1"].T,
        "br1": column_chunks(c["br1"], 2), "wr2": row_chunks(c["Wr2"].T), "br2": every(c["br2"]),
        "g1": every(c["g1"]), "b1": every(c["b1"]), "g2": every(c["g2"]), "b2": every(c["b2"])})
    packs["pd"] = packed(PACK_D, {
        "w1": m["w1_w"].T, "w2": m["w2_w"].T, "h1": row_chunks(m["h1_w"].T), "h2": row_chunks(m["h2_w"].T),
        "w3": row_chunks(m["w3_w"].T), "s1": column_chunks(m["w1_s"], 4), "s2": column_chunks(m["w2_s"], 4),
        "t1": column_chunks(m["h1_s"], 4), "t2": column_chunks(m["h2_s"], 4), "s3": every(m["w3_s"])})
    packs["x"] = a["hs"].reshape(NT, P, D).transpose(1, 0, 2)
    return packs


def kernel(**inputs):
    import concourse.bacc as bacc
    from concourse.bass_utils import run_bass_kernel_spmd

    nc = bacc.Bacc("TRN2", target_bir_lowering=False, num_devices=1)
    arrays, args = {}, []
    for name, a in layout(inputs).items():
        arrays[f"in_{name}"] = np.ascontiguousarray(a, dtype=np.float32)
        args.append((name, nc.dram_tensor(f"in_{name}", a.shape, F32, kind="ExternalInput").ap()))
    args = dict(args)
    out = nc.dram_tensor("out_x", (P, NT, D), F32, kind="ExternalOutput").ap()
    build(nc, args["x"], args["pa"], args["pb"], args["pc"], args["pd"], out)
    r = run_bass_kernel_spmd(nc, [arrays], core_ids=[0])
    got = np.asarray(r.results[0]["out_x"])
    return got.transpose(1, 0, 2).reshape(B, L, D)
```
